# Optimizing a Trainium2 kernel written in Bass

```python
import numpy as np
import jax
import jax.numpy as jnp

def _softmax(x, axis=-1):
    return jax.nn.softmax(x, axis=axis)

def _gelu(x):
    return jax.nn.gelu(x, approximate=True)

def _silu(x):
    return jax.nn.silu(x)

def _sigmoid(x):
    return jax.nn.sigmoid(x)

def _layernorm(x, axis=-1, eps=1e-05):
    m = jnp.mean(x, axis=axis, keepdims=True)
    v = jnp.var(x, axis=axis, keepdims=True)
    return (x - m) / jnp.sqrt(v + eps)

def _scatter_add(tgt, idx, src, axis=0):
    return tgt.at[idx].add(src)

def _segment_sum(src, seg, n):
    return jax.ops.segment_sum(src, seg, n)
kernel_name = 'mk_prb_d2_jaxref_r8_67abf5'

def setup_inputs(seed: int=0):
    np.random.seed(seed)
    _w = jnp.asarray

    def _L0_attn_setup():
        import jax, jax.numpy as jnp
        import numpy as np
        import math
        B, T, C = (4, 256, 128)
        H, DQK, DV = (16, 64, 64)
        key = jax.random.key(seed)
        k1, k2, k3, k4, k5 = jax.random.split(key, 5)
        x_q = jax.random.normal(k1, (B, T, C), dtype=jnp.float32)
        w_q = jax.random.normal(k2, (H, DQK, C), dtype=jnp.float32) / math.sqrt(C)
        w_k = jax.random.normal(k3, (H, DQK, C), dtype=jnp.float32) / math.sqrt(C)
        w_v = jax.random.normal(k4, (H, DV, C), dtype=jnp.float32) / math.sqrt(C)
        w_o = jax.random.normal(k5, (DV * H, C), dtype=jnp.float32) / math.sqrt(C)
        return {'x_q': x_q, 'w_q': w_q, 'w_k': w_k, 'w_v': w_v, 'w_o': w_o}
    _L0_attn_in = _L0_attn_setup()

    def _L0_ffn_setup():
        import jax, jax.numpy as jnp
        import numpy as np
        D_MODEL = 128
        D_FF = 512
        N_EXPERTS = 8
        TOP_K = 2
        B, T = (4, 256)
        key = jax.random.key(seed)
        ks = jax.random.split(key, 5)
        x = jax.random.normal(ks[0], (B, T, D_MODEL), dtype=jnp.float32)

        def lin(k, shape, fan_in):
            return jax.random.normal(k, shape, dtype=jnp.float32) / np.float32(np.sqrt(fan_in))
        return {'x': x, 'router_w': lin(ks[1], (N_EXPERTS, D_MODEL), D_MODEL), 'w_gate': lin(ks[2], (N_EXPERTS, D_MODEL, D_FF), D_MODEL), 'w_up': lin(ks[3], (N_EXPERTS, D_MODEL, D_FF), D_MODEL), 'w_down': lin(ks[4], (N_EXPERTS, D_FF, D_MODEL), D_FF)}
    _L0_ffn_in = _L0_ffn_setup()

    def _L1_attn_setup():
        import jax, jax.numpy as jnp
        import numpy as np
        D_MODEL = 128
        NUM_HEADS = 4
        EXPAND_K = 1.0
        EXPAND_V = 2.0
        KEY_DIM = int(D_MODEL * EXPAND_K)
        VALUE_DIM = int(D_MODEL * EXPAND_V)
        HEAD_K = KEY_DIM // NUM_HEADS
        HEAD_V = VALUE_DIM // NUM_HEADS
        CHUNK = 64
        EPS = 1e-05
        ROPE_BASE = 10000.0

        def _apply_rotary(q, k):
            d = q.shape[-1]
            half = d // 2
            inv_freq = 1.0 / ROPE_BASE ** (jnp.arange(0, d, 2, dtype=jnp.float32) / d)
            t = jnp.arange(q.shape[1], dtype=jnp.float32)
            freqs = t[:, None] * inv_freq[None, :]
            cos = jnp.cos(freqs)[None, :, None, :]
            sin = jnp.sin(freqs)[None, :, None, :]

            def rot(x):
                x1, x2 = (x[..., :half], x[..., half:])
                return jnp.concatenate([x1 * cos - x2 * sin, x2 * cos + x1 * sin], axis=-1)
            return (rot(q), rot(k))

        def _chunk_retention(q, k, v, gamma):
            B, T, H, dk = q.shape
            dv = v.shape[-1]
            C = CHUNK
            N = T // C
            qc = q.reshape(B, N, C, H, dk).transpose(1, 0, 3, 2, 4)
            kc = k.reshape(B, N, C, H, dk).transpose(1, 0, 3, 2, 4)
            vc = v.reshape(B, N, C, H, dv).transpose(1, 0, 3, 2, 4)
            i = jnp.arange(C, dtype=jnp.float32)
            cross_dec = gamma[:, None] ** (i + 1.0)
            k_dec = gamma[:, None] ** (C - 1.0 - i)
            diff = i[:, None] - i[None, :]
            mask = jnp.where(diff >= 0, gamma[:, None, None] ** diff, 0.0)
            gC = gamma ** C

            def step(S, inp):
                qb, kb, vb = inp
                attn = jnp.einsum('bhid,bhjd->bhij', qb, kb) * mask
                o_intra = jnp.einsum('bhij,bhjv->bhiv', attn, vb)
                o_inter = jnp.einsum('bhid,bhdv->bhiv', qb * cross_dec[:, :, None], S)
                S_new = gC[:, None, None] * S + jnp.einsum('bhjd,bhjv->bhdv', kb * k_dec[:, :, None], vb)
                return (S_new, o_intra + o_inter)
            S0 = jnp.zeros((B, H, dk, dv), dtype=q.dtype)
            _, o = jax.lax.scan(step, S0, (qc, kc, vc))
            return o.transpose(1, 0, 3, 2, 4).reshape(B, T, H, dv)
        key = jax.random.key(seed)
        ks = jax.random.split(key, 7)
        B, T = (4, 256)
        s = 0.02
        return {'x': jax.random.normal(ks[0], (B, T, D_MODEL), dtype=jnp.float32), 'Wq': jax.random.normal(ks[1], (KEY_DIM, D_MODEL), dtype=jnp.float32) * s, 'Wk': jax.random.normal(ks[2], (KEY_DIM, D_MODEL), dtype=jnp.float32) * s, 'Wv': jax.random.normal(ks[3], (VALUE_DIM, D_MODEL), dtype=jnp.float32) * s, 'Wg': jax.random.normal(ks[4], (VALUE_DIM, D_MODEL), dtype=jnp.float32) * s, 'Wo': jax.random.normal(ks[5], (D_MODEL, VALUE_DIM), dtype=jnp.float32) * s, 'gnorm_w': jnp.ones((HEAD_V,), dtype=jnp.float32)}
    _L1_attn_in = _L1_attn_setup()

    def _L1_ffn_setup():
        import jax, jax.numpy as jnp
        import numpy as np
        DIM = 128
        DEPTH = 6
        HEADS = 16
        DIM_HEAD = 64
        WINDOW = 32
        INNER = HEADS * DIM_HEAD
        DIM_INNER = int(DIM * 4 * 2 / 3)
        QK_SCALE = 8.0

        def shift_tokens(t):
            a, s = jnp.split(t, 2, -1)
            s = jnp.pad(s, ((0, 0), (1, 0), (0, 0)))[:, :-1]
            return jnp.concatenate([a, s], -1)

        def l2norm(t):
            return t / jnp.maximum(jnp.linalg.norm(t, axis=-1, keepdims=True), 1e-12)

        def rotate_half(x):
            x1, x2 = jnp.split(x, 2, -1)
            return jnp.concatenate([-x2, x1], -1)

        def rotary_tables(n):
            half = jnp.arange(0, DIM_HEAD, 2, dtype=jnp.float32)
            inv_freq = 1.0 / 10000.0 ** (half / DIM_HEAD)
            t = jnp.arange(n, dtype=jnp.float32)
            freqs = t[:, None] * inv_freq[None, :]
            freqs = jnp.concatenate([freqs, freqs], -1)
            base_scale = (half + 0.4 * DIM_HEAD) / (1.4 * DIM_HEAD)
            power = (t - n // 2) / (WINDOW // 2)
            scale = base_scale[None, :] ** power[:, None]
            scale = jnp.concatenate([scale, scale], -1)
            return (freqs, scale)

        def local_attention(q, k, v):
            b, h, n, d = q.shape
            w = WINDOW
            nw = n // w
            bq = q.reshape(b, h, nw, w, d)
            bk = k.reshape(b, h, nw, w, d)
            bv = v.reshape(b, h, nw, w, d)

            def look(t):
                p = jnp.pad(t, ((0, 0), (0, 0), (1, 0), (0, 0), (0, 0)))
                return jnp.concatenate([p[:, :, :nw], p[:, :, 1:]], axis=3)
            bk2, bv2 = (look(bk), look(bv))
            seq = jnp.arange(n).reshape(nw, w)
            seq_p = jnp.pad(seq, ((1, 0), (0, 0)), constant_values=-1)
            jt = jnp.concatenate([seq_p[:nw], seq_p[1:]], axis=1)
            it = seq[:, :, None]
            jb = jt[:, None, :]
            mask = (it < jb) | (it > jb + w) | (jb == -1)
            sim = jnp.einsum('bhwie,bhwje->bhwij', bq, bk2) * QK_SCALE
            sim = jnp.where(mask, -jnp.finfo(sim.dtype).max, sim)
            attn = jax.nn.softmax(sim, -1)
            out = jnp.einsum('bhwij,bhwje->bhwie', attn, bv2)
            return out.reshape(b, h, n, d)

        def attn_layer(x, Wqkv, qs, ksc, Wo):
            b, n, _ = x.shape
            qkv = x @ Wqkv
            q, k, v = jnp.split(qkv, 3, -1)
            sh = lambda t: t.reshape(b, n, HEADS, DIM_HEAD).transpose(0, 2, 1, 3)
            q, k, v = (sh(q), sh(k), sh(v))
            q = l2norm(q) * qs
            k = l2norm(k) * ksc
            freqs, scale = rotary_tables(n)
            cos, sin = (jnp.cos(freqs), jnp.sin(freqs))
            q = q * cos * scale + rotate_half(q) * sin * scale
            inv = 1.0 / scale
            k = k * cos * inv + rotate_half(k) * sin * inv
            out = local_attention(q, k, v)
            out = out.transpose(0, 2, 1, 3).reshape(b, n, INNER)
            return out @ Wo

        def ffn_layer(x, g, bln, W1, b1, W2, b2):
            mu = x.mean(-1, keepdims=True)
            var = ((x - mu) ** 2).mean(-1, keepdims=True)
            xn = (x - mu) / jnp.sqrt(var + 1e-05) * g + bln
            hg = xn @ W1 + b1
            a, gate = jnp.split(hg, 2, -1)
            return a * jax.nn.gelu(gate, approximate=False) @ W2 + b2
        key = jax.random.key(seed)
        ks = jax.random.split(key, 8)
        B, N = (2, 256)
        init = lambda k, shape: jax.random.normal(k, shape, jnp.float32) * 0.02
        return {'x': jax.random.normal(ks[0], (B, N, DIM), jnp.float32), 'Wqkv': init(ks[1], (DEPTH, DIM, 3 * INNER)), 'q_scale': jnp.ones((DEPTH, DIM_HEAD), jnp.float32), 'k_scale': jnp.ones((DEPTH, DIM_HEAD), jnp.float32), 'Wo': init(ks[2], (DEPTH, INNER, DIM)), 'ln_g': jnp.ones((DEPTH, DIM), jnp.float32), 'ln_b': jnp.zeros((DEPTH, DIM), jnp.float32), 'W1': init(ks[3], (DEPTH, DIM, 2 * DIM_INNER)), 'b1': jnp.zeros((DEPTH, 2 * DIM_INNER), jnp.float32), 'W2': init(ks[4], (DEPTH, DIM_INNER, DIM)), 'b2': jnp.zeros((DEPTH, DIM), jnp.float32)}
    _L1_ffn_in = _L1_ffn_setup()
    _d = {'L0_attn_x_q': _L0_attn_in['x_q'], 'L0_attn_w_q': _L0_attn_in['w_q'], 'L0_attn_w_k': _L0_attn_in['w_k'], 'L0_attn_w_v': _L0_attn_in['w_v'], 'L0_attn_w_o': _L0_attn_in['w_o'], 'L0_ffn_router_w': _L0_ffn_in['router_w'], 'L0_ffn_w_gate': _L0_ffn_in['w_gate'], 'L0_ffn_w_up': _L0_ffn_in['w_up'], 'L0_ffn_w_down': _L0_ffn_in['w_down'], 'L1_attn_Wq': _L1_attn_in['Wq'], 'L1_attn_Wk': _L1_attn_in['Wk'], 'L1_attn_Wv': _L1_attn_in['Wv'], 'L1_attn_Wg': _L1_attn_in['Wg'], 'L1_attn_Wo': _L1_attn_in['Wo'], 'L1_attn_gnorm_w': _L1_attn_in['gnorm_w'], 'L1_ffn_Wqkv': _L1_ffn_in['Wqkv'], 'L1_ffn_q_scale': _L1_ffn_in['q_scale'], 'L1_ffn_k_scale': _L1_ffn_in['k_scale'], 'L1_ffn_Wo': _L1_ffn_in['Wo'], 'L1_ffn_ln_g': _L1_ffn_in['ln_g'], 'L1_ffn_ln_b': _L1_ffn_in['ln_b'], 'L1_ffn_W1': _L1_ffn_in['W1'], 'L1_ffn_b1': _L1_ffn_in['b1'], 'L1_ffn_W2': _L1_ffn_in['W2'], 'L1_ffn_b2': _L1_ffn_in['b2']}
    _x0 = _d['L0_attn_x_q']
    _d['L0_attn_x_q'] = jax.random.normal(jax.random.fold_in(jax.random.key(seed), 1), (16, 256, 128), dtype=_x0.dtype)
    del _x0
    return _d

def reference(L0_attn_x_q, L0_attn_w_q, L0_attn_w_k, L0_attn_w_v, L0_attn_w_o, L0_ffn_router_w, L0_ffn_w_gate, L0_ffn_w_up, L0_ffn_w_down, L1_attn_Wq, L1_attn_Wk, L1_attn_Wv, L1_attn_Wg, L1_attn_Wo, L1_attn_gnorm_w, L1_ffn_Wqkv, L1_ffn_q_scale, L1_ffn_k_scale, L1_ffn_Wo, L1_ffn_ln_g, L1_ffn_ln_b, L1_ffn_W1, L1_ffn_b1, L1_ffn_W2, L1_ffn_b2):

    def _L0_attn_ref(x_q, w_q, w_k, w_v, w_o):
        import jax, jax.numpy as jnp
        import numpy as np
        import math
        B, T, C = (4, 256, 128)
        H, DQK, DV = (16, 64, 64)
        q = jnp.einsum('ntc,hdc->nhtd', x_q, w_q)
        k = jnp.einsum('ntc,hdc->nhtd', x_q, w_k)
        v = jnp.einsum('ntc,hdc->nhtd', x_q, w_v)
        a = jnp.einsum('nhtd,nhsd->nhts', q, k) / math.sqrt(q.shape[3])
        t = a.shape[2]
        causal_forbidden = jnp.arange(t)[:, None] < jnp.arange(t)[None, :]
        a = jnp.where(causal_forbidden[None, None], -jnp.inf, a)
        a = jax.nn.softmax(a, axis=3)
        y = jnp.einsum('nhts,nhsd->nthd', a, v).reshape(a.shape[0], t, -1)
        return y @ w_o

    def _L0_ffn_ref(x, router_w, w_gate, w_up, w_down):
        import jax, jax.numpy as jnp
        import numpy as np
        D_MODEL = 128
        D_FF = 512
        N_EXPERTS = 8
        TOP_K = 2
        B, T = (4, 256)
        Bx, Tx, D = x.shape
        xf = x.reshape(-1, D)
        logits = xf @ router_w.T
        scores = jax.nn.softmax(logits, axis=-1)
        topk_scores, topk_ids = jax.lax.top_k(scores, TOP_K)
        topk_scores = topk_scores / topk_scores.sum(-1, keepdims=True)
        cw = (jax.nn.one_hot(topk_ids, N_EXPERTS, dtype=xf.dtype) * topk_scores[..., None]).sum(1)

        def body(acc, inputs):
            wg, wu, wd, w = inputs
            h = jax.nn.silu(xf @ wg) * (xf @ wu)
            acc = acc + w[:, None] * (h @ wd)
            return (acc, None)
        out, _ = jax.lax.scan(body, jnp.zeros_like(xf), (w_gate, w_up, w_down, cw.T))
        return out.reshape(Bx, Tx, D)

    def _L1_attn_ref(x, Wq, Wk, Wv, Wg, Wo, gnorm_w):
        import jax, jax.numpy as jnp
        import numpy as np
        D_MODEL = 128
        NUM_HEADS = 4
        EXPAND_K = 1.0
        EXPAND_V = 2.0
        KEY_DIM = int(D_MODEL * EXPAND_K)
        VALUE_DIM = int(D_MODEL * EXPAND_V)
        HEAD_K = KEY_DIM // NUM_HEADS
        HEAD_V = VALUE_DIM // NUM_HEADS
        CHUNK = 64
        EPS = 1e-05
        ROPE_BASE = 10000.0

        def _apply_rotary(q, k):
            d = q.shape[-1]
            half = d // 2
            inv_freq = 1.0 / ROPE_BASE ** (jnp.arange(0, d, 2, dtype=jnp.float32) / d)
            t = jnp.arange(q.shape[1], dtype=jnp.float32)
            freqs = t[:, None] * inv_freq[None, :]
            cos = jnp.cos(freqs)[None, :, None, :]
            sin = jnp.sin(freqs)[None, :, None, :]

            def rot(x):
                x1, x2 = (x[..., :half], x[..., half:])
                return jnp.concatenate([x1 * cos - x2 * sin, x2 * cos + x1 * sin], axis=-1)
            return (rot(q), rot(k))

        def _chunk_retention(q, k, v, gamma):
            B, T, H, dk = q.shape
            dv = v.shape[-1]
            C = CHUNK
            N = T // C
            qc = q.reshape(B, N, C, H, dk).transpose(1, 0, 3, 2, 4)
            kc = k.reshape(B, N, C, H, dk).transpose(1, 0, 3, 2, 4)
            vc = v.reshape(B, N, C, H, dv).transpose(1, 0, 3, 2, 4)
            i = jnp.arange(C, dtype=jnp.float32)
            cross_dec = gamma[:, None] ** (i + 1.0)
            k_dec = gamma[:, None] ** (C - 1.0 - i)
            diff = i[:, None] - i[None, :]
            mask = jnp.where(diff >= 0, gamma[:, None, None] ** diff, 0.0)
            gC = gamma ** C

            def step(S, inp):
                qb, kb, vb = inp
                attn = jnp.einsum('bhid,bhjd->bhij', qb, kb) * mask
                o_intra = jnp.einsum('bhij,bhjv->bhiv', attn, vb)
                o_inter = jnp.einsum('bhid,bhdv->bhiv', qb * cross_dec[:, :, None], S)
                S_new = gC[:, None, None] * S + jnp.einsum('bhjd,bhjv->bhdv', kb * k_dec[:, :, None], vb)
                return (S_new, o_intra + o_inter)
            S0 = jnp.zeros((B, H, dk, dv), dtype=q.dtype)
            _, o = jax.lax.scan(step, S0, (qc, kc, vc))
            return o.transpose(1, 0, 3, 2, 4).reshape(B, T, H, dv)
        B, T, _ = x.shape
        H = NUM_HEADS
        q = (x @ Wq.T).reshape(B, T, H, HEAD_K)
        k = (x @ Wk.T).reshape(B, T, H, HEAD_K)
        v = (x @ Wv.T).reshape(B, T, H, HEAD_V)
        g = (x @ Wg.T).reshape(B, T, H, HEAD_V)
        q, k = _apply_rotary(q, k)
        q = q * HEAD_K ** (-0.5)
        gamma = 1.0 - jnp.exp2(-5.0 - jnp.arange(H, dtype=jnp.float32))
        o = _chunk_retention(q, k, v, gamma)
        var = jnp.mean(o * o, axis=-1, keepdims=True)
        o = o * jax.lax.rsqrt(var + EPS) * gnorm_w
        o = o * (g * jax.nn.sigmoid(g))
        return o.reshape(B, T, H * HEAD_V) @ Wo.T

    def _L1_ffn_ref(x, Wqkv, q_scale, k_scale, Wo, ln_g, ln_b, W1, b1, W2, b2):
        import jax, jax.numpy as jnp
        import numpy as np
        DIM = 128
        DEPTH = 6
        HEADS = 16
        DIM_HEAD = 64
        WINDOW = 32
        INNER = HEADS * DIM_HEAD
        DIM_INNER = int(DIM * 4 * 2 / 3)
        QK_SCALE = 8.0

        def shift_tokens(t):
            a, s = jnp.split(t, 2, -1)
            s = jnp.pad(s, ((0, 0), (1, 0), (0, 0)))[:, :-1]
            return jnp.concatenate([a, s], -1)

        def l2norm(t):
            return t / jnp.maximum(jnp.linalg.norm(t, axis=-1, keepdims=True), 1e-12)

        def rotate_half(x):
            x1, x2 = jnp.split(x, 2, -1)
            return jnp.concatenate([-x2, x1], -1)

        def rotary_tables(n):
            half = jnp.arange(0, DIM_HEAD, 2, dtype=jnp.float32)
            inv_freq = 1.0 / 10000.0 ** (half / DIM_HEAD)
            t = jnp.arange(n, dtype=jnp.float32)
            freqs = t[:, None] * inv_freq[None, :]
            freqs = jnp.concatenate([freqs, freqs], -1)
            base_scale = (half + 0.4 * DIM_HEAD) / (1.4 * DIM_HEAD)
            power = (t - n // 2) / (WINDOW // 2)
            scale = base_scale[None, :] ** power[:, None]
            scale = jnp.concatenate([scale, scale], -1)
            return (freqs, scale)

        def local_attention(q, k, v):
            b, h, n, d = q.shape
            w = WINDOW
            nw = n // w
            bq = q.reshape(b, h, nw, w, d)
            bk = k.reshape(b, h, nw, w, d)
            bv = v.reshape(b, h, nw, w, d)

            def look(t):
                p = jnp.pad(t, ((0, 0), (0, 0), (1, 0), (0, 0), (0, 0)))
                return jnp.concatenate([p[:, :, :nw], p[:, :, 1:]], axis=3)
            bk2, bv2 = (look(bk), look(bv))
            seq = jnp.arange(n).reshape(nw, w)
            seq_p = jnp.pad(seq, ((1, 0), (0, 0)), constant_values=-1)
            jt = jnp.concatenate([seq_p[:nw], seq_p[1:]], axis=1)
            it = seq[:, :, None]
            jb = jt[:, None, :]
            mask = (it < jb) | (it > jb + w) | (jb == -1)
            sim = jnp.einsum('bhwie,bhwje->bhwij', bq, bk2) * QK_SCALE
            sim = jnp.where(mask, -jnp.finfo(sim.dtype).max, sim)
            attn = jax.nn.softmax(sim, -1)
            out = jnp.einsum('bhwij,bhwje->bhwie', attn, bv2)
            return out.reshape(b, h, n, d)

        def attn_layer(x, Wqkv, qs, ksc, Wo):
            b, n, _ = x.shape
            qkv = x @ Wqkv
            q, k, v = jnp.split(qkv, 3, -1)
            sh = lambda t: t.reshape(b, n, HEADS, DIM_HEAD).transpose(0, 2, 1, 3)
            q, k, v = (sh(q), sh(k), sh(v))
            q = l2norm(q) * qs
            k = l2norm(k) * ksc
            freqs, scale = rotary_tables(n)
            cos, sin = (jnp.cos(freqs), jnp.sin(freqs))
            q = q * cos * scale + rotate_half(q) * sin * scale
            inv = 1.0 / scale
            k = k * cos * inv + rotate_half(k) * sin * inv
            out = local_attention(q, k, v)
            out = out.transpose(0, 2, 1, 3).reshape(b, n, INNER)
            return out @ Wo

        def ffn_layer(x, g, bln, W1, b1, W2, b2):
            mu = x.mean(-1, keepdims=True)
            var = ((x - mu) ** 2).mean(-1, keepdims=True)
            xn = (x - mu) / jnp.sqrt(var + 1e-05) * g + bln
            hg = xn @ W1 + b1
            a, gate = jnp.split(hg, 2, -1)
            return a * jax.nn.gelu(gate, approximate=False) @ W2 + b2
        for i in range(DEPTH):
            x = attn_layer(shift_tokens(x), Wqkv[i], q_scale[i], k_scale[i], Wo[i]) + x
            x = ffn_layer(shift_tokens(x), ln_g[i], ln_b[i], W1[i], b1[i], W2[i], b2[i]) + x
        return x
    x = L0_attn_x_q
    xn = _layernorm(x, axis=-1)
    x = x + _L0_attn_ref(xn, L0_attn_w_q, L0_attn_w_k, L0_attn_w_v, L0_attn_w_o) + _L0_ffn_ref(xn, L0_ffn_router_w, L0_ffn_w_gate, L0_ffn_w_up, L0_ffn_w_down)
    xn = _layernorm(x, axis=-1)
    x = x + _L1_attn_ref(xn, L1_attn_Wq, L1_attn_Wk, L1_attn_Wv, L1_attn_Wg, L1_attn_Wo, L1_attn_gnorm_w) + _L1_ffn_ref(xn, L1_ffn_Wqkv, L1_ffn_q_scale, L1_ffn_k_scale, L1_ffn_Wo, L1_ffn_ln_g, L1_ffn_ln_b, L1_ffn_W1, L1_ffn_b1, L1_ffn_W2, L1_ffn_b2)
    return x

_drawn_inputs = setup_inputs


def setup_inputs(seed=0):
    import zlib

    import numpy as np

    out = dict(_drawn_inputs(seed))
    spreads = {'L1_attn_gnorm_w': (1.0, 0.6),
     'L1_ffn_q_scale': (1.0, 0.6),
     'L1_ffn_k_scale': (1.0, 0.6),
     'L1_ffn_ln_g': (1.0, 0.6),
     'L1_ffn_ln_b': (0.0, 0.8),
     'L1_ffn_b1': (0.0, 0.8),
     'L1_ffn_b2': (0.0, 0.1)}
    factors = {'L1_attn_Wq': 3.319,
     'L1_attn_Wk': 3.303,
     'L1_attn_Wv': 3.29,
     'L1_attn_Wg': 3.389,
     'L1_attn_Wo': 3.315,
     'L1_ffn_W1': 4.112,
     'L1_ffn_W2': 4.032}
    for name, (base, spread) in spreads.items():
        noise = np.random.default_rng([zlib.crc32(name.encode()), seed]).standard_normal(out[name].shape)
        drawn = base * np.exp(spread * noise) if base else spread * noise
        out[name] = jnp.asarray(drawn.astype(out[name].dtype))
    for name, factor in factors.items():
        out[name] = (out[name] * factor).astype(out[name].dtype)
    return out
```

```python
from contextlib import ExitStack

import numpy as np

import concourse.bass as bass
from concourse import mybir

F32 = mybir.dt.float32
BF16 = mybir.dt.bfloat16
ACT = mybir.ActivationFunctionType
ALU = mybir.AluOpType
AX = mybir.AxisListType

P = 128
SEQS, TOKENS, D = 16, 256, 128
BLOCKS = SEQS * TOKENS // P
BPS = TOKENS // P
LN_EPS = 1e-5
MASKED = -1e30

CONSTS = {}
_at = 0
for _name, _n in (("ident", P), ("causal", 3 * P), ("rank", 256), ("ret_cos", 512), ("ret_sin", 512),
                  ("ret_decay", 4 * 3 * P), ("rotary", 512), ("band", 512), ("band_prev", 512)):
    CONSTS[_name] = (_at, _n)
    _at += _n
N_CONST = _at


def const_tables():
    p = np.arange(P)[:, None]
    j = np.arange(P)[None, :]
    causal = np.where(j > p, MASKED, 0.0)
    parts = {
        "ident": np.eye(P),
        "causal": np.concatenate([causal, np.zeros((P, P)), causal], 1),
    }
    parts["rank"] = np.tile(8.0 - np.arange(8), (P, 32))
    parts.update(retention_tables())
    parts["rotary"] = rotary_base()
    parts.update(band_masks())
    return np.ascontiguousarray(np.concatenate([parts[n] for n in CONSTS], 1).astype(np.float32))


class Memory:

    def __init__(self, nc, stack, phase):
        self.nc, self.stack, self.phase = nc, stack, phase

    def sb(self, name, shape, dt=F32):
        return self.stack.enter_context(self.nc.sbuf_tensor(f"{self.phase}_{name}", shape, dt))

    def banks(self):
        return [self.stack.enter_context(self.nc.psum_tensor(f"{self.phase}_bank{i}", [P, 512], F32)) for i in range(8)]

    def sem(self, name):
        return self.stack.enter_context(self.nc.semaphore(f"{self.phase}_{name}"))


def normalise(nc, phase, x1, xn_t, const, eps, x_dram=None, const_dram=None, bf16_tables=()):
    groups, per = 4, BLOCKS // 4
    with ExitStack() as stack:
        m = Memory(nc, stack, phase)
        xn = m.sb("xn", [P, BLOCKS, D])
        stats = m.sb("stats", [P, BLOCKS, 6])
        mv = m.sb("mean_var", [P, BLOCKS, 2])
        rstd = m.sb("rstd", [P, BLOCKS])
        std = m.sb("std", [P, BLOCKS])
        bank = m.banks()
        x_in, const_in = [m.sem(f"x_in{g}") for g in range(groups)], m.sem("const_in")
        stats_done, mv_done, std_done = m.sem("stats_done"), m.sem("mv_done"), m.sem("std_done")
        rstd_done, xn_done = m.sem("rstd_done"), m.sem("xn_done")
        turned, copied = m.sem("turned"), m.sem("copied")
        eps_done, tables_done = m.sem("eps_done"), m.sem("tables_done")
        block = stack.enter_context(nc.Block())

        @block.sync
        def _(sp):
            if x_dram is not None:
                x_view = x_dram.rearrange("s (b p) f -> p (s b) f", p=P)
                for g in range(groups):
                    ks = slice(g * per, (g + 1) * per)
                    sp.dma_start(x1[:, ks, :], x_view[:, ks, :]).then_inc(x_in[g], 16)
                sp.dma_start(const[:, :], const_dram).then_inc(const_in, 16)

        @block.gpsimd
        def _(pool):
            if x_dram is not None:
                pool.memset(eps[:, :], LN_EPS).then_inc(eps_done, 1)

        @block.vector
        def _(dve):
            for g in range(groups):
                ks = range(g * per, (g + 1) * per)
                if x_dram is not None:
                    dve.wait_ge(x_in[g], 16)
                for k in ks:
                    last = nc.vector.bn_stats(stats[:, k, :], x1[:, k, :])
                last.then_inc(stats_done, 1)
                dve.wait_ge(stats_done, g + 1)
                for k in ks:
                    last = nc.vector.bn_aggr(mv[:, k, :], stats[:, k, :])
                last.then_inc(mv_done, 1)
                dve.wait_ge(std_done, g + 1)
                nc.vector.reciprocal(rstd[:, g * per:(g + 1) * per], std[:, g * per:(g + 1) * per]).then_inc(rstd_done, 1)
                dve.wait_ge(rstd_done, g + 1)
                for k in ks:
                    nc.vector.tensor_scalar(xn[:, k, :], x1[:, k, :], mv[:, k, 0:1], rstd[:, k:k + 1],
                                            ALU.subtract, ALU.mult).then_inc(xn_done, 1)
            if x_dram is not None:
                dve.wait_ge(const_in, 16)
            for table, name in bf16_tables:
                nc.vector.tensor_copy(table[:, :], const[:, slice_of(name)]).then_inc(tables_done, 1)

        @block.tensor
        def _(pe):
            if x_dram is not None:
                pe.wait_ge(const_in, 16)
            ident = const[:, slice_of("ident")]
            for k in range(BLOCKS):
                pe.wait_ge(xn_done, k + 1)
                last = nc.tensor.transpose(bank[k // 4][:, k % 4 * P:(k % 4 + 1) * P], xn[:, k, :], ident)
                if k % 4 == 3:
                    last.then_inc(turned, 1)

        @block.scalar
        def _(act):
            if x_dram is not None:
                act.wait_ge(eps_done, 1)
            for g in range(groups):
                act.wait_ge(mv_done, g + 1)
                nc.scalar.activation(std[:, g * per:(g + 1) * per], mv[:, g * per:(g + 1) * per, 1],
                                     ACT.Sqrt, bias=eps[:, 0:1]).then_inc(std_done, 1)
            for q in range(8):
                act.wait_ge(turned, q + 1)
                nc.scalar.activation(xn_t[:, q * 512:(q + 1) * 512], bank[q][:, :], ACT.Copy).then_inc(copied, 1)


def slice_of(name):
    at, n = CONSTS[name]
    return slice(at, at + n)


A_HEADS, A_DIM = 16, 64
A_CHUNKS = A_HEADS // 2
A_WIDE = A_HEADS * A_DIM


def causal_attention(nc, wq_dram, wk_dram, wv_dram, wo_dram, x1, xn_t, ident_f, ident_b, causal_b,
                     for_later):
    with ExitStack() as stack:
        m = Memory(nc, stack, "att")
        wq, wk, wv = (m.sb(n, [P, A_WIDE]) for n in ("wq", "wk", "wv"))
        wo = m.sb("wo", [P, A_CHUNKS, D])
        xs = m.sb("xs", [P, TOKENS])
        q_even = m.sb("q_even", [P, A_CHUNKS, TOKENS])
        q_odd = m.sb("q_odd", [P, A_CHUNKS, TOKENS])
        k_t = m.sb("k_t", [P, A_CHUNKS, TOKENS])
        v = m.sb("v", [P, BPS, A_WIDE])
        probs = m.sb("probs", [P, 4, 3 * P])
        probs_t = m.sb("probs_t", [P, 2, 3 * P])
        neg_max = m.sb("neg_max", [P, A_HEADS, 2])
        sums = m.sb("sums", [P, A_HEADS, 2])
        inv = m.sb("inv", [P, A_HEADS, 2])
        o_t = m.sb("o_t", [P, A_CHUNKS, TOKENS])
        bank = m.banks()
        proj_bank, score_bank, turn_bank, out_bank = bank[0:2], bank[2:4], bank[4:6], bank[6:8]
        w_in, zeros_done = m.sem("w_in"), m.sem("zeros_done")
        xs_ready = m.sem("xs_ready")
        qk_psum, v_psum, wo_psum = m.sem("qk_psum"), m.sem("v_psum"), m.sem("wo_psum")
        qk_act, qk_dve, v_act, v_dve = m.sem("qk_act"), m.sem("qk_dve"), m.sem("v_act"), m.sem("v_dve")
        scores_ready, max_ready, exp_done = m.sem("scores_ready"), m.sem("max_ready"), m.sem("exp_done")
        inv_done, probs_ready = m.sem("inv_done"), m.sem("probs_ready")
        turned, turned_sb, out_psum, out_sb = m.sem("turned"), m.sem("turned_sb"), m.sem("out_psum"), m.sem("out_sb")
        added, later_in = m.sem("added"), m.sem("later_in")
        block = stack.enter_context(nc.Block())
        H, C = A_HEADS, A_CHUNKS

        @block.sync
        def _(sp):
            for w, dram in ((wq, wq_dram), (wk, wk_dram), (wv, wv_dram)):
                sp.dma_start(w[:, :], dram).then_inc(w_in, 16)
            sp.dma_start(wo[:, :, :], wo_dram.rearrange("(c p) f -> p c f", p=P)).then_inc(w_in, 16)
            for i, (tile, dram) in enumerate(for_later):
                sp.dma_start(tile, dram).then_inc(later_in, 16)
            sp.wait_ge(later_in, 16 * len(for_later))

        @block.gpsimd
        def _(pool):
            nc.gpsimd.memset(q_even[A_DIM:P, :, :], 0.0).then_inc(zeros_done, 1)
            pool.wait_ge(zeros_done, 1)
            nc.gpsimd.memset(q_odd[0:A_DIM, :, :], 0.0).then_inc(zeros_done, 1)
            pool.wait_ge(zeros_done, 2)
            nc.gpsimd.tensor_copy(xs[:, :], xn_t[:, 0:TOKENS]).then_inc(xs_ready, 1)
            with pool.Fori(1, SEQS) as s:
                pool.wait_ge(v_psum, s * 4)
                nc.gpsimd.tensor_copy(xs[:, :], xn_t[:, bass.ds(s * TOKENS, TOKENS)]).then_inc(xs_ready, 1)

        @block.tensor
        def _(pe):
            def project_qk(n, c, first=False):
                if c >= 2:
                    pe.wait_ge(qk_act if c % 2 == 0 else qk_dve, n * (C // 2) + c // 2)
                elif not first:
                    pe.wait_ge(v_act if c % 2 == 0 else v_dve, n * 2)
                    pe.wait_ge(added, n * BPS)
                for i, w in enumerate((wq, wk)):
                    last = nc.tensor.matmul(proj_bank[c % 2][:, i * TOKENS:(i + 1) * TOKENS],
                                            w[:, c * P:(c + 1) * P], xs[:, :], start=True, stop=True)
                last.then_inc(qk_psum, 1)

            def project_v(n, u):
                if u < 2:
                    pe.wait_ge(qk_act if u == 0 else qk_dve, (n + 1) * (C // 2))
                else:
                    pe.wait_ge(v_act if u % 2 == 0 else v_dve, n * 2 + u // 2)
                last = nc.tensor.matmul(proj_bank[u % 2][:, :], xs[:, u // 2 * P:(u // 2 + 1) * P],
                                        wv[:, u % 2 * 512:(u % 2 + 1) * 512], start=True, stop=True)
                last.then_inc(v_psum, 1)

            def job(s, ahead):
                for t in range(H + 3):
                    if t < H:
                        c = t // 2
                        if t % 2 == 0:
                            pe.wait_ge(qk_act if c % 2 == 0 else qk_dve, s * (C // 2) + c // 2 + 1)
                        pe.wait_ge(exp_done, s * H + t)
                        sc, q = score_bank[t % 2], (q_even, q_odd)[t % 2]
                        nc.tensor.matmul(sc[:, 0:3 * P], ident_b[:, :], causal_b[:, :], start=True, stop=False)
                        nc.tensor.matmul(sc[:, 0:P], q[:, c, 0:P], k_t[:, c, 0:P], start=False, stop=False)
                        nc.tensor.matmul(sc[:, P:3 * P], q[:, c, P:TOKENS], k_t[:, c, :],
                                         start=False, stop=True).then_inc(scores_ready, 1)
                    elif ahead:
                        for c in range(3 * (t - H), min(3 * (t - H) + 3, C)):
                            if t == H and c == 0:
                                pe.wait_ge(xs_ready, s + 2)
                            project_qk(s + 1, c)
                    h = t - 2
                    if 0 <= h < H:
                        pe.wait_ge(probs_ready, s * H + h + 1)
                        pe.wait_ge(turned_sb, s * H + h)
                        for i, at in enumerate((0, P, 2 * P)):
                            last = nc.tensor.transpose(turn_bank[h % 2][:, i * P:(i + 1) * P],
                                                       probs[:, h % 4, at:at + P], ident_f)
                        last.then_inc(turned, 1)
                    h = t - 3
                    if h >= 0:
                        if h == 0:
                            pe.wait_ge(v_act, 2 * (s + 1))
                            pe.wait_ge(v_dve, 2 * (s + 1))
                        if h % 2 == 0:
                            pe.wait_ge(out_sb, s * C + h // 2 + 1)
                        pe.wait_ge(turned_sb, s * H + h + 2)
                        rows = slice(h % 2 * A_DIM, (h % 2 + 1) * A_DIM)
                        dst = out_bank[h // 2 % 2][rows, 0:TOKENS]
                        nc.tensor.matmul(dst, v[:, 0, h * A_DIM:(h + 1) * A_DIM], probs_t[:, h % 2, 0:TOKENS],
                                         start=True, stop=False)
                        nc.tensor.matmul(out_bank[h // 2 % 2][rows, P:TOKENS], v[:, 1, h * A_DIM:(h + 1) * A_DIM],
                                         probs_t[:, h % 2, TOKENS:3 * P], start=False, stop=True).then_inc(out_psum, 1)
                if ahead:
                    for u in range(4):
                        project_v(s + 1, u)
                pe.wait_ge(out_sb, (s + 1) * C + 2)
                for b in range(BPS):
                    if ahead:
                        pe.wait_ge((v_act, v_dve)[b], 2 * (s + 2))
                    for c in range(C):
                        last = nc.tensor.matmul(proj_bank[b][:, 0:D], o_t[:, c, b * P:(b + 1) * P], wo[:, c, :],
                                                start=c == 0, stop=c == C - 1)
                    last.then_inc(wo_psum, 1)

            pe.wait_ge(w_in, 64)
            pe.wait_ge(xs_ready, 1)
            for c in range(C):
                project_qk(0, c, first=True)
            for u in range(4):
                project_v(0, u)
            pe.wait_ge(zeros_done, 2)
            with pe.Fori(0, SEQS - 1) as s:
                job(s, True)
            job(SEQS - 1, False)

        def copy_qk(copy, c, done):
            src = proj_bank[c % 2]
            copy(q_even[0:A_DIM, c, :], src[0:A_DIM, 0:TOKENS], A_DIM ** -0.5)
            copy(q_odd[A_DIM:P, c, :], src[A_DIM:P, 0:TOKENS], A_DIM ** -0.5)
            copy(k_t[:, c, :], src[:, TOKENS:2 * TOKENS], 1.0).then_inc(done, 1)

        @block.scalar
        def _(act):
            def copy(out, src, scale):
                return nc.scalar.activation(out, src, ACT.Copy, scale=scale)

            def job(s, ahead):
                for t in range(H + 3):
                    if t < H:
                        act.wait_ge(max_ready, s * H + t + 1)
                        if t >= 4:
                            act.wait_ge(turned, s * H + t - 3)
                        for i, (a, e) in enumerate(((0, P), (P, 3 * P))):
                            last = nc.scalar.activation(probs[:, t % 4, a:e], score_bank[t % 2][:, a:e], ACT.Exp,
                                                        bias=neg_max[:, t, i:i + 1], accum_out=sums[:, t, i:i + 1])
                        last.then_inc(exp_done, 1)
                    elif ahead:
                        for c in range(3 * (t - H), min(3 * (t - H) + 3, C)):
                            if c % 2 == 0:
                                act.wait_ge(qk_psum, (s + 1) * C + c + 1)
                                copy_qk(copy, c, qk_act)
                    h = t - 2
                    if 0 <= h < H:
                        act.wait_ge(turned, s * H + h + 1)
                        if h >= 2:
                            act.wait_ge(out_psum, s * H + h - 1)
                        nc.scalar.activation(probs_t[:, h % 2, :], turn_bank[h % 2][:, 0:3 * P], ACT.Copy).then_inc(turned_sb, 1)
                if ahead:
                    copy_v(s + 1)

            def copy_v(n):
                for u in (0, 2):
                    act.wait_ge(v_psum, n * 4 + u + 1)
                    nc.scalar.activation(v[:, u // 2, 0:512], proj_bank[0][:, :], ACT.Copy).then_inc(v_act, 1)

            act.sem_inc(exp_done, 1)
            act.sem_inc(turned_sb, 1)
            for c in range(0, C, 2):
                act.wait_ge(qk_psum, c + 1)
                copy_qk(copy, c, qk_act)
            copy_v(0)
            with act.Fori(0, SEQS - 1) as s:
                job(s, True)
            job(SEQS - 1, False)

        @block.vector
        def _(dve):
            def copy(out, src, scale):
                return nc.vector.tensor_scalar(out, src, scale, None, ALU.mult)

            def job(s, ahead):
                for t in range(H + 4):
                    if t < H:
                        dve.wait_ge(scores_ready, s * H + t + 1)
                        for i, (a, e) in enumerate(((0, P), (P, 3 * P))):
                            last = nc.vector.tensor_reduce(neg_max[:, t, i:i + 1], score_bank[t % 2][:, a:e], AX.X, ALU.max,
                                                           negate=True)
                        last.then_inc(max_ready, 1)
                    h = t - 1
                    if 0 <= h < H:
                        dve.wait_ge(exp_done, s * H + h + 2)
                        nc.vector.reciprocal(inv[:, h, :], sums[:, h, :]).then_inc(inv_done, 1)
                        dve.wait_ge(inv_done, s * H + h + 1)
                        for i, (a, e) in enumerate(((0, P), (P, 3 * P))):
                            last = nc.vector.tensor_scalar(probs[:, h % 4, a:e], probs[:, h % 4, a:e], inv[:, h, i:i + 1],
                                                           None, ALU.mult)
                        last.then_inc(probs_ready, 1)
                    if ahead and t >= H:
                        for c in range(3 * (t - H), min(3 * (t - H) + 3, C)):
                            if c % 2 == 1:
                                dve.wait_ge(qk_psum, (s + 1) * C + c + 1)
                                copy_qk(copy, c, qk_dve)
                    h = t - 4
                    if h >= 0 and h % 2 == 1:
                        dve.wait_ge(out_psum, s * H + h + 1)
                        nc.vector.tensor_copy(o_t[:, h // 2, :], out_bank[h // 2 % 2][:, 0:TOKENS]).then_inc(out_sb, 1)
                if ahead:
                    copy_v(s + 1)
                for b in range(BPS):
                    dve.wait_ge(wo_psum, BPS * s + b + 1)
                    dst = x1[:, bass.ds(s * BPS + b, 1), :]
                    nc.vector.tensor_tensor(dst, proj_bank[b][:, 0:D].rearrange("p (o f) -> p o f", o=1), dst, ALU.add).then_inc(added, 1)

            def copy_v(n):
                for u in (1, 3):
                    dve.wait_ge(v_psum, n * 4 + u + 1)
                    nc.vector.tensor_copy(v[:, u // 2, 512:1024], proj_bank[1][:, :]).then_inc(v_dve, 1)

            dve.sem_inc(out_sb, 2)
            dve.sem_inc(added, BPS)
            for c in range(1, C, 2):
                dve.wait_ge(qk_psum, c + 1)
                copy_qk(copy, c, qk_dve)
            copy_v(0)
            with dve.Fori(0, SEQS - 1) as s:
                job(s, True)
            job(SEQS - 1, False)


EXPERTS, D_FF = 8, 512
FC = D_FF // P


def mixture_of_experts(nc, router_dram, x1, xn_t, const, wg, wu, wd):
    NB, E = BLOCKS, EXPERTS
    TC = 4
    CHUNKS = NB // TC
    with ExitStack() as stack:
        m = Memory(nc, stack, "moe")
        rw = m.sb("router_w", [P, E])
        small = {n: m.sb(n, [P, NB, E]) for n in ("logit", "below", "ranked", "first", "rest", "ranked2", "second", "chosen",
                                                 "expo", "picked", "weight")}
        top = {n: m.sb(n, [P, NB]) for n in ("max1", "rank1", "max2", "rank2", "total", "inv")}
        xs = m.sb("xs", [P, TC * P])
        gate = m.sb("gate", [P, 2, TC * P])
        hid = m.sb("hidden", [P, 2, FC, TC * P])
        bank = m.banks()
        gate_bank, up_bank, down_bank, route_bank = bank[0:2], bank[2:4], bank[4:6], bank[6]
        rw_in, logits_psum, route, expo_done = m.sem("rw_in"), m.sem("logits_psum"), m.sem("route"), m.sem("expo_done")
        xs_ready, gate_psum, up_psum, gate_done = m.sem("xs_ready"), m.sem("gate_psum"), m.sem("up_psum"), m.sem("gate_done")
        hid_done, down_psum, added = m.sem("hid_done"), m.sem("down_psum"), m.sem("added")
        block = stack.enter_context(nc.Block())
        ROUTE_STEPS = 16

        @block.sync
        def _(sp):
            sp.dma_start(rw[:, :], router_dram).then_inc(rw_in, 16)

        @block.gpsimd
        def _(pool):
            nc.gpsimd.tensor_copy(xs[:, :], xn_t[:, 0:TC * P]).then_inc(xs_ready, 1)
            with pool.Fori(1, CHUNKS) as n:
                pool.wait_ge(up_psum, n * E * FC)
                nc.gpsimd.tensor_copy(xs[:, :], xn_t[:, bass.ds(n * (TC * P), TC * P)]).then_inc(xs_ready, 1)

        @block.tensor
        def _(pe):
            def down(n, e):
                pe.wait_ge(hid_done, (n * E + e + 1) * FC)
                pe.wait_ge(added, (n * E + e - 1) * TC + 2 * TC)
                for b in range(TC):
                    for c in range(FC):
                        last = nc.tensor.matmul(down_bank[e % 2][:, b * P:(b + 1) * P], hid[:, e % 2, c, b * P:(b + 1) * P],
                                                wd[:, e, c, :], start=c == 0, stop=c == FC - 1)
                last.then_inc(down_psum, 1)

            pe.wait_ge(rw_in, 16)
            for k in range(NB):
                last = nc.tensor.matmul(route_bank[:, k * E:(k + 1) * E], xn_t[:, k * P:(k + 1) * P], rw[:, :],
                                        start=True, stop=True)
            last.then_inc(logits_psum, 1)
            with pe.Fori(0, CHUNKS) as n:
                pe.wait_ge(xs_ready, n + 1)
                for e in range(E):
                    for c in range(FC):
                        i = e * FC + c
                        pe.wait_ge(gate_done, n * (E * FC) + i + 1)
                        nc.tensor.matmul(gate_bank[i % 2][:, :], wg[:, e, c * P:(c + 1) * P], xs[:, :],
                                         start=True, stop=True).then_inc(gate_psum, 1)
                        if i >= 2:
                            pe.wait_ge(hid_done, n * (E * FC) + i - 1)
                        nc.tensor.matmul(up_bank[i % 2][:, :], wu[:, e, c * P:(c + 1) * P], xs[:, :],
                                         start=True, stop=True).then_inc(up_psum, 1)
                        if c == 1 and e > 0:
                            down(n, e - 1)
                down(n, E - 1)

        @block.scalar
        def _(act):
            act.wait_ge(route, 2)
            nc.scalar.activation(small["expo"][:, :, :], small["below"][:, :, :], ACT.Exp).then_inc(expo_done, 1)
            act.sem_inc(gate_done, 2)
            with act.Fori(0, CHUNKS) as n:
                for i in range(E * FC):
                    act.wait_ge(gate_psum, n * (E * FC) + i + 1)
                    if i >= 2:
                        act.wait_ge(hid_done, n * (E * FC) + i - 1)
                    nc.scalar.activation(gate[:, i % 2, :], gate_bank[i % 2][:, :], ACT.Silu).then_inc(gate_done, 1)

        @block.vector
        def _(dve):
            s, v = small, nc.vector

            def over_experts(t):
                return t[:, :].unsqueeze(2).broadcast_to([P, NB, E])

            rank = const[:, slice_of("rank")].rearrange("p (k e) -> p k e", e=E)
            logits = route_bank[:, 0:NB * E].rearrange("p (k e) -> p k e", e=E)
            dve.wait_ge(logits_psum, 1)
            v.tensor_reduce(top["max1"][:, :], logits, AX.X, ALU.max).then_inc(route, 1)
            dve.wait_ge(route, 1)
            v.tensor_tensor(s["below"][:, :, :], logits, over_experts(top["max1"]), ALU.subtract).then_inc(route, 1)
            dve.wait_ge(route, 2)
            v.scalar_tensor_tensor(s["ranked"][:, :, :], s["below"][:, :, :], 0.0, rank, ALU.is_ge, ALU.mult).then_inc(route, 1)
            dve.wait_ge(route, 3)
            v.tensor_reduce(top["rank1"][:, :], s["ranked"][:, :, :], AX.X, ALU.max).then_inc(route, 1)
            dve.wait_ge(route, 4)
            v.tensor_tensor(s["first"][:, :, :], s["ranked"][:, :, :], over_experts(top["rank1"]), ALU.is_equal).then_inc(route, 1)
            dve.wait_ge(route, 5)
            v.scalar_tensor_tensor(s["rest"][:, :, :], s["first"][:, :, :], MASKED, s["below"][:, :, :], ALU.mult, ALU.add).then_inc(route, 1)
            dve.wait_ge(route, 6)
            v.tensor_reduce(top["max2"][:, :], s["rest"][:, :, :], AX.X, ALU.max).then_inc(route, 1)
            dve.wait_ge(route, 7)
            v.tensor_tensor(s["chosen"][:, :, :], s["rest"][:, :, :], over_experts(top["max2"]), ALU.is_equal).then_inc(route, 1)
            dve.wait_ge(route, 8)
            v.tensor_tensor(s["ranked2"][:, :, :], s["chosen"][:, :, :], rank, ALU.mult).then_inc(route, 1)
            dve.wait_ge(route, 9)
            v.tensor_reduce(top["rank2"][:, :], s["ranked2"][:, :, :], AX.X, ALU.max).then_inc(route, 1)
            dve.wait_ge(route, 10)
            v.tensor_tensor(s["second"][:, :, :], s["ranked2"][:, :, :], over_experts(top["rank2"]), ALU.is_equal).then_inc(route, 1)
            dve.wait_ge(route, 11)
            v.tensor_tensor(s["picked"][:, :, :], s["first"][:, :, :], s["second"][:, :, :], ALU.add).then_inc(route, 1)
            dve.wait_ge(route, 12)
            dve.wait_ge(expo_done, 1)
            v.tensor_tensor(s["picked"][:, :, :], s["picked"][:, :, :], s["expo"][:, :, :], ALU.mult).then_inc(route, 1)
            dve.wait_ge(route, 13)
            v.tensor_reduce(top["total"][:, :], s["picked"][:, :, :], AX.X, ALU.add).then_inc(route, 1)
            dve.wait_ge(route, 14)
            v.reciprocal(top["inv"][:, :], top["total"][:, :]).then_inc(route, 1)
            dve.wait_ge(route, 15)
            v.tensor_tensor(s["weight"][:, :, :], s["picked"][:, :, :], over_experts(top["inv"]), ALU.mult).then_inc(route, 1)
            dve.wait_ge(route, 16)

            def add_expert(n, e):
                dve.wait_ge(down_psum, n * E + e + 1)
                dve.wait_ge(added, (n * E + e) * TC + TC)
                for b in range(TC):
                    dst = x1[:, bass.ds(n * TC + b, 1), :].rearrange("p o f -> p (o f)")
                    w = s["weight"][:, bass.ds(n * TC + b, 1), e]
                    v.scalar_tensor_tensor(dst, down_bank[e % 2][:, b * P:(b + 1) * P], w, dst, ALU.mult, ALU.add).then_inc(added, 1)

            dve.sem_inc(added, TC)
            with dve.Fori(0, CHUNKS) as n:
                for e in range(E):
                    for c in range(FC):
                        i = e * FC + c
                        dve.wait_ge(gate_done, n * (E * FC) + i + 3)
                        dve.wait_ge(up_psum, n * (E * FC) + i + 1)
                        if e >= 2 and c == 0:
                            dve.wait_ge(down_psum, n * E + e - 1)
                        v.tensor_tensor(hid[:, e % 2, c, :], gate[:, i % 2, :], up_bank[i % 2][:, :], ALU.mult).then_inc(hid_done, 1)
                        if c == 2 and e > 0:
                            add_expert(n, e - 1)
                add_expert(n, E - 1)


R_HEADS, R_DK, R_DV = 4, 32, 64


def retention_tables():
    half = R_DK // 2
    inv_freq = (1.0 / np.float32(10000.0) ** (np.arange(0, R_DK, 2, dtype=np.float32) / R_DK)).astype(np.float32)
    freqs = np.arange(TOKENS, dtype=np.float32)[:, None] * inv_freq[None, :]
    cos, sin = np.cos(freqs), np.sin(freqs)
    c = np.concatenate([cos, cos], 1)
    s = np.concatenate([-sin, sin], 1)
    scale = np.repeat([R_DK ** -0.5, 1.0], R_HEADS)
    wide = {}
    for name, t in (("ret_cos", c), ("ret_sin", s)):
        w = scale[None, :, None] * t[:, None, :]
        wide[name] = w.reshape(BPS, P, -1).transpose(1, 0, 2).reshape(P, -1)
    gamma = 1.0 - 2.0 ** (-5.0 - np.arange(R_HEADS))
    j, i = np.arange(P)[:, None], np.arange(TOKENS)[None, :]
    d0 = np.where(i >= j, gamma[:, None, None] ** np.maximum(i - j, 0), 0.0)
    d1 = d0[:, :, 0:P]
    decay = np.concatenate([d0, d1], 2)
    wide["ret_decay"] = decay.transpose(1, 0, 2).reshape(P, -1)
    return wide


def retention(nc, wqkv_dram, wg_dram, wo_dram, gnorm_dram, x1, xn_t, const, eps):
    V_WIDE = R_HEADS * R_DV
    with ExitStack() as stack:
        m = Memory(nc, stack, "ret")
        wqkv = m.sb("wqkv", [P, 512])
        wg = m.sb("wg", [P, V_WIDE])
        wo = m.sb("wo", [P, 2, D])
        gnorm = m.sb("gnorm", [P, R_DV])
        gate = m.sb("gate", [P, BLOCKS, V_WIDE])
        xs = m.sb("xs", [P, TOKENS])
        raw = m.sb("raw", [P, BPS, 256])
        part1 = m.sb("part1", [P, BPS, 256])
        part2 = m.sb("part2", [P, BPS, 256])
        rot = m.sb("rot", [P, BPS, 256])
        v = m.sb("v", [P, BPS, V_WIDE])
        q_t = m.sb("q_t", [P, R_HEADS, TOKENS])
        k_t = m.sb("k_t", [P, TOKENS])
        probs_t = m.sb("probs_t", [P, R_HEADS, 3 * P])
        o_raw = m.sb("o_raw", [P, BPS * R_HEADS, R_DV])
        sq = m.sb("sq", [P, BPS * R_HEADS, R_DV])
        ms = m.sb("ms", [P, BPS * R_HEADS])
        ln_ms = m.sb("ln_ms", [P, BPS * R_HEADS])
        rstd = m.sb("rstd", [P, BPS * R_HEADS])
        o_n = m.sb("o_n", [P, BPS * R_HEADS, R_DV])
        gated = m.sb("gated", [P, BPS * R_HEADS, R_DV])
        o_t = m.sb("o_t", [P, BPS, 2, P])
        bank = m.banks()
        w_in, zeroed = m.sem("w_in"), m.sem("zeroed")
        gate_psum, gate_done, xs_ready = m.sem("gate_psum"), m.sem("gate_done"), m.sem("xs_ready")
        qkv_psum, raw_ready, rot_steps, rot_ready = m.sem("qkv_psum"), m.sem("raw_ready"), m.sem("rot_steps"), m.sem("rot_ready")
        part1_done = m.sem("part1_done")
        qk_turned, qk_sb, scores_ready, decayed = m.sem("qk_turned"), m.sem("qk_sb"), m.sem("scores_ready"), m.sem("decayed")
        out_psum, o_copied, squared, ms_done, ln_done, rstd_done = (m.sem(n) for n in (
            "out_psum", "o_copied", "squared", "ms_done", "ln_done", "rstd_done"))
        norm_steps, gated_done, o_turned, o_sb, wo_psum, added = (m.sem(n) for n in (
            "norm_steps", "gated_done", "o_turned", "o_sb", "wo_psum", "added"))
        block = stack.enter_context(nc.Block())
        NBH = BPS * R_HEADS

        @block.sync
        def _(sp):
            sp.dma_start(wqkv[:, :], wqkv_dram).then_inc(w_in, 16)
            sp.dma_start(wg[:, :], wg_dram).then_inc(w_in, 16)
            sp.dma_start(wo[:, :, :], wo_dram.rearrange("(c p) f -> p c f", p=P)).then_inc(w_in, 16)
            sp.dma_start(gnorm[:, :], gnorm_dram.partition_broadcast(P)).then_inc(w_in, 16)

        @block.gpsimd
        def _(pool):
            nc.gpsimd.memset(q_t[:, :, :], 0.0).then_inc(zeroed, 1)
            cos = const[:, slice_of("ret_cos")].rearrange("p (b n) -> p b n", b=BPS)

            def job(s):
                pool.wait_ge(qkv_psum, s * BPS + 1)
                nc.gpsimd.tensor_copy(xs[:, :], xn_t[:, bass.ds(s * TOKENS, TOKENS)]).then_inc(xs_ready, 1)
                pool.wait_ge(raw_ready, BPS * (s + 1))
                nc.gpsimd.tensor_tensor(part1[:, :, :], raw[:, :, :], cos, ALU.mult).then_inc(part1_done, 1)

            with pool.Fori(0, SEQS) as s:
                job(s)

        @block.tensor
        def _(pe):
            ident = const[:, slice_of("ident")]
            pe.wait_ge(w_in, 64)
            for k in range(BLOCKS):
                if k >= 4 and k % 2 == 0:
                    pe.wait_ge(gate_done, k // 2 - 1)
                last = nc.tensor.matmul(bank[k // 2 % 2][:, k % 2 * V_WIDE:(k % 2 + 1) * V_WIDE],
                                        xn_t[:, k * P:(k + 1) * P], wg[:, :], start=True, stop=True)
                if k % 2 == 1:
                    last.then_inc(gate_psum, 1)
            pe.wait_ge(gate_done, BLOCKS // 2)
            pe.sem_inc(qkv_psum, 1)
            with pe.Fori(0, SEQS) as s:
                pe.wait_ge(xs_ready, s + 1)
                for b in range(BPS):
                    last = nc.tensor.matmul(bank[b][:, :], xs[:, b * P:(b + 1) * P], wqkv[:, :], start=True, stop=True)
                    last.then_inc(qkv_psum, 1)
                pe.wait_ge(rot_ready, s + 1)
                for half in range(2):
                    for b in range(BPS):
                        at = (half * BPS + b) * P
                        last = nc.tensor.transpose(bank[2][:, at:at + P], rot[:, b, half * P:(half + 1) * P], ident)
                last.then_inc(qk_turned, 1)
                pe.wait_ge(qk_sb, s + 1)
                for h in range(R_HEADS):
                    sc = bank[3 + h]
                    nc.tensor.matmul(sc[:, 0:TOKENS], k_t[:, 0:P], q_t[:, h, :], start=True, stop=True)
                    nc.tensor.matmul(sc[:, TOKENS:3 * P], k_t[:, P:TOKENS], q_t[:, h, P:TOKENS],
                                     start=True, stop=True).then_inc(scores_ready, 1)
                for h in range(R_HEADS):
                    pe.wait_ge(decayed, s * R_HEADS + h + 1)
                    vs = slice(h * R_DV, (h + 1) * R_DV)
                    o0 = bank[7][:, vs]
                    o1 = bank[7][:, V_WIDE + h * R_DV:V_WIDE + (h + 1) * R_DV]
                    nc.tensor.matmul(o0, probs_t[:, h, 0:P], v[:, 0, vs], start=True, stop=True)
                    nc.tensor.matmul(o1, probs_t[:, h, P:TOKENS], v[:, 0, vs], start=True, stop=False)
                    last = nc.tensor.matmul(o1, probs_t[:, h, TOKENS:3 * P], v[:, 1, vs], start=False, stop=True)
                last.then_inc(out_psum, 1)
                pe.wait_ge(gated_done, s + 1)
                for b in range(BPS):
                    for c in range(2):
                        at = (b * 2 + c) * P
                        last = nc.tensor.transpose(bank[2][:, at:at + P],
                                                   gated[:, b * R_HEADS + 2 * c:b * R_HEADS + 2 * c + 2, :].rearrange("p h d -> p (h d)"), ident)
                last.then_inc(o_turned, 1)
                pe.wait_ge(o_sb, s + 1)
                for b in range(BPS):
                    for c in range(2):
                        last = nc.tensor.matmul(bank[b][:, 0:D], o_t[:, b, c, :], wo[:, c, :], start=c == 0, stop=c == 1)
                    last.then_inc(wo_psum, 1)
                pe.wait_ge(added, (s + 1) * BPS)

        @block.scalar
        def _(act):
            for k in range(BLOCKS // 2):
                act.wait_ge(gate_psum, k + 1)
                nc.scalar.activation(gate[:, 2 * k:2 * k + 2, :], bank[k % 2][:, :].rearrange("p (b n) -> p b n", b=2),
                                     ACT.Silu).then_inc(gate_done, 1)
            with act.Fori(0, SEQS) as s:
                for b in range(BPS):
                    act.wait_ge(qkv_psum, s * BPS + b + 2)
                    nc.scalar.activation(raw[:, b, :], bank[b][:, 0:256], ACT.Copy)
                    nc.scalar.activation(v[:, b, :], bank[b][:, 256:512], ACT.Copy).then_inc(raw_ready, 1)
                act.wait_ge(qk_turned, s + 1)
                for h in range(R_HEADS):
                    rows = slice(h * R_DK, (h + 1) * R_DK)
                    nc.scalar.activation(q_t[rows, h, :], bank[2][rows, 0:TOKENS], ACT.Copy)
                nc.scalar.activation(k_t[:, :], bank[2][:, TOKENS:2 * TOKENS], ACT.Copy).then_inc(qk_sb, 1)
                act.wait_ge(out_psum, s + 1)
                nc.scalar.activation(o_raw[:, :, :], bank[7][:, :].rearrange("p (n d) -> p n d", d=R_DV), ACT.Copy).then_inc(o_copied, 1)
                nc.scalar.activation(sq[:, :, :], bank[7][:, :].rearrange("p (n d) -> p n d", d=R_DV), ACT.Square).then_inc(squared, 1)
                act.wait_ge(ms_done, s + 1)
                nc.scalar.activation(ln_ms[:, :], ms[:, :], ACT.Ln, scale=1.0 / R_DV, bias=eps[:, 0:1]).then_inc(ln_done, 1)
                act.wait_ge(ln_done, s + 1)
                nc.scalar.activation(rstd[:, :], ln_ms[:, :], ACT.Exp, scale=-0.5).then_inc(rstd_done, 1)
                act.wait_ge(o_turned, s + 1)
                nc.scalar.activation(o_t[:, :, :, :], bank[2][:, :].rearrange("p (b c n) -> p b c n", b=BPS, c=2), ACT.Copy).then_inc(o_sb, 1)

        @block.vector
        def _(dve):
            sin = const[:, slice_of("ret_sin")].rearrange("p (b n) -> p b n", b=BPS)
            decay = const[:, slice_of("ret_decay")].rearrange("p (h n) -> p h n", h=R_HEADS)
            hd = R_DK // 2

            def halves(t, which):
                return t.rearrange("p b (n two d) -> p two (b n) d", two=2, d=hd)[:, which]

            dve.wait_ge(w_in, 64)
            dve.wait_ge(zeroed, 1)
            with dve.Fori(0, SEQS) as s:
                dve.wait_ge(raw_ready, BPS * (s + 1))
                for out_half in range(2):
                    last = nc.vector.tensor_tensor(halves(part2[:, :, :], out_half), halves(raw[:, :, :], 1 - out_half),
                                                   halves(sin, out_half), ALU.mult)
                last.then_inc(rot_steps, 1)
                dve.wait_ge(rot_steps, s + 1)
                dve.wait_ge(part1_done, s + 1)
                nc.vector.tensor_tensor(rot[:, :, :], part1[:, :, :], part2[:, :, :], ALU.add).then_inc(rot_ready, 1)
                for h in range(R_HEADS):
                    dve.wait_ge(scores_ready, s * R_HEADS + h + 1)
                    nc.vector.tensor_tensor(probs_t[:, h, :], bank[3 + h][:, 0:3 * P], decay[:, h, :], ALU.mult).then_inc(decayed, 1)
                dve.wait_ge(squared, s + 1)
                nc.vector.tensor_reduce(ms[:, :], sq[:, :, :], AX.X, ALU.add).then_inc(ms_done, 1)
                g = gnorm[:, :].unsqueeze(1).broadcast_to([P, NBH, R_DV])
                dve.wait_ge(o_copied, s + 1)
                nc.vector.tensor_tensor(o_n[:, :, :], o_raw[:, :, :], g, ALU.mult).then_inc(norm_steps, 1)
                dve.wait_ge(norm_steps, 2 * s + 1)
                gt = gate[:, bass.ds(s * BPS, BPS), :].rearrange("p b (h d) -> p (b h) d", d=R_DV)
                nc.vector.tensor_tensor(o_n[:, :, :], o_n[:, :, :], gt, ALU.mult).then_inc(norm_steps, 1)
                dve.wait_ge(norm_steps, 2 * s + 2)
                dve.wait_ge(rstd_done, s + 1)
                nc.vector.tensor_tensor(gated[:, :, :], o_n[:, :, :], rstd[:, :].unsqueeze(2).broadcast_to([P, NBH, R_DV]),
                                        ALU.mult).then_inc(gated_done, 1)
                for b in range(BPS):
                    dve.wait_ge(wo_psum, s * BPS + b + 1)
                    dst = x1[:, bass.ds(s * BPS + b, 1), :].rearrange("p o f -> p (o f)")
                    nc.vector.tensor_tensor(dst, bank[b][:, 0:D], dst, ALU.add).then_inc(added, 1)


LAYERS, HEADS, DIM, WINDOW = 6, 16, 64, 32
PAIRS = HEADS // 2
HIDDEN = 341
H_ROWS = (128, 128, 85)
QK_SCALE = 8.0
VEC = {"ln_g": 0, "ln_b": 1, "b2": 2, "b_a": 3, "b_gate": 6}
N_VEC = 9


def rotary_base():
    half = np.arange(0, DIM, 2, dtype=np.float32)
    inv_freq = (1.0 / np.float32(10000.0) ** (half / np.float32(DIM))).astype(np.float32)
    t = np.arange(TOKENS, dtype=np.float32)
    freqs = t[:, None] * inv_freq[None, :]
    base = ((half + np.float32(0.4 * DIM)) / np.float32(1.4 * DIM)).astype(np.float32)
    power = ((t - TOKENS // 2) / (WINDOW // 2)).astype(np.float32)
    scale = base[None, :] ** power[:, None]
    scale = np.concatenate([scale, scale], 1)
    cos = np.concatenate([np.cos(freqs)] * 2, 1)
    sin = np.concatenate([-np.sin(freqs), np.sin(freqs)], 1)
    t4 = np.stack([cos * scale, sin * scale, cos / scale, sin / scale], 1)
    return t4.reshape(BPS, P, 4 * DIM).transpose(1, 0, 2).reshape(P, -1)


def band_masks():
    i, j = np.arange(P)[:, None], np.arange(P)[None, :]
    own = np.where((j <= i) & (i - j <= WINDOW), 0.0, MASKED)
    before = np.where(i <= j[:, 0:WINDOW], 0.0, MASKED)
    return {"band": np.tile(own, (1, 4)), "band_prev": np.tile(before, (1, HEADS))}


def transformer(nc, t, y_t, const, ident_f, ident_b, eps):
    with ExitStack() as stack:
        m = Memory(nc, stack, "tr")
        wqkv = m.sb("wqkv", [P, 3 * HEADS * DIM])
        wo = m.sb("wo", [P, PAIRS, D])
        w1 = m.sb("w1", [P, 2 * HIDDEN])
        w2 = m.sb("w2", [P, 3, D])
        vec = m.sb("vec", [P, N_VEC])
        qk_scales = m.sb("qk_scales", [P, 4 * DIM])
        table = m.sb("table", [P, BPS, 4, DIM])
        ones = m.sb("ones", [P, P])
        carrier = m.sb("carrier", [P, 1])
        band_b, prev_b = m.sb("band_b", [P, 4 * P], BF16), m.sb("prev_b", [P, 512], BF16)
        ln_q = m.sb("ln_q", [P, 2])
        xs = m.sb("xs", [P, BPS, P])
        raw, sq, part1, part2, rot = (m.sb(n, [P, 2, 512]) for n in ("raw", "sq", "part1", "part2", "rot"))
        norm2 = m.sb("norm2", [P, BPS, 4, 8])
        ln_n = m.sb("ln_n", [P, 2, 8])
        q_even, q_odd, k_t = (m.sb(n, [P, PAIRS, TOKENS]) for n in ("q_even", "q_odd", "k_t"))
        v = m.sb("v", [P, BPS, HEADS * DIM])
        top, top_prev, neg_top = m.sb("top", [P, 8, 4]), m.sb("top_prev", [WINDOW, 4, 4]), m.sb("neg_top", [P, 8, 4])
        sums, sum_prev, inv = m.sb("sums", [P, 8, 4]), m.sb("sum_prev", [WINDOW, 4, 4]), m.sb("inv", [P, 8, 4])
        probs = m.sb("probs", [P, 4, 4, P])
        arg_prev = m.sb("arg_prev", [WINDOW, 4, 4, WINDOW])
        probs_prev = m.sb("probs_prev", [WINDOW, 4, 4, WINDOW])
        probs_t = m.sb("probs_t", [P, 2, 4 * P])
        probs_prev_t = m.sb("probs_prev_t", [P, 4, 4 * WINDOW])
        o_t = m.sb("o_t", [P, PAIRS, TOKENS])
        xf, centred, sq_f, ln_var, rstd_f, scaled, xn_f = (m.sb(n, [P, TOKENS]) for n in (
            "xf", "centred", "sq_f", "ln_var", "rstd_f", "scaled", "xn_f"))
        gelu = m.sb("gelu", [P, 3, TOKENS])
        hid = m.sb("hid", [P, 3, TOKENS])
        bank = m.banks()
        unit_bank, v_bank, score_bank, q_turn_bank, p_turn_bank, out_bank, misc_bank = (
            bank[0], bank[1], bank[2:4], bank[4], bank[5], bank[6], bank[7])
        w1_bank = (bank[1], bank[0], bank[1])
        S = {n: m.sem(n) for n in (
            "const_done", "zeroed", "wqkv_in", "wo_in", "ffn_in", "scales_in", "table_done",
            "xs_ready", "unit_psum", "raw_ready", "part1_done", "norm2_done", "ln_n_done", "inv_norm_done",
            "part2_done", "rot_done", "k_scaled", "unit_turned", "q_even_sb", "q_odd_sb", "k_sb",
            "v_psum", "v_sb", "prev_psum", "scores_psum", "top_done", "top_joined", "neg_top_done", "exp_done",
            "arg_scaled", "arg_ready", "exp_prev_done", "sum_prev_done", "sums_joined", "inv_done",
            "prev_normed", "prev_turned", "probs_ready", "turned", "turned_sb", "out_psum", "o_sb", "wo_psum", "y_added",
            "xf_ready", "mean_psum", "centred_done", "sq_f_done", "var_psum", "ln_var_done", "rstd_f_done",
            "scaled_done", "xn_f_done", "w1_psum", "gelu_done", "hid_done", "w2_psum", "ffn_added")}
        block = stack.enter_context(nc.Block())
        K = 8


        def jobs(eng, body, ffn_alone, layer_start):
            with eng.Fori(0, LAYERS) as layer:
                layer_start(layer)
                body(layer, 0, layer * SEQS, False, True)
                with eng.Fori(1, SEQS - 1) as s:
                    body(layer, s, layer * SEQS + s, True, True)
                body(layer, SEQS - 1, layer * SEQS + SEQS - 1, True, False)
                ffn_alone(layer * SEQS + SEQS - 1)

        def plain_wait(eng):
            eng.wait_ge(S["zeroed"], 7)

        def units_of(slot, J):
            return (8 * J + 4 + slot, 1, slot) if slot < 4 else (8 * J + 4 + slot, 0, slot - 4)

        def first_unit(u, J):
            return 8 * J + u, 0, u

        def y_tokens(s, start, n):
            return y_t[:, bass.ds(s * TOKENS + start, n)]

        @block.sync
        def _(sp):
            def load(layer):
                sp.wait_ge(S["v_psum"], layer * (4 * SEQS) + 3)
                sp.dma_start(wqkv[:, :], t["tr_qkv"][bass.ds(layer, 1), :, :].rearrange("o p n -> p (o n)")).then_inc(S["wqkv_in"], 16)
                sp.wait_ge(S["table_done"], layer + 1)
                sp.dma_start(qk_scales[:, :], t["tr_scales"][bass.ds(layer, 1), :].partition_broadcast(P).rearrange("p o n -> p (o n)")
                             ).then_inc(S["scales_in"], 16)
                sp.wait_ge(S["wo_psum"], layer * SEQS + 1)
                sp.dma_start(wo[:, :, :], t["tr_o"][bass.ds(layer, 1), :, :].rearrange("o (c p) f -> p (o c) f", p=P)).then_inc(S["wo_in"], 16)
                sp.wait_ge(S["ffn_added"], layer * SEQS + 1)
                sp.dma_start(w1[:, :], t["tr_w1"][bass.ds(layer, 1), :, :].rearrange("o p n -> p (o n)")).then_inc(S["ffn_in"], 16)
                for c, rows in enumerate(H_ROWS):
                    sp.dma_start(w2[0:rows, c, :], t["tr_w2"][bass.ds(layer, 1), c * P:c * P + rows, :].rearrange("o p n -> p (o n)")
                                 ).then_inc(S["ffn_in"], 16)
                sp.dma_start(vec[:, :], t["tr_vec"][bass.ds(layer, 1), :, :].rearrange("o p n -> p (o n)")).then_inc(S["ffn_in"], 16)

            with sp.Fori(0, LAYERS) as layer:
                load(layer)

        @block.gpsimd
        def _(pool):
            g = nc.gpsimd
            g.memset(ones[:, :], 1.0 / D).then_inc(S["zeroed"], 1)
            pool.wait_ge(S["zeroed"], 1)
            g.memset(xs[:, :, :], 0.0).then_inc(S["zeroed"], 1)
            pool.wait_ge(S["zeroed"], 2)
            g.memset(xf[:, :], 0.0).then_inc(S["zeroed"], 1)
            pool.wait_ge(S["zeroed"], 3)
            g.memset(q_even[:, :, :], 0.0).then_inc(S["zeroed"], 1)
            pool.wait_ge(S["zeroed"], 4)
            g.memset(q_odd[:, :, :], 0.0).then_inc(S["zeroed"], 1)
            pool.wait_ge(S["zeroed"], 5)
            g.memset(ln_q[:, 0:1], float(np.log(QK_SCALE) + 8 * np.log(2.0))).then_inc(S["zeroed"], 1)
            pool.wait_ge(S["zeroed"], 6)
            g.memset(ln_q[:, 1:2], float(8 * np.log(2.0))).then_inc(S["zeroed"], 1)
            pool.wait_ge(S["zeroed"], 7)
            h = D // 2

            def carry_wait():
                g.tensor_tensor(carrier[0:h, :], ones[0:h, 0:1], ones[0:h, 0:1], ALU.mult)

            def products_written(pairs, extra=0):
                pool.wait_ge(S["part1_done"], 2 * pairs + extra)
                pool.wait_ge(S["k_scaled"], pairs)

            def load_xs(s, J, b):
                pool.wait_ge(S["v_psum"], 4 * J + 2 * b + 1)
                carry_wait()
                g.tensor_copy(xs[0:h, b, :], y_t[0:h, bass.ds(s * TOKENS + b * P, P)]).then_inc(S["xs_ready"], 1)
                if b == 0:
                    g.tensor_copy(xs[h:D, 0, 1:P], y_t[h:D, bass.ds(s * TOKENS, P - 1)]).then_inc(S["xs_ready"], 1)
                else:
                    g.tensor_copy(xs[h:D, 1, :], y_t[h:D, bass.ds(s * TOKENS + P - 1, P)]).then_inc(S["xs_ready"], 1)
                pool.wait_ge(S["xs_ready"], 4 * J + 2 * b + 2)

            def unit(U, b, u):
                kind = u % 2
                pool.wait_ge(S["raw_ready"], U + 1)
                pool.wait_ge(S["rot_done"], U + 1)
                src = raw[:, u % 2, :].rearrange("p (n d) -> p n d", d=DIM)
                cos = table[:, b, 2 * kind, :].unsqueeze(1).broadcast_to([P, 8, DIM])
                g.tensor_tensor(part1[:, u % 2, :].rearrange("p (n d) -> p n d", d=DIM), src, cos, ALU.mult).then_inc(S["part1_done"], 1)

            def scale_k(U, b, u):
                pool.wait_ge(S["rot_done"], U + 3)
                pool.wait_ge(S["inv_norm_done"], U + 1)
                r = rot[:, u % 2, :].rearrange("p (n d) -> p n d", d=DIM)
                g.tensor_tensor(r, r, norm2[:, b, u, :].unsqueeze(2).broadcast_to([P, 8, DIM]), ALU.mult).then_inc(S["k_scaled"], 1)

            def one_unit(U, b, u):
                unit(U, b, u)
                if u % 2:
                    scale_k(U, b, u)

            def load_xf(s, J):
                pool.wait_ge(S["centred_done"], J + 1)
                pool.wait_ge(S["y_added"], J + 1)
                carry_wait()
                g.tensor_copy(xf[0:h, :], y_t[0:h, bass.ds(s * TOKENS, TOKENS)]).then_inc(S["xf_ready"], 1)
                g.tensor_copy(xf[h:D, 1:TOKENS], y_t[h:D, bass.ds(s * TOKENS, TOKENS - 1)]).then_inc(S["xf_ready"], 1)
                pool.wait_ge(S["xf_ready"], 2 * J + 2)

            def body(layer, s, J, has_ffn, has_next):
                if has_ffn:
                    products_written(4 * J + 2)
                    load_xf(s - 1, J - 1)
                for slot in range(K):
                    if slot < 4 or has_next:
                        if slot == 3 and has_next:
                            products_written(4 * J + 3, 1)
                            load_xs(s + 1, J + 1, 0)
                        one_unit(*units_of(slot, J))
                        if slot == 5:
                            products_written(4 * J + 5)
                            load_xs(s + 1, J + 1, 1)

            def layer_start(layer):
                J = layer * SEQS
                pool.wait_ge(S["ffn_added"], J + 1)
                load_xs(0, J, 0)
                load_xs(0, J, 1)
                pool.wait_ge(S["table_done"], layer + 2)
                for u in range(4):
                    one_unit(*first_unit(u, J))

            def ffn_alone(F):
                products_written(4 * F + 4)
                load_xf(SEQS - 1, F)

            jobs(pool, body, ffn_alone, layer_start)

        @block.tensor
        def _(pe):
            mm = nc.tensor.matmul

            def unit_project(U, b, u, first=False):
                if not first:
                    pe.wait_ge(S["raw_ready"], U)
                half = u // 2
                at = (u % 2) * HEADS * DIM + half * 512
                mm(unit_bank[:, :], xs[:, b, :], wqkv[:, at:at + 512], start=True, stop=True).then_inc(S["unit_psum"], 1)

            def unit_turn(U, b, u, J_unit):
                if u % 2:
                    pe.wait_ge(S["k_scaled"], 4 * J_unit + 2 * b + u // 2 + 1)
                else:
                    pe.wait_ge(S["rot_done"], U + 3)
                if u % 2:
                    pe.wait_ge(S["q_even_sb"], 4 * J_unit + 2 * b + u // 2 + 2)
                    pe.wait_ge(S["q_odd_sb"], 4 * J_unit + 2 * b + u // 2 + 2)
                else:
                    pe.wait_ge(S["k_sb"], 4 * J_unit + 2 * b + u // 2 + 1)
                for i in range(4):
                    last = nc.tensor.transpose(q_turn_bank[:, i * P:(i + 1) * P], rot[:, u % 2, i * P:(i + 1) * P], ident_f)
                last.then_inc(S["unit_turned"], 1)

            def v_project(J, u):
                b, half = u // 2, u % 2
                if u:
                    pe.wait_ge(S["v_sb"], 4 * J + u)
                at = 2 * HEADS * DIM + half * 512
                mm(v_bank[:, :], xs[:, b, :], wqkv[:, at:at + 512], start=True, stop=True).then_inc(S["v_psum"], 1)

            def scores(J, k, has_ffn):
                b, g4 = k // 4, k % 4
                if k % 2 == 0:
                    n = 4 * J + 2 * b + g4 // 2 + 1 + 1
                    pe.wait_ge(S["q_even_sb"], n)
                    pe.wait_ge(S["q_odd_sb"], n)
                    pe.wait_ge(S["k_sb"], n)
                if k == 4:
                    if has_ffn:
                        pe.wait_ge(S["ln_var_done"], J)
                    else:
                        pe.wait_ge(S["ffn_added"], J + 1)
                    for name in ("q_even_sb", "q_odd_sb"):
                        pe.wait_ge(S[name], n + 1)
                    scores_before(J)
                pe.wait_ge(S["exp_done"], K * J + k - 1 + 2)
                sc = score_bank[k % 2]
                mm(sc[:, :], ident_b[:, :], band_b[:, :], start=True, stop=False)
                for i in range(4):
                    h = 4 * g4 + i
                    q = (q_even, q_odd)[h % 2]
                    tok = slice(b * P, (b + 1) * P)
                    last = mm(sc[:, i * P:(i + 1) * P], q[:, h // 2, tok], k_t[:, h // 2, tok], start=False, stop=i == 3)
                last.then_inc(S["scores_psum"], 1)

            def scores_before(J):
                mm(misc_bank[0:WINDOW, :], ident_b[:, 0:WINDOW], prev_b[:, :], start=True, stop=False)
                for h in range(HEADS):
                    q = (q_even, q_odd)[h % 2]
                    last = mm(misc_bank[0:WINDOW, h * WINDOW:(h + 1) * WINDOW], q[:, h // 2, P:P + WINDOW],
                              k_t[:, h // 2, P - WINDOW:P], start=False, stop=h == HEADS - 1)
                last.then_inc(S["prev_psum"], 1)

            def turn_probs(J, k):
                pe.wait_ge(S["probs_ready"], K * J + k + 1)
                pe.wait_ge(S["turned_sb"], K * J + k + 1)
                for i in range(4):
                    last = nc.tensor.transpose(p_turn_bank[:, i * P:(i + 1) * P], probs[:, k % 4, i, :], ident_f)
                last.then_inc(S["turned"], 1)

            def outputs(J, k):
                b, g4 = k // 4, k % 4
                if k % 2 == 0:
                    pe.wait_ge(S["o_sb"], 4 * J + k // 2 + 1)
                    pe.wait_ge(S["v_sb"], 4 * J + 2 * b + (k % 4) // 2 + 1)
                pe.wait_ge(S["turned_sb"], K * J + k + 2)
                if b:
                    pe.wait_ge(S["prev_turned"], 4 * J + k - 4 + 1)
                for i in range(4):
                    h = 4 * g4 + i
                    rows = slice(h % 2 * DIM, (h % 2 + 1) * DIM)
                    at = (h // 2 % 4) * P
                    hd = slice(h * DIM, (h + 1) * DIM)
                    last = mm(out_bank[rows, at:at + P], v[:, b, hd], probs_t[:, k % 2, i * P:(i + 1) * P], start=True, stop=b == 0)
                    if b:
                        last = mm(out_bank[rows, at:at + WINDOW], v[P - WINDOW:P, 0, hd],
                                  probs_prev_t[P - WINDOW:P, g4, i * WINDOW:(i + 1) * WINDOW], start=False, stop=True)
                last.then_inc(S["out_psum"], 1)

            def project_out(J):
                pe.wait_ge(S["o_sb"], 4 * J + 4 + 1)
                for c in range(PAIRS):
                    last = mm(bank[0][:, 0:TOKENS], wo[:, c, :], o_t[:, c, :], start=c == 0, stop=c == PAIRS - 1)
                last.then_inc(S["wo_psum"], 1)

            def ffn_mean(F):
                pe.wait_ge(S["ffn_added"], F + 1)
                pe.wait_ge(S["xf_ready"], 2 * F + 2)
                mm(misc_bank[:, 0:TOKENS], ones[:, :], xf[:, :], start=True, stop=True).then_inc(S["mean_psum"], 1)

            def ffn_var(F):
                pe.wait_ge(S["sq_f_done"], F + 1)
                mm(misc_bank[:, 0:TOKENS], ones[:, :], sq_f[:, :], start=True, stop=True).then_inc(S["var_psum"], 1)

            def ffn_w1(F, c):
                rows = H_ROWS[c]
                if c == 0:
                    pe.wait_ge(S["xn_f_done"], F + 1)
                if c == 2:
                    pe.wait_ge(S["hid_done"], 3 * F + 1)
                for i in range(2):
                    at = i * HIDDEN + c * P
                    last = mm(w1_bank[c][0:rows, i * TOKENS:(i + 1) * TOKENS], w1[:, at:at + rows], xn_f[:, :], start=True, stop=True)
                last.then_inc(S["w1_psum"], 1)

            def ffn_w2(F):
                pe.wait_ge(S["hid_done"], 3 * F + 3)
                for c, rows in enumerate(H_ROWS):
                    last = mm(misc_bank[:, 0:TOKENS], w2[0:rows, c, :], hid[0:rows, c, :], start=c == 0, stop=c == 2)
                last.then_inc(S["w2_psum"], 1)

            def body(layer, s, J, has_ffn, has_next):
                if has_ffn:
                    ffn_mean(J - 1)
                for k in range(K + 2):
                    if k < K:
                        scores(J, k, has_ffn)
                        if k < 4 or has_next:
                            U, b, u = units_of(k, J)
                            if k % 4 == 0:
                                pe.wait_ge(S["xs_ready"], 4 * J + 4 + k // 2)
                            unit_project(U, b, u)
                        if k < 4:
                            v_project(J, k)
                    if k == 1 and has_ffn:
                        ffn_var(J - 1)
                    if k >= 1 and (k <= 4 or has_next) and k - 1 < K:
                        U, b, u = units_of(k - 1, J)
                        unit_turn(U, b, u, J if k <= 4 else J + 1)
                    if k == K and has_ffn:
                        pe.wait_ge(S["v_sb"], 4 * J + 4)
                        ffn_w1(J - 1, 0)
                        ffn_w1(J - 1, 1)
                    if k >= 2:
                        outputs(J, k - 2)
                    if k == K and has_ffn:
                        ffn_w1(J - 1, 2)
                    if 1 <= k <= K:
                        turn_probs(J, k - 1)
                if has_ffn:
                    ffn_w2(J - 1)
                if has_ffn:
                    pe.wait_ge(S["hid_done"], 3 * J)
                project_out(J)
                plain_wait(pe)
                pe.wait_ge(S["y_added"], J + 1)

            def layer_start(layer):
                J = layer * SEQS
                pe.wait_ge(S["wqkv_in"], 16 * (layer + 1))
                pe.wait_ge(S["xs_ready"], 4 * J + 4)
                for u in range(5):
                    if u < 4:
                        unit_project(*first_unit(u, J), first=u == 0)
                    if u:
                        unit_turn(*first_unit(u - 1, J), J)
                plain_wait(pe)
                pe.wait_ge(S["wo_in"], 16 * (layer + 1))
                pe.wait_ge(S["ffn_in"], 16 * 5 * (layer + 1))

            def ffn_alone(F):
                ffn_mean(F)
                ffn_var(F)
                for c in range(3):
                    ffn_w1(F, c)
                ffn_w2(F)
                plain_wait(pe)
                pe.wait_ge(S["ffn_added"], F + 2)

            pe.sem_inc(S["v_psum"], 3)
            pe.sem_inc(S["wo_psum"], 1)
            pe.wait_ge(S["const_done"], 2)
            pe.wait_ge(S["zeroed"], 7)
            jobs(pe, body, ffn_alone, layer_start)

        @block.scalar
        def _(act):
            a = nc.scalar.activation

            def unit_copy(U, b, u):
                act.wait_ge(S["unit_psum"], U + 1)
                act.wait_ge(S["rot_done"], U + 1)
                a(raw[:, u % 2, :], unit_bank[:, :], ACT.Copy)
                a(sq[:, u % 2, :], unit_bank[:, :], ACT.Square).then_inc(S["raw_ready"], 1)

            def unit_norm(U, b, u):
                act.wait_ge(S["norm2_done"], 2 * U + 2)
                a(ln_n[:, u % 2, :], norm2[:, b, u, :], ACT.Ln, scale=2.0 ** 16).then_inc(S["ln_n_done"], 1)
                act.wait_ge(S["ln_n_done"], U + 1)
                a(norm2[:, b, u, :], ln_n[:, u % 2, :], ACT.Exp, scale=-0.5, bias=ln_q[:, u % 2:u % 2 + 1]).then_inc(S["inv_norm_done"], 1)

            def unit_out(U, b, u):
                act.wait_ge(S["unit_turned"], U + 1 + 2)
                src = q_turn_bank[:, :].rearrange("p (c t) -> p c t", t=P)
                pairs, tok = slice(u // 2 * 4, u // 2 * 4 + 4), slice(b * P, (b + 1) * P)
                if u % 2:
                    a(k_t[:, pairs, tok], src, ACT.Copy).then_inc(S["k_sb"], 1)
                else:
                    a(q_even[0:DIM, pairs, tok], src[0:DIM], ACT.Copy).then_inc(S["q_even_sb"], 1)

            def v_copy(J, u):
                act.wait_ge(S["v_psum"], 4 * J + u + 1 + 3)
                b, half = u // 2, u % 2
                a(v[:, b, half * 512:(half + 1) * 512], v_bank[:, :], ACT.Copy).then_inc(S["v_sb"], 1)

            def exps(J, k):
                b, g4 = k // 4, k % 4
                act.wait_ge(S["neg_top_done"], K * J + k + 1)
                for i in range(4):
                    h = 4 * g4 + i
                    last = a(probs[:, k % 4, i, :], score_bank[k % 2][:, i * P:(i + 1) * P], ACT.Exp,
                             scale=norm2[:, b, h // 8 * 2, h % 8:h % 8 + 1], bias=neg_top[:, k, i:i + 1],
                             accum_out=sums[:, k, i:i + 1])
                last.then_inc(S["exp_done"], 1)
                if b:
                    act.wait_ge(S["arg_ready"], 4 * J + g4 + 1)
                    a(probs_prev[:, g4, :, :], arg_prev[:, g4, :, :], ACT.Exp).then_inc(S["exp_prev_done"], 1)

            def turned_copy(J, k):
                act.wait_ge(S["turned"], K * J + k + 1)
                a(probs_t[:, k % 2, :], p_turn_bank[:, :], ACT.Copy).then_inc(S["turned_sb"], 1)

            def ffn_square(F):
                act.wait_ge(S["centred_done"], F + 2)
                a(sq_f[:, :], centred[:, :], ACT.Square).then_inc(S["sq_f_done"], 1)

            def ffn_rstd(F):
                act.wait_ge(S["var_psum"], F + 1)
                a(ln_var[:, :], misc_bank[:, 0:TOKENS], ACT.Ln, bias=eps[:, 0:1]).then_inc(S["ln_var_done"], 1)
                act.wait_ge(S["ln_var_done"], F + 1)
                a(rstd_f[:, :], ln_var[:, :], ACT.Exp, scale=-0.5).then_inc(S["rstd_f_done"], 1)

            def ffn_gelu(F, c):
                rows = H_ROWS[c]
                act.wait_ge(S["w1_psum"], 3 * F + c + 1)
                a(gelu[0:rows, c, :], w1_bank[c][0:rows, TOKENS:2 * TOKENS], ACT.Gelu,
                  bias=vec[0:rows, VEC["b_gate"] + c:VEC["b_gate"] + c + 1]).then_inc(S["gelu_done"], 1)

            def body(layer, s, J, has_ffn, has_next):
                for k in range(K + 2):
                    has_unit = k < 4 or (k < K and has_next)
                    if has_unit:
                        U, b, u = units_of(k, J)
                        unit_copy(U, b, u)
                    if k < K:
                        exps(J, k)
                    if k < 4:
                        v_copy(J, k)
                    if has_unit:
                        unit_norm(U, b, u)
                    if k == 0 and has_ffn:
                        ffn_square(J - 1)
                    if k == 2 and has_ffn:
                        ffn_rstd(J - 1)
                    if k >= 1 and (k <= 4 or has_next) and k - 1 < K:
                        U, b, u = units_of(k - 1, J)
                        unit_out(U, b, u)
                    if k == K and has_ffn:
                        for c in range(3):
                            ffn_gelu(J - 1, c)
                    if 1 <= k <= K:
                        turned_copy(J, k - 1)

            def layer_start(layer):
                J = layer * SEQS
                for u in range(5):
                    if u < 4:
                        unit_copy(*first_unit(u, J))
                        unit_norm(*first_unit(u, J))
                    if u:
                        unit_out(*first_unit(u - 1, J))

            def ffn_alone(F):
                ffn_square(F)
                ffn_rstd(F)
                for c in range(3):
                    ffn_gelu(F, c)

            act.sem_inc(S["exp_done"], 2)
            act.sem_inc(S["turned_sb"], 1)
            act.sem_inc(S["k_sb"], 1)
            act.sem_inc(S["q_even_sb"], 1)
            act.wait_ge(S["zeroed"], 7)
            jobs(act, body, ffn_alone, layer_start)

        @block.vector
        def _(dve):
            w = nc.vector
            hd = DIM // 2

            def unit_rotate(U, b, u):
                kind, slot = u % 2, u % 2
                dve.wait_ge(S["raw_ready"], U + 1)
                w.tensor_reduce(norm2[:, b, u, :], sq[:, slot, :].rearrange("p (n d) -> p n d", d=DIM), AX.X, ALU.add
                                ).then_inc(S["norm2_done"], 1)
                src = raw[:, slot, :].rearrange("p (n two d) -> p two n d", two=2, d=hd)
                dst = part2[:, slot, :].rearrange("p (n two d) -> p two n d", two=2, d=hd)
                for o in range(2):
                    sin = table[:, b, 2 * kind + 1, o * hd:(o + 1) * hd].unsqueeze(1).broadcast_to([P, 8, hd])
                    last = w.tensor_tensor(dst[:, o], src[:, 1 - o], sin, ALU.mult)
                last.then_inc(S["part2_done"], 1)
                dve.wait_ge(S["norm2_done"], 2 * U + 1)
                w.tensor_scalar(norm2[:, b, u, :], norm2[:, b, u, :], 1e-24, None, ALU.max).then_inc(S["norm2_done"], 1)
                dve.wait_ge(S["part2_done"], U + 1)
                dve.wait_ge(S["part1_done"], U + 1)
                dve.wait_ge(S["unit_turned"], U + 1)
                w.tensor_tensor(rot[:, slot, :], part1[:, slot, :], part2[:, slot, :], ALU.add).then_inc(S["rot_done"], 1)

            def unit_out(U, b, u):
                if u % 2 == 0:
                    dve.wait_ge(S["unit_turned"], U + 1 + 2)
                    src = q_turn_bank[:, :].rearrange("p (c t) -> p c t", t=P)
                    w.tensor_copy(q_odd[DIM:P, u // 2 * 4:u // 2 * 4 + 4, b * P:(b + 1) * P], src[DIM:P]).then_inc(S["q_odd_sb"], 1)

            def maxima(J, k):
                b, g4 = k // 4, k % 4
                dve.wait_ge(S["scores_psum"], K * J + k + 1)
                last = w.tensor_reduce(top[:, k, :], score_bank[k % 2][:, :].rearrange("p (n j) -> p n j", j=P), AX.X, ALU.max)
                if b:
                    dve.wait_ge(S["prev_psum"], J + 1)
                    before = misc_bank[0:WINDOW, g4 * P:(g4 + 1) * P].rearrange("p (n j) -> p n j", j=WINDOW)
                    last = w.tensor_reduce(top_prev[:, g4, :], before, AX.X, ALU.max)
                last.then_inc(S["top_done"], 1)
                dve.wait_ge(S["top_done"], K * J + k + 1)
                if b:
                    w.tensor_tensor(top[0:WINDOW, k, :], top[0:WINDOW, k, :], top_prev[:, g4, :], ALU.max).then_inc(S["top_joined"], 1)
                    dve.wait_ge(S["top_joined"], 4 * J + g4 + 1)
                inv_q = norm2[:, b, g4 // 2 * 2, g4 % 2 * 4:g4 % 2 * 4 + 4]
                w.scalar_tensor_tensor(neg_top[:, k, :], top[:, k, :], -1.0, inv_q, ALU.mult, ALU.mult).then_inc(S["neg_top_done"], 1)
                if b:
                    w.tensor_tensor(arg_prev[:, g4, :, :], before, inv_q[0:WINDOW].unsqueeze(2).broadcast_to([WINDOW, 4, WINDOW]),
                                    ALU.mult).then_inc(S["arg_scaled"], 1)
                    dve.wait_ge(S["arg_scaled"], 4 * J + g4 + 1 + 1)
                    dve.wait_ge(S["neg_top_done"], K * J + k + 1)
                    w.tensor_tensor(arg_prev[:, g4, :, :], arg_prev[:, g4, :, :],
                                    neg_top[0:WINDOW, k, :].unsqueeze(2).broadcast_to([WINDOW, 4, WINDOW]), ALU.add).then_inc(S["arg_ready"], 1)

            def normalise_probs(J, k):
                b, g4 = k // 4, k % 4
                dve.wait_ge(S["exp_done"], K * J + k + 1 + 2)
                if b:
                    dve.wait_ge(S["exp_prev_done"], 4 * J + g4 + 1)
                    w.tensor_reduce(sum_prev[:, g4, :], probs_prev[:, g4, :, :], AX.X, ALU.add).then_inc(S["sum_prev_done"], 1)
                    dve.wait_ge(S["sum_prev_done"], 4 * J + g4 + 1)
                    w.tensor_tensor(sums[0:WINDOW, k, :], sums[0:WINDOW, k, :], sum_prev[:, g4, :], ALU.add).then_inc(S["sums_joined"], 1)
                    dve.wait_ge(S["sums_joined"], 4 * J + g4 + 1)
                w.reciprocal(inv[:, k, :], sums[:, k, :]).then_inc(S["inv_done"], 1)
                dve.wait_ge(S["inv_done"], K * J + k + 1)
                w.tensor_tensor(probs[:, k % 4, :, :], probs[:, k % 4, :, :], inv[:, k, :].unsqueeze(2).broadcast_to([P, 4, P]),
                                ALU.mult).then_inc(S["probs_ready"], 1)
                if b:
                    w.tensor_tensor(probs_prev[:, g4, :, :], probs_prev[:, g4, :, :],
                                    inv[0:WINDOW, k, :].unsqueeze(2).broadcast_to([WINDOW, 4, WINDOW]), ALU.mult).then_inc(S["prev_normed"], 1)
                    dve.wait_ge(S["prev_normed"], 4 * J + g4 + 1)
                    w.transpose(probs_prev_t[P - WINDOW:P, g4, :], probs_prev[:, g4, :, :].rearrange("p n j -> p (n j)")).then_inc(S["prev_turned"], 1)

            def out_copy(J, f):
                dve.wait_ge(S["out_psum"], K * J + 2 * f + 2)
                b, half = f // 2, f % 2
                w.tensor_copy(o_t[:, 4 * half:4 * half + 4, b * P:(b + 1) * P], out_bank[:, :].rearrange("p (c t) -> p c t", t=P)
                              ).then_inc(S["o_sb"], 1)

            def ffn_centre(F):
                dve.wait_ge(S["mean_psum"], F + 1)
                w.tensor_tensor(centred[:, :], xf[:, :], misc_bank[:, 0:TOKENS], ALU.subtract).then_inc(S["centred_done"], 1)

            def ffn_norm(F):
                dve.wait_ge(S["rstd_f_done"], F + 1)
                w.scalar_tensor_tensor(scaled[:, :], centred[:, :], vec[:, VEC["ln_g"]:VEC["ln_g"] + 1], rstd_f[:, :],
                                       ALU.mult, ALU.mult).then_inc(S["scaled_done"], 1)
                dve.wait_ge(S["scaled_done"], F + 1)
                w.tensor_scalar(xn_f[:, :], scaled[:, :], vec[:, VEC["ln_b"]:VEC["ln_b"] + 1], None, ALU.add).then_inc(S["xn_f_done"], 1)

            def ffn_hidden(F, c):
                rows = H_ROWS[c]
                dve.wait_ge(S["gelu_done"], 3 * F + c + 1)
                w.scalar_tensor_tensor(hid[0:rows, c, :], w1_bank[c][0:rows, 0:TOKENS], vec[0:rows, VEC["b_a"] + c:VEC["b_a"] + c + 1],
                                       gelu[0:rows, c, :], ALU.add, ALU.mult).then_inc(S["hid_done"], 1)

            def ffn_add(s, F):
                dve.wait_ge(S["w2_psum"], F + 1)
                dst = y_tokens(s, 0, TOKENS)
                w.scalar_tensor_tensor(dst, misc_bank[:, 0:TOKENS], vec[:, VEC["b2"]:VEC["b2"] + 1], dst, ALU.add, ALU.add
                                       ).then_inc(S["ffn_added"], 1)

            def body(layer, s, J, has_ffn, has_next):
                for k in range(K + 2):
                    if k < K:
                        maxima(J, k)
                    if 1 <= k <= K:
                        normalise_probs(J, k - 1)
                    if k == 0 and has_ffn:
                        ffn_centre(J - 1)
                    if k < 4 or (k < K and has_next):
                        U, b, u = units_of(k, J)
                        unit_rotate(U, b, u)
                    if k >= 1 and (k <= 4 or has_next) and k - 1 < K:
                        U, b, u = units_of(k - 1, J)
                        unit_out(U, b, u)
                    if k == 3 and has_ffn:
                        ffn_norm(J - 1)
                    if k == K and has_ffn:
                        for c in range(3):
                            ffn_hidden(J - 1, c)
                    if k >= 3 and k % 2 == 1:
                        out_copy(J, (k - 3) // 2)
                if has_ffn:
                    ffn_add(s - 1, J - 1)
                dve.wait_ge(S["wo_psum"], J + 2)
                dst = y_tokens(s, 0, TOKENS)
                w.tensor_tensor(dst, bank[0][:, 0:TOKENS], dst, ALU.add).then_inc(S["y_added"], 1)

            def layer_start(layer):
                J = layer * SEQS
                dve.wait_ge(S["scales_in"], 16 * (layer + 1))
                for b in range(BPS):
                    base = const[:, slice_of("rotary")].rearrange("p (b n) -> p b n", b=BPS)[:, b, :]
                    last = w.tensor_tensor(table[:, b, :, :].rearrange("p a d -> p (a d)"), base, qk_scales[:, :], ALU.mult)
                last.then_inc(S["table_done"], 1)
                dve.wait_ge(S["table_done"], layer + 2)
                for u in range(5):
                    if u < 4:
                        unit_rotate(*first_unit(u, J))
                    if u:
                        unit_out(*first_unit(u - 1, J))
                dve.wait_ge(S["ffn_in"], 16 * 5 * (layer + 1))

            def ffn_alone(F):
                ffn_centre(F)
                ffn_norm(F)
                for c in range(3):
                    ffn_hidden(F, c)
                ffn_add(SEQS - 1, F)

            w.tensor_copy(band_b[:, :], const[:, slice_of("band")]).then_inc(S["const_done"], 1)
            w.tensor_copy(prev_b[:, :], const[:, slice_of("band_prev")]).then_inc(S["const_done"], 1)
            for name, n in (("rot_done", 2), ("unit_turned", 2), ("q_odd_sb", 1), ("o_sb", 1), ("table_done", 1),
                            ("ffn_added", 1), ("centred_done", 1), ("arg_scaled", 1)):
                dve.sem_inc(S[name], n)
            dve.wait_ge(S["zeroed"], 7)
            jobs(dve, body, ffn_alone, layer_start)


def add_transposed(nc, x1, y_t, ident):
    with ExitStack() as stack:
        m = Memory(nc, stack, "last")
        bank = m.banks()
        turned, added = m.sem("turned"), m.sem("added")
        block = stack.enter_context(nc.Block())

        @block.tensor
        def _(pe):
            for k in range(BLOCKS):
                last = nc.tensor.transpose(bank[k // 4][:, k % 4 * P:(k % 4 + 1) * P], y_t[:, k * P:(k + 1) * P], ident)
                if k % 4 == 3:
                    last.then_inc(turned, 1)

        @block.vector
        def _(dve):
            for q in range(8):
                dve.wait_ge(turned, q + 1)
                dst = x1[:, 4 * q:4 * q + 4, :]
                nc.vector.tensor_tensor(dst, bank[q][:, :].rearrange("p (k f) -> p k f", f=D), dst, ALU.add).then_inc(added, 1)


def store_output(nc, x1, out_dram):
    with ExitStack() as stack:
        m = Memory(nc, stack, "store")
        stored = m.sem("stored")
        block = stack.enter_context(nc.Block())
        view = out_dram.rearrange("s (b p) f -> p (s b) f", p=P)

        @block.sync
        def _(sp):
            sp.dma_start(view, x1[:, :, :]).then_inc(stored, 16)
            sp.wait_ge(stored, 16)


def program(nc, t, out):
    with ExitStack() as stack:
        m = Memory(nc, stack, "main")
        x1 = m.sb("x1", [P, BLOCKS, D])
        xn_t = m.sb("xn_t", [P, SEQS * TOKENS])
        const = m.sb("const", [P, N_CONST])
        eps = m.sb("eps", [P, 1])
        ident_b = m.sb("ident_b", [P, P], BF16)
        ident_f = const[:, slice_of("ident")]
        with ExitStack() as first_layer:
            f = Memory(nc, first_layer, "layer0")
            causal_b = f.sb("causal_b", [P, 3 * P], BF16)
            wg, wu = (f.sb(n, [P, EXPERTS, D_FF]) for n in ("wg", "wu"))
            wd = f.sb("wd", [P, EXPERTS, FC, D])
            normalise(nc, "norm0", x1, xn_t, const, eps, t["x"], t["const"], ((ident_b, "ident"), (causal_b, "causal")))
            causal_attention(nc, t["wq"], t["wk"], t["wv"], t["wo"], x1, xn_t, ident_f, ident_b, causal_b,
                             ((wg[:, :, :], t["moe_gate"].rearrange("e p n -> p e n")), (wu[:, :, :], t["moe_up"].rearrange("e p n -> p e n")),
                              (wd[:, :, :, :], t["moe_down"].rearrange("e (c p) n -> p e c n", p=P))))
            mixture_of_experts(nc, t["router"], x1, xn_t, const, wg, wu, wd)
        normalise(nc, "norm1", x1, xn_t, const, eps)
        retention(nc, t["ret_qkv"], t["ret_g"], t["ret_o"], t["ret_gnorm"], x1, xn_t, const, eps)
        transformer(nc, t, xn_t, const, ident_f, ident_b, eps)
        add_transposed(nc, x1, xn_t, ident_f)
        store_output(nc, x1, out)


def kernel(**inputs):
    import concourse.bacc as bacc
    from concourse.bass_utils import run_bass_kernel_spmd

    a = {n: np.asarray(v) for n, v in inputs.items()}

    def proj(w):
        return w.reshape(-1, D).T

    b1 = np.zeros((LAYERS, 2, 3 * P), np.float32)
    b1[:, :, 0:HIDDEN] = a["L1_ffn_b1"].reshape(LAYERS, 2, HIDDEN)
    vectors = np.concatenate([a["L1_ffn_ln_g"][:, None], a["L1_ffn_ln_b"][:, None], a["L1_ffn_b2"][:, None],
                              b1.reshape(LAYERS, 6, P)], 1).transpose(0, 2, 1)
    scales = np.concatenate([f(a[n]) for n in ("L1_ffn_q_scale", "L1_ffn_k_scale")
                             for f in (lambda w: w, lambda w: np.roll(w, DIM // 2, 1))], 1)
    arrays = {
        "tr_qkv": a["L1_ffn_Wqkv"], "tr_o": a["L1_ffn_Wo"], "tr_w1": a["L1_ffn_W1"], "tr_w2": a["L1_ffn_W2"],
        "tr_vec": vectors, "tr_scales": scales,
        "x": a["L0_attn_x_q"],
        "const": const_tables(),
        "router": a["L0_ffn_router_w"].T, "moe_gate": a["L0_ffn_w_gate"], "moe_up": a["L0_ffn_w_up"], "moe_down": a["L0_ffn_w_down"],
        "ret_qkv": np.concatenate([a["L1_attn_Wq"].T, a["L1_attn_Wk"].T, a["L1_attn_Wv"].T], 1),
        "ret_g": a["L1_attn_Wg"].T, "ret_o": a["L1_attn_Wo"].T, "ret_gnorm": a["L1_attn_gnorm_w"],
        "wq": proj(a["L0_attn_w_q"]), "wk": proj(a["L0_attn_w_k"]), "wv": proj(a["L0_attn_w_v"]), "wo": a["L0_attn_w_o"],
    }
    arrays = {"in_" + n: np.ascontiguousarray(v) for n, v in arrays.items()}
    nc = bacc.Bacc("TRN2", target_bir_lowering=False, num_devices=1)
    t = {n[3:]: nc.dram_tensor(n, list(v.shape), F32, kind="ExternalInput").ap() for n, v in arrays.items()}
    out = nc.dram_tensor("result", [SEQS, TOKENS, D], F32, kind="ExternalOutput").ap()
    program(nc, t, out)
    r = run_bass_kernel_spmd(nc, [arrays], core_ids=[0])
    return r.results[0]["result"]
```

```python
from contextlib import ExitStack

import numpy as np

import concourse.bass as bass
from concourse import mybir

F32 = mybir.dt.float32
BF16 = mybir.dt.bfloat16
I32 = mybir.dt.int32
F32R = mybir.dt.float32r
TOP_BITS = -4096
ACT = mybir.ActivationFunctionType
ALU = mybir.AluOpType
AX = mybir.AxisListType

P = 128
SEQS, TOKENS, D = 16, 256, 128
BLOCKS = SEQS * TOKENS // P
BPS = TOKENS // P
LN_EPS = 1e-5
MASKED = -1e30
LN_EXP = "natural_log_exp_and_others"

CONSTS = {}
_at = 0
for _name, _n in (("ident", P), ("causal", 3 * P), ("rank", 256), ("ret_cos", 512), ("ret_sin", 512),
                  ("ret_decay", 4 * 3 * P), ("rotary", 512), ("band", 512), ("band_prev", 512)):
    CONSTS[_name] = (_at, _n)
    _at += _n
N_CONST = _at


def const_tables():
    p = np.arange(P)[:, None]
    j = np.arange(P)[None, :]
    causal = np.where(j > p, MASKED, 0.0)
    parts = {
        "ident": np.eye(P),
        "causal": np.concatenate([causal, np.zeros((P, P)), causal], 1),
    }
    parts["rank"] = np.tile(8.0 - np.arange(8), (P, 32))
    parts.update(retention_tables())
    parts["rotary"] = rotary_base()
    parts.update(band_masks())
    return np.ascontiguousarray(np.concatenate([parts[n] for n in CONSTS], 1).astype(np.float32))


class Memory:

    def __init__(self, nc, stack, phase):
        self.nc, self.stack, self.phase = nc, stack, phase

    def sb(self, name, shape, dt=F32):
        return self.stack.enter_context(self.nc.sbuf_tensor(f"{self.phase}_{name}", shape, dt))

    def banks(self):
        return [self.stack.enter_context(self.nc.psum_tensor(f"{self.phase}_bank{i}", [P, 512], F32)) for i in range(8)]

    def sem(self, name):
        return self.stack.enter_context(self.nc.semaphore(f"{self.phase}_{name}"))


def normalise(nc, phase, x1, xn_t, const, eps, x_dram=None, const_dram=None, bf16_tables=()):
    groups, per = 4, BLOCKS // 4
    with ExitStack() as stack:
        m = Memory(nc, stack, phase)
        xn = m.sb("xn", [P, BLOCKS, D])
        stats = m.sb("stats", [P, BLOCKS, 6])
        mv = m.sb("mean_var", [P, BLOCKS, 2])
        rstd = m.sb("rstd", [P, BLOCKS])
        std = m.sb("std", [P, BLOCKS])
        bank = m.banks()
        x_in, const_in = [m.sem(f"x_in{g}") for g in range(groups)], m.sem("const_in")
        stats_done, mv_done, std_done = m.sem("stats_done"), m.sem("mv_done"), m.sem("std_done")
        rstd_done, xn_done = m.sem("rstd_done"), m.sem("xn_done")
        turned, copied = m.sem("turned"), m.sem("copied")
        eps_done, tables_done = m.sem("eps_done"), m.sem("tables_done")
        block = stack.enter_context(nc.Block())

        @block.sync
        def _(sp):
            if x_dram is not None:
                x_view = x_dram.rearrange("s (b p) f -> p (s b) f", p=P)
                for g in range(groups):
                    ks = slice(g * per, (g + 1) * per)
                    sp.dma_start(x1[:, ks, :], x_view[:, ks, :]).then_inc(x_in[g], 16)
                sp.dma_start(const[:, :], const_dram).then_inc(const_in, 16)

        @block.gpsimd
        def _(pool):
            if x_dram is not None:
                pool.memset(eps[:, :], LN_EPS).then_inc(eps_done, 1)

        @block.vector
        def _(dve):
            for g in range(groups):
                ks = range(g * per, (g + 1) * per)
                if x_dram is not None:
                    dve.wait_ge(x_in[g], 16)
                for k in ks:
                    last = nc.vector.bn_stats(stats[:, k, :], x1[:, k, :])
                last.then_inc(stats_done, 1)
                dve.wait_ge(stats_done, g + 1)
                for k in ks:
                    last = nc.vector.bn_aggr(mv[:, k, :], stats[:, k, :])
                last.then_inc(mv_done, 1)
                dve.wait_ge(std_done, g + 1)
                nc.vector.reciprocal(rstd[:, g * per:(g + 1) * per], std[:, g * per:(g + 1) * per]).then_inc(rstd_done, 1)
                dve.wait_ge(rstd_done, g + 1)
                for k in ks:
                    nc.vector.tensor_scalar(xn[:, k, :], x1[:, k, :], mv[:, k, 0:1], rstd[:, k:k + 1],
                                            ALU.subtract, ALU.mult).then_inc(xn_done, 1)
            if x_dram is not None:
                dve.wait_ge(const_in, 16)
            for table, name in bf16_tables:
                nc.vector.tensor_copy(table[:, :], const[:, slice_of(name)]).then_inc(tables_done, 1)

        @block.tensor
        def _(pe):
            if x_dram is not None:
                pe.wait_ge(const_in, 16)
            ident = const[:, slice_of("ident")]
            for k in range(BLOCKS):
                pe.wait_ge(xn_done, k + 1)
                last = nc.tensor.transpose(bank[k // 4][:, k % 4 * P:(k % 4 + 1) * P], xn[:, k, :], ident)
                if k % 4 == 3:
                    last.then_inc(turned, 1)

        @block.scalar
        def _(act):
            if x_dram is not None:
                act.wait_ge(eps_done, 1)
            for g in range(groups):
                act.wait_ge(mv_done, g + 1)
                nc.scalar.activation(std[:, g * per:(g + 1) * per], mv[:, g * per:(g + 1) * per, 1],
                                     ACT.Sqrt, bias=eps[:, 0:1]).then_inc(std_done, 1)
            for q in range(8):
                act.wait_ge(turned, q + 1)
                nc.scalar.activation(xn_t[:, q * 512:(q + 1) * 512], bank[q][:, :], ACT.Copy).then_inc(copied, 1)


def product_of_halves(nc, out, w_high, w_low, x_high, x_low, first=True, final=True):
    nc.tensor.matmul(out, w_high, x_high, start=first, stop=False)
    nc.tensor.matmul(out, w_high, x_low, start=False, stop=False)
    return nc.tensor.matmul(out, w_low, x_high, start=False, stop=final)


def slice_of(name):
    at, n = CONSTS[name]
    return slice(at, at + n)


A_HEADS, A_DIM = 16, 64
A_CHUNKS = A_HEADS // 2
A_WIDE = A_HEADS * A_DIM


def causal_attention(nc, wq_dram, wk_dram, wv_dram, wo_dram, x1, xn_t, ident_f, ident_b, causal_b,
                     for_later):
    with ExitStack() as stack:
        m = Memory(nc, stack, "att")
        wq, wk, wv = (m.sb(n, [P, A_WIDE]) for n in ("wq", "wk", "wv"))
        wo = m.sb("wo", [P, A_CHUNKS, D])
        xs = m.sb("xs", [P, TOKENS])
        q_even = m.sb("q_even", [P, A_CHUNKS, TOKENS])
        q_odd = m.sb("q_odd", [P, A_CHUNKS, TOKENS])
        k_t = m.sb("k_t", [P, A_CHUNKS, TOKENS])
        v = m.sb("v", [P, BPS, A_WIDE])
        probs = m.sb("probs", [P, 4, 3 * P])
        probs_t = m.sb("probs_t", [P, 2, 3 * P])
        neg_max = m.sb("neg_max", [P, A_HEADS, 2])
        sums = m.sb("sums", [P, A_HEADS, 2])
        inv = m.sb("inv", [P, A_HEADS, 2])
        o_t = m.sb("o_t", [P, A_CHUNKS, TOKENS])
        bank = m.banks()
        proj_bank, score_bank, turn_bank, out_bank = bank[0:2], bank[2:4], bank[4:6], bank[6:8]
        w_in, zeros_done = m.sem("w_in"), m.sem("zeros_done")
        xs_ready = m.sem("xs_ready")
        qk_psum, v_psum, wo_psum = m.sem("qk_psum"), m.sem("v_psum"), m.sem("wo_psum")
        qk_act, qk_dve, v_act, v_dve = m.sem("qk_act"), m.sem("qk_dve"), m.sem("v_act"), m.sem("v_dve")
        scores_ready, max_ready, exp_done = m.sem("scores_ready"), m.sem("max_ready"), m.sem("exp_done")
        inv_done, probs_ready = m.sem("inv_done"), m.sem("probs_ready")
        turned, turned_sb, out_psum, out_sb = m.sem("turned"), m.sem("turned_sb"), m.sem("out_psum"), m.sem("out_sb")
        added, later_in = m.sem("added"), m.sem("later_in")
        block = stack.enter_context(nc.Block())
        H, C = A_HEADS, A_CHUNKS

        @block.sync
        def _(sp):
            for w, dram in ((wq, wq_dram), (wk, wk_dram), (wv, wv_dram)):
                sp.dma_start(w[:, :], dram).then_inc(w_in, 16)
            sp.dma_start(wo[:, :, :], wo_dram.rearrange("(c p) f -> p c f", p=P)).then_inc(w_in, 16)
            for i, (tile, dram) in enumerate(for_later):
                sp.dma_start(tile, dram).then_inc(later_in, 16)
            sp.wait_ge(later_in, 16 * len(for_later))

        @block.gpsimd
        def _(pool):
            nc.gpsimd.memset(q_even[A_DIM:P, :, :], 0.0).then_inc(zeros_done, 1)
            pool.wait_ge(zeros_done, 1)
            nc.gpsimd.memset(q_odd[0:A_DIM, :, :], 0.0).then_inc(zeros_done, 1)
            pool.wait_ge(zeros_done, 2)
            nc.gpsimd.tensor_copy(xs[:, :], xn_t[:, 0:TOKENS]).then_inc(xs_ready, 1)
            with pool.Fori(1, SEQS) as s:
                pool.wait_ge(v_psum, s * 4)
                nc.gpsimd.tensor_copy(xs[:, :], xn_t[:, bass.ds(s * TOKENS, TOKENS)]).then_inc(xs_ready, 1)

        @block.tensor
        def _(pe):
            def project_qk(n, c, first=False):
                if c >= 2:
                    pe.wait_ge(qk_act if c % 2 == 0 else qk_dve, n * (C // 2) + c // 2)
                elif not first:
                    pe.wait_ge(v_act if c % 2 == 0 else v_dve, n * 2)
                    pe.wait_ge(added, n * BPS)
                for i, w in enumerate((wq, wk)):
                    last = nc.tensor.matmul(proj_bank[c % 2][:, i * TOKENS:(i + 1) * TOKENS],
                                            w[:, c * P:(c + 1) * P], xs[:, :], start=True, stop=True)
                last.then_inc(qk_psum, 1)

            def project_v(n, u):
                if u < 2:
                    pe.wait_ge(qk_act if u == 0 else qk_dve, (n + 1) * (C // 2))
                else:
                    pe.wait_ge(v_act if u % 2 == 0 else v_dve, n * 2 + u // 2)
                last = nc.tensor.matmul(proj_bank[u % 2][:, :], xs[:, u // 2 * P:(u // 2 + 1) * P],
                                        wv[:, u % 2 * 512:(u % 2 + 1) * 512], start=True, stop=True)
                last.then_inc(v_psum, 1)

            def job(s, ahead):
                for t in range(H + 3):
                    if t < H:
                        c = t // 2
                        if t % 2 == 0:
                            pe.wait_ge(qk_act if c % 2 == 0 else qk_dve, s * (C // 2) + c // 2 + 1)
                        pe.wait_ge(exp_done, s * H + t)
                        sc, q = score_bank[t % 2], (q_even, q_odd)[t % 2]
                        nc.tensor.matmul(sc[:, 0:3 * P], ident_b[:, :], causal_b[:, :], start=True, stop=False)
                        nc.tensor.matmul(sc[:, 0:P], q[:, c, 0:P], k_t[:, c, 0:P], start=False, stop=False)
                        nc.tensor.matmul(sc[:, P:3 * P], q[:, c, P:TOKENS], k_t[:, c, :],
                                         start=False, stop=True).then_inc(scores_ready, 1)
                    elif ahead:
                        for c in range(3 * (t - H), min(3 * (t - H) + 3, C)):
                            if t == H and c == 0:
                                pe.wait_ge(xs_ready, s + 2)
                            project_qk(s + 1, c)
                    h = t - 2
                    if 0 <= h < H:
                        pe.wait_ge(probs_ready, s * H + h + 1)
                        pe.wait_ge(turned_sb, s * H + h)
                        for i, at in enumerate((0, P, 2 * P)):
                            last = nc.tensor.transpose(turn_bank[h % 2][:, i * P:(i + 1) * P],
                                                       probs[:, h % 4, at:at + P], ident_f)
                        last.then_inc(turned, 1)
                    h = t - 3
                    if h >= 0:
                        if h == 0:
                            pe.wait_ge(v_act, 2 * (s + 1))
                            pe.wait_ge(v_dve, 2 * (s + 1))
                        if h % 2 == 0:
                            pe.wait_ge(out_sb, s * C + h // 2 + 1)
                        pe.wait_ge(turned_sb, s * H + h + 2)
                        rows = slice(h % 2 * A_DIM, (h % 2 + 1) * A_DIM)
                        dst = out_bank[h // 2 % 2][rows, 0:TOKENS]
                        nc.tensor.matmul(dst, v[:, 0, h * A_DIM:(h + 1) * A_DIM], probs_t[:, h % 2, 0:TOKENS],
                                         start=True, stop=False)
                        nc.tensor.matmul(out_bank[h // 2 % 2][rows, P:TOKENS], v[:, 1, h * A_DIM:(h + 1) * A_DIM],
                                         probs_t[:, h % 2, TOKENS:3 * P], start=False, stop=True).then_inc(out_psum, 1)
                if ahead:
                    for u in range(4):
                        project_v(s + 1, u)
                pe.wait_ge(out_sb, (s + 1) * C + 2)
                for b in range(BPS):
                    if ahead:
                        pe.wait_ge((v_act, v_dve)[b], 2 * (s + 2))
                    for c in range(C):
                        last = nc.tensor.matmul(proj_bank[b][:, 0:D], o_t[:, c, b * P:(b + 1) * P], wo[:, c, :],
                                                start=c == 0, stop=c == C - 1)
                    last.then_inc(wo_psum, 1)

            pe.wait_ge(w_in, 64)
            pe.wait_ge(xs_ready, 1)
            for c in range(C):
                project_qk(0, c, first=True)
            for u in range(4):
                project_v(0, u)
            pe.wait_ge(zeros_done, 2)
            with pe.Fori(0, SEQS - 1) as s:
                job(s, True)
            job(SEQS - 1, False)

        def copy_qk(copy, c, done):
            src = proj_bank[c % 2]
            copy(q_even[0:A_DIM, c, :], src[0:A_DIM, 0:TOKENS], A_DIM ** -0.5)
            copy(q_odd[A_DIM:P, c, :], src[A_DIM:P, 0:TOKENS], A_DIM ** -0.5)
            copy(k_t[:, c, :], src[:, TOKENS:2 * TOKENS], 1.0).then_inc(done, 1)

        @block.scalar
        def _(act):
            def copy(out, src, scale):
                return nc.scalar.activation(out, src, ACT.Copy, scale=scale)

            def job(s, ahead):
                for t in range(H + 3):
                    if t < H:
                        act.wait_ge(max_ready, s * H + t + 1)
                        if t >= 4:
                            act.wait_ge(turned, s * H + t - 3)
                        for i, (a, e) in enumerate(((0, P), (P, 3 * P))):
                            last = nc.scalar.activation(probs[:, t % 4, a:e], score_bank[t % 2][:, a:e], ACT.Exp,
                                                        bias=neg_max[:, t, i:i + 1], accum_out=sums[:, t, i:i + 1])
                        last.then_inc(exp_done, 1)
                    elif ahead:
                        for c in range(3 * (t - H), min(3 * (t - H) + 3, C)):
                            if c % 2 == 0:
                                act.wait_ge(qk_psum, (s + 1) * C + c + 1)
                                copy_qk(copy, c, qk_act)
                    h = t - 2
                    if 0 <= h < H:
                        act.wait_ge(turned, s * H + h + 1)
                        if h >= 2:
                            act.wait_ge(out_psum, s * H + h - 1)
                        nc.scalar.activation(probs_t[:, h % 2, :], turn_bank[h % 2][:, 0:3 * P], ACT.Copy).then_inc(turned_sb, 1)
                if ahead:
                    copy_v(s + 1)

            def copy_v(n):
                for u in (0, 2):
                    act.wait_ge(v_psum, n * 4 + u + 1)
                    nc.scalar.activation(v[:, u // 2, 0:512], proj_bank[0][:, :], ACT.Copy).then_inc(v_act, 1)

            act.sem_inc(exp_done, 1)
            act.sem_inc(turned_sb, 1)
            for c in range(0, C, 2):
                act.wait_ge(qk_psum, c + 1)
                copy_qk(copy, c, qk_act)
            copy_v(0)
            with act.Fori(0, SEQS - 1) as s:
                job(s, True)
            job(SEQS - 1, False)

        @block.vector
        def _(dve):
            def copy(out, src, scale):
                return nc.vector.tensor_scalar(out, src, scale, None, ALU.mult)

            def job(s, ahead):
                for t in range(H + 4):
                    if t < H:
                        dve.wait_ge(scores_ready, s * H + t + 1)
                        for i, (a, e) in enumerate(((0, P), (P, 3 * P))):
                            last = nc.vector.tensor_reduce(neg_max[:, t, i:i + 1], score_bank[t % 2][:, a:e], AX.X, ALU.max,
                                                           negate=True)
                        last.then_inc(max_ready, 1)
                    h = t - 1
                    if 0 <= h < H:
                        dve.wait_ge(exp_done, s * H + h + 2)
                        nc.vector.reciprocal(inv[:, h, :], sums[:, h, :]).then_inc(inv_done, 1)
                        dve.wait_ge(inv_done, s * H + h + 1)
                        for i, (a, e) in enumerate(((0, P), (P, 3 * P))):
                            last = nc.vector.tensor_scalar(probs[:, h % 4, a:e], probs[:, h % 4, a:e], inv[:, h, i:i + 1],
                                                           None, ALU.mult)
                        last.then_inc(probs_ready, 1)
                    if ahead and t >= H:
                        for c in range(3 * (t - H), min(3 * (t - H) + 3, C)):
                            if c % 2 == 1:
                                dve.wait_ge(qk_psum, (s + 1) * C + c + 1)
                                copy_qk(copy, c, qk_dve)
                    h = t - 4
                    if h >= 0 and h % 2 == 1:
                        dve.wait_ge(out_psum, s * H + h + 1)
                        nc.vector.tensor_copy(o_t[:, h // 2, :], out_bank[h // 2 % 2][:, 0:TOKENS]).then_inc(out_sb, 1)
                if ahead:
                    copy_v(s + 1)
                for b in range(BPS):
                    dve.wait_ge(wo_psum, BPS * s + b + 1)
                    dst = x1[:, bass.ds(s * BPS + b, 1), :]
                    nc.vector.tensor_tensor(dst, proj_bank[b][:, 0:D].rearrange("p (o f) -> p o f", o=1), dst, ALU.add).then_inc(added, 1)

            def copy_v(n):
                for u in (1, 3):
                    dve.wait_ge(v_psum, n * 4 + u + 1)
                    nc.vector.tensor_copy(v[:, u // 2, 512:1024], proj_bank[1][:, :]).then_inc(v_dve, 1)

            dve.sem_inc(out_sb, 2)
            dve.sem_inc(added, BPS)
            for c in range(1, C, 2):
                dve.wait_ge(qk_psum, c + 1)
                copy_qk(copy, c, qk_dve)
            copy_v(0)
            with dve.Fori(0, SEQS - 1) as s:
                job(s, True)
            job(SEQS - 1, False)


EXPERTS, D_FF = 8, 512
FC = D_FF // P


def mixture_of_experts(nc, router_dram, w_drams, x1, xn_t, const, staged, wd):
    NB, E = BLOCKS, EXPERTS
    TC = 4
    CHUNKS = NB // TC
    with ExitStack() as stack:
        m = Memory(nc, stack, "moe")
        rw = m.sb("router_w", [P, E])
        small = {n: m.sb(n, [P, NB, E]) for n in ("logit", "below", "ranked", "first", "rest", "ranked2", "second", "chosen",
                                                 "expo", "picked", "weight")}
        top = {n: m.sb(n, [P, NB]) for n in ("max1", "rank1", "max2", "rank2", "total", "inv")}
        w_top = m.sb("w_top", [P, 2, 2, D_FF], I32)
        w_high, w_low = m.sb("w_high", [P, 2, E, D_FF], F32R), m.sb("w_low", [P, 2, E, D_FF], F32R)
        xs_top = m.sb("xs_top", [P, TC * P], I32)
        xs_high, xs_low = m.sb("xs_high", [P, TC * P], F32R), m.sb("xs_low", [P, TC * P], F32R)
        gate = m.sb("gate", [P, 2, TC * P])
        hid = m.sb("hidden", [P, 2, FC, TC * P])
        bank = m.banks()
        gate_bank, up_bank, down_bank, route_bank = bank[0:2], bank[2:4], bank[4:6], bank[6]
        rw_in, logits_psum, route, expo_done = m.sem("rw_in"), m.sem("logits_psum"), m.sem("route"), m.sem("expo_done")
        xs_ready, gate_psum, up_psum, gate_done = m.sem("xs_ready"), m.sem("gate_psum"), m.sem("up_psum"), m.sem("gate_done")
        hid_done, down_psum, added = m.sem("hid_done"), m.sem("down_psum"), m.sem("added")
        w_top_done, w_low_done, w_high_done = m.sem("w_top_done"), m.sem("w_low_done"), m.sem("w_high_done")
        xs_top_done = m.sem("xs_top_done")
        staged_in = [[m.sem(f"staged_in{place}{side}") for side in range(2)] for place in range(2)]
        block = stack.enter_context(nc.Block())

        @block.sync
        def _(sp):
            sp.dma_start(rw[:, :], router_dram).then_inc(rw_in, 16)
            for e in range(2, E):
                for side in range(2):
                    sp.wait_ge(w_low_done, 2 * (e - 2) + side + 1)
                    sp.dma_start(staged[:, e % 2, side, :], w_drams[side][e]).then_inc(staged_in[e % 2][side], 16)

        @block.gpsimd
        def _(pool):
            def halves_of_xs(pool, n):
                pool.wait_ge(xs_top_done, n + 1)
                nc.gpsimd.tensor_tensor(xs_low[:, :], xn_t[:, bass.ds(n * (TC * P), TC * P)], xs_top[:, :].bitcast(F32), ALU.subtract
                                        ).then_inc(xs_ready, 1)
                nc.gpsimd.tensor_copy(xs_high[:, :], xs_top[:, :].bitcast(F32)).then_inc(xs_ready, 1)

            for e in range(E):
                for side in range(2):
                    pool.wait_ge(w_top_done, 2 * e + side + 1)
                    nc.gpsimd.tensor_tensor(w_low[:, side, e, :], staged[:, e % 2, side, :], w_top[:, e % 2, side, :].bitcast(F32), ALU.subtract
                                            ).then_inc(w_low_done, 1)
                if e == 0:
                    halves_of_xs(pool, 0)
            with pool.Fori(1, CHUNKS) as n:
                pool.wait_ge(up_psum, n * E * FC)
                halves_of_xs(pool, n)

        @block.tensor
        def _(pe):
            def down(n, e):
                pe.wait_ge(hid_done, (n * E + e + 1) * FC)
                pe.wait_ge(added, (n * E + e - 1) * TC + 2 * TC)
                for b in range(TC):
                    for c in range(FC):
                        last = nc.tensor.matmul(down_bank[e % 2][:, b * P:(b + 1) * P], hid[:, e % 2, c, b * P:(b + 1) * P],
                                                wd[:, e, c, :], start=c == 0, stop=c == FC - 1)
                last.then_inc(down_psum, 1)

            pe.wait_ge(rw_in, 16)
            for k in range(NB):
                last = nc.tensor.matmul(route_bank[:, k * E:(k + 1) * E], xn_t[:, k * P:(k + 1) * P], rw[:, :],
                                        start=True, stop=True)
            last.then_inc(logits_psum, 1)
            with pe.Fori(0, CHUNKS) as n:
                pe.wait_ge(xs_ready, 2 * n + 2)
                for e in range(E):
                    pe.wait_ge(w_high_done, 2 * e + 2)
                    for c in range(FC):
                        i = e * FC + c
                        ff = slice(c * P, (c + 1) * P)
                        pe.wait_ge(gate_done, n * (E * FC) + i + 1)
                        product_of_halves(nc, gate_bank[i % 2][:, :], w_high[:, 0, e, ff], w_low[:, 0, e, ff],
                                          xs_high[:, :], xs_low[:, :]).then_inc(gate_psum, 1)
                        if i >= 2:
                            pe.wait_ge(hid_done, n * (E * FC) + i - 1)
                        product_of_halves(nc, up_bank[i % 2][:, :], w_high[:, 1, e, ff], w_low[:, 1, e, ff],
                                          xs_high[:, :], xs_low[:, :]).then_inc(up_psum, 1)
                        if c == 1 and e > 0:
                            down(n, e - 1)
                down(n, E - 1)

        @block.scalar
        def _(act):
            for e in range(E):
                for side in range(2):
                    act.wait_ge(w_low_done, 2 * e + side + 1)
                    nc.scalar.activation(w_high[:, side, e, :], w_top[:, e % 2, side, :].bitcast(F32), ACT.Copy).then_inc(w_high_done, 1)
            act.wait_ge(route, 2)
            nc.scalar.activation(small["expo"][:, :, :], small["below"][:, :, :], ACT.Exp).then_inc(expo_done, 1)
            act.sem_inc(gate_done, 2)
            with act.Fori(0, CHUNKS) as n:
                for i in range(E * FC):
                    act.wait_ge(gate_psum, n * (E * FC) + i + 1)
                    if i >= 2:
                        act.wait_ge(hid_done, n * (E * FC) + i - 1)
                    nc.scalar.activation(gate[:, i % 2, :], gate_bank[i % 2][:, :], ACT.Silu).then_inc(gate_done, 1)

        @block.vector
        def _(dve):
            s, v = small, nc.vector

            def over_experts(t):
                return t[:, :].unsqueeze(2).broadcast_to([P, NB, E])

            v.tensor_scalar(xs_top[:, :], xn_t[:, 0:TC * P].bitcast(I32), TOP_BITS, None, ALU.bitwise_and).then_inc(xs_top_done, 1)
            for e in range(E):
                for side in range(2):
                    if e >= 2:
                        dve.wait_ge(staged_in[e % 2][side], 16 * (e // 2))
                        dve.wait_ge(w_high_done, 2 * (e - 2) + side + 1)
                    v.tensor_scalar(w_top[:, e % 2, side, :], staged[:, e % 2, side, :].bitcast(I32), TOP_BITS, None, ALU.bitwise_and
                                    ).then_inc(w_top_done, 1)
            rank = const[:, slice_of("rank")].rearrange("p (k e) -> p k e", e=E)
            logits = route_bank[:, 0:NB * E].rearrange("p (k e) -> p k e", e=E)
            dve.wait_ge(logits_psum, 1)
            v.tensor_reduce(top["max1"][:, :], logits, AX.X, ALU.max).then_inc(route, 1)
            dve.wait_ge(route, 1)
            v.tensor_tensor(s["below"][:, :, :], logits, over_experts(top["max1"]), ALU.subtract).then_inc(route, 1)
            dve.wait_ge(route, 2)
            v.scalar_tensor_tensor(s["ranked"][:, :, :], s["below"][:, :, :], 0.0, rank, ALU.is_ge, ALU.mult).then_inc(route, 1)
            dve.wait_ge(route, 3)
            v.tensor_reduce(top["rank1"][:, :], s["ranked"][:, :, :], AX.X, ALU.max).then_inc(route, 1)
            dve.wait_ge(route, 4)
            v.tensor_tensor(s["first"][:, :, :], s["ranked"][:, :, :], over_experts(top["rank1"]), ALU.is_equal).then_inc(route, 1)
            dve.wait_ge(route, 5)
            v.scalar_tensor_tensor(s["rest"][:, :, :], s["first"][:, :, :], MASKED, s["below"][:, :, :], ALU.mult, ALU.add).then_inc(route, 1)
            dve.wait_ge(route, 6)
            v.tensor_reduce(top["max2"][:, :], s["rest"][:, :, :], AX.X, ALU.max).then_inc(route, 1)
            dve.wait_ge(route, 7)
            v.tensor_tensor(s["chosen"][:, :, :], s["rest"][:, :, :], over_experts(top["max2"]), ALU.is_equal).then_inc(route, 1)
            dve.wait_ge(route, 8)
            v.tensor_tensor(s["ranked2"][:, :, :], s["chosen"][:, :, :], rank, ALU.mult).then_inc(route, 1)
            dve.wait_ge(route, 9)
            v.tensor_reduce(top["rank2"][:, :], s["ranked2"][:, :, :], AX.X, ALU.max).then_inc(route, 1)
            dve.wait_ge(route, 10)
            v.tensor_tensor(s["second"][:, :, :], s["ranked2"][:, :, :], over_experts(top["rank2"]), ALU.is_equal).then_inc(route, 1)
            dve.wait_ge(route, 11)
            v.tensor_tensor(s["picked"][:, :, :], s["first"][:, :, :], s["second"][:, :, :], ALU.add).then_inc(route, 1)
            dve.wait_ge(route, 12)
            dve.wait_ge(expo_done, 1)
            v.tensor_tensor(s["picked"][:, :, :], s["picked"][:, :, :], s["expo"][:, :, :], ALU.mult).then_inc(route, 1)
            dve.wait_ge(route, 13)
            v.tensor_reduce(top["total"][:, :], s["picked"][:, :, :], AX.X, ALU.add).then_inc(route, 1)
            dve.wait_ge(route, 14)
            v.reciprocal(top["inv"][:, :], top["total"][:, :]).then_inc(route, 1)
            dve.wait_ge(route, 15)
            v.tensor_tensor(s["weight"][:, :, :], s["picked"][:, :, :], over_experts(top["inv"]), ALU.mult).then_inc(route, 1)
            dve.wait_ge(route, 16)

            def add_expert(n, e):
                dve.wait_ge(down_psum, n * E + e + 1)
                dve.wait_ge(added, (n * E + e) * TC + TC)
                for b in range(TC):
                    dst = x1[:, bass.ds(n * TC + b, 1), :].rearrange("p o f -> p (o f)")
                    w = s["weight"][:, bass.ds(n * TC + b, 1), e]
                    v.scalar_tensor_tensor(dst, down_bank[e % 2][:, b * P:(b + 1) * P], w, dst, ALU.mult, ALU.add).then_inc(added, 1)

            dve.sem_inc(added, TC)

            def chunk(n, has_next):
                for e in range(E):
                    if e == E - 1 and has_next:
                        dve.wait_ge(xs_ready, 2 * n + 2)
                        v.tensor_scalar(xs_top[:, :], xn_t[:, bass.ds((n + 1) * (TC * P), TC * P)].bitcast(I32), TOP_BITS, None,
                                        ALU.bitwise_and).then_inc(xs_top_done, 1)
                    for c in range(FC):
                        i = e * FC + c
                        dve.wait_ge(gate_done, n * (E * FC) + i + 3)
                        dve.wait_ge(up_psum, n * (E * FC) + i + 1)
                        if e >= 2 and c == 0:
                            dve.wait_ge(down_psum, n * E + e - 1)
                        v.tensor_tensor(hid[:, e % 2, c, :], gate[:, i % 2, :], up_bank[i % 2][:, :], ALU.mult).then_inc(hid_done, 1)
                        if c == 2 and e > 0:
                            add_expert(n, e - 1)
                add_expert(n, E - 1)

            with dve.Fori(0, CHUNKS - 1) as n:
                chunk(n, True)
            chunk(CHUNKS - 1, False)


R_HEADS, R_DK, R_DV = 4, 32, 64


def retention_tables():
    half = R_DK // 2
    inv_freq = (1.0 / np.float32(10000.0) ** (np.arange(0, R_DK, 2, dtype=np.float32) / R_DK)).astype(np.float32)
    freqs = np.arange(TOKENS, dtype=np.float32)[:, None] * inv_freq[None, :]
    cos, sin = np.cos(freqs), np.sin(freqs)
    c = np.concatenate([cos, cos], 1)
    s = np.concatenate([-sin, sin], 1)
    scale = np.repeat([R_DK ** -0.5, 1.0], R_HEADS)
    wide = {}
    for name, t in (("ret_cos", c), ("ret_sin", s)):
        w = scale[None, :, None] * t[:, None, :]
        wide[name] = w.reshape(BPS, P, -1).transpose(1, 0, 2).reshape(P, -1)
    gamma = 1.0 - 2.0 ** (-5.0 - np.arange(R_HEADS))
    j, i = np.arange(P)[:, None], np.arange(TOKENS)[None, :]
    d0 = np.where(i >= j, gamma[:, None, None] ** np.maximum(i - j, 0), 0.0)
    d1 = d0[:, :, 0:P]
    decay = np.concatenate([d0, d1], 2)
    wide["ret_decay"] = decay.transpose(1, 0, 2).reshape(P, -1)
    return wide


def retention(nc, wqkv_dram, wg_dram, wo_dram, gnorm_dram, x1, xn_t, const, eps):
    V_WIDE = R_HEADS * R_DV
    with ExitStack() as stack:
        m = Memory(nc, stack, "ret")
        wqkv = m.sb("wqkv", [P, 512])
        wg = m.sb("wg", [P, V_WIDE])
        wo = m.sb("wo", [P, 2, D])
        gnorm = m.sb("gnorm", [P, R_DV])
        gate = m.sb("gate", [P, BLOCKS, V_WIDE])
        xs = m.sb("xs", [P, TOKENS])
        raw = m.sb("raw", [P, BPS, 256])
        part1 = m.sb("part1", [P, BPS, 256])
        part2 = m.sb("part2", [P, BPS, 256])
        rot = m.sb("rot", [P, BPS, 256])
        v = m.sb("v", [P, BPS, V_WIDE])
        q_t = m.sb("q_t", [P, R_HEADS, TOKENS])
        k_t = m.sb("k_t", [P, TOKENS])
        probs_t = m.sb("probs_t", [P, R_HEADS, 3 * P])
        o_raw = m.sb("o_raw", [P, BPS * R_HEADS, R_DV])
        sq = m.sb("sq", [P, BPS * R_HEADS, R_DV])
        ms = m.sb("ms", [P, BPS * R_HEADS])
        ln_ms = m.sb("ln_ms", [P, BPS * R_HEADS])
        rstd = m.sb("rstd", [P, BPS * R_HEADS])
        o_n = m.sb("o_n", [P, BPS * R_HEADS, R_DV])
        gated = m.sb("gated", [P, BPS * R_HEADS, R_DV])
        o_t = m.sb("o_t", [P, BPS, 2, P])
        bank = m.banks()
        w_in, zeroed = m.sem("w_in"), m.sem("zeroed")
        gate_psum, gate_done, xs_ready = m.sem("gate_psum"), m.sem("gate_done"), m.sem("xs_ready")
        qkv_psum, raw_ready, rot_steps, rot_ready = m.sem("qkv_psum"), m.sem("raw_ready"), m.sem("rot_steps"), m.sem("rot_ready")
        part1_done = m.sem("part1_done")
        qk_turned, qk_sb, scores_ready, decayed = m.sem("qk_turned"), m.sem("qk_sb"), m.sem("scores_ready"), m.sem("decayed")
        out_psum, o_copied, squared, ms_done, ln_done, rstd_done = (m.sem(n) for n in (
            "out_psum", "o_copied", "squared", "ms_done", "ln_done", "rstd_done"))
        norm_steps, gated_done, o_turned, o_sb, wo_psum, added = (m.sem(n) for n in (
            "norm_steps", "gated_done", "o_turned", "o_sb", "wo_psum", "added"))
        block = stack.enter_context(nc.Block())
        NBH = BPS * R_HEADS

        @block.sync
        def _(sp):
            sp.dma_start(wqkv[:, :], wqkv_dram).then_inc(w_in, 16)
            sp.dma_start(wg[:, :], wg_dram).then_inc(w_in, 16)
            sp.dma_start(wo[:, :, :], wo_dram.rearrange("(c p) f -> p c f", p=P)).then_inc(w_in, 16)
            sp.dma_start(gnorm[:, :], gnorm_dram.partition_broadcast(P)).then_inc(w_in, 16)

        @block.gpsimd
        def _(pool):
            nc.gpsimd.memset(q_t[:, :, :], 0.0).then_inc(zeroed, 1)
            cos = const[:, slice_of("ret_cos")].rearrange("p (b n) -> p b n", b=BPS)

            def job(s):
                pool.wait_ge(qkv_psum, s * BPS + 1)
                nc.gpsimd.tensor_copy(xs[:, :], xn_t[:, bass.ds(s * TOKENS, TOKENS)]).then_inc(xs_ready, 1)
                pool.wait_ge(raw_ready, BPS * (s + 1))
                nc.gpsimd.tensor_tensor(part1[:, :, :], raw[:, :, :], cos, ALU.mult).then_inc(part1_done, 1)

            with pool.Fori(0, SEQS) as s:
                job(s)

        @block.tensor
        def _(pe):
            ident = const[:, slice_of("ident")]
            pe.wait_ge(w_in, 64)
            for k in range(BLOCKS):
                if k >= 4 and k % 2 == 0:
                    pe.wait_ge(gate_done, k // 2 - 1)
                last = nc.tensor.matmul(bank[k // 2 % 2][:, k % 2 * V_WIDE:(k % 2 + 1) * V_WIDE],
                                        xn_t[:, k * P:(k + 1) * P], wg[:, :], start=True, stop=True)
                if k % 2 == 1:
                    last.then_inc(gate_psum, 1)
            pe.wait_ge(gate_done, BLOCKS // 2)
            pe.sem_inc(qkv_psum, 1)
            with pe.Fori(0, SEQS) as s:
                pe.wait_ge(xs_ready, s + 1)
                for b in range(BPS):
                    last = nc.tensor.matmul(bank[b][:, :], xs[:, b * P:(b + 1) * P], wqkv[:, :], start=True, stop=True)
                    last.then_inc(qkv_psum, 1)
                pe.wait_ge(rot_ready, s + 1)
                for half in range(2):
                    for b in range(BPS):
                        at = (half * BPS + b) * P
                        last = nc.tensor.transpose(bank[2][:, at:at + P], rot[:, b, half * P:(half + 1) * P], ident)
                last.then_inc(qk_turned, 1)
                pe.wait_ge(qk_sb, s + 1)
                for h in range(R_HEADS):
                    sc = bank[3 + h]
                    nc.tensor.matmul(sc[:, 0:TOKENS], k_t[:, 0:P], q_t[:, h, :], start=True, stop=True)
                    nc.tensor.matmul(sc[:, TOKENS:3 * P], k_t[:, P:TOKENS], q_t[:, h, P:TOKENS],
                                     start=True, stop=True).then_inc(scores_ready, 1)
                for h in range(R_HEADS):
                    pe.wait_ge(decayed, s * R_HEADS + h + 1)
                    vs = slice(h * R_DV, (h + 1) * R_DV)
                    o0 = bank[7][:, vs]
                    o1 = bank[7][:, V_WIDE + h * R_DV:V_WIDE + (h + 1) * R_DV]
                    nc.tensor.matmul(o0, probs_t[:, h, 0:P], v[:, 0, vs], start=True, stop=True)
                    nc.tensor.matmul(o1, probs_t[:, h, P:TOKENS], v[:, 0, vs], start=True, stop=False)
                    last = nc.tensor.matmul(o1, probs_t[:, h, TOKENS:3 * P], v[:, 1, vs], start=False, stop=True)
                last.then_inc(out_psum, 1)
                pe.wait_ge(gated_done, s + 1)
                for b in range(BPS):
                    for c in range(2):
                        at = (b * 2 + c) * P
                        last = nc.tensor.transpose(bank[2][:, at:at + P],
                                                   gated[:, b * R_HEADS + 2 * c:b * R_HEADS + 2 * c + 2, :].rearrange("p h d -> p (h d)"), ident)
                last.then_inc(o_turned, 1)
                pe.wait_ge(o_sb, s + 1)
                for b in range(BPS):
                    for c in range(2):
                        last = nc.tensor.matmul(bank[b][:, 0:D], o_t[:, b, c, :], wo[:, c, :], start=c == 0, stop=c == 1)
                    last.then_inc(wo_psum, 1)
                pe.wait_ge(added, (s + 1) * BPS)

        @block.scalar
        def _(act):
            for k in range(BLOCKS // 2):
                act.wait_ge(gate_psum, k + 1)
                nc.scalar.activation(gate[:, 2 * k:2 * k + 2, :], bank[k % 2][:, :].rearrange("p (b n) -> p b n", b=2),
                                     ACT.Silu).then_inc(gate_done, 1)
            nc.scalar.preload_act_table_set(LN_EXP)
            with act.Fori(0, SEQS) as s:
                for b in range(BPS):
                    act.wait_ge(qkv_psum, s * BPS + b + 2)
                    nc.scalar.activation(raw[:, b, :], bank[b][:, 0:256], ACT.Copy)
                    nc.scalar.activation(v[:, b, :], bank[b][:, 256:512], ACT.Copy).then_inc(raw_ready, 1)
                act.wait_ge(qk_turned, s + 1)
                for h in range(R_HEADS):
                    rows = slice(h * R_DK, (h + 1) * R_DK)
                    nc.scalar.activation(q_t[rows, h, :], bank[2][rows, 0:TOKENS], ACT.Copy)
                nc.scalar.activation(k_t[:, :], bank[2][:, TOKENS:2 * TOKENS], ACT.Copy).then_inc(qk_sb, 1)
                act.wait_ge(out_psum, s + 1)
                nc.scalar.activation(o_raw[:, :, :], bank[7][:, :].rearrange("p (n d) -> p n d", d=R_DV), ACT.Copy).then_inc(o_copied, 1)
                nc.scalar.activation(sq[:, :, :], bank[7][:, :].rearrange("p (n d) -> p n d", d=R_DV), ACT.Square).then_inc(squared, 1)
                act.wait_ge(ms_done, s + 1)
                nc.scalar.activation(ln_ms[:, :], ms[:, :], ACT.Ln, scale=1.0 / R_DV, bias=eps[:, 0:1]).then_inc(ln_done, 1)
                act.wait_ge(ln_done, s + 1)
                nc.scalar.activation(rstd[:, :], ln_ms[:, :], ACT.Exp, scale=-0.5).then_inc(rstd_done, 1)
                act.wait_ge(o_turned, s + 1)
                nc.scalar.activation(o_t[:, :, :, :], bank[2][:, :].rearrange("p (b c n) -> p b c n", b=BPS, c=2), ACT.Copy).then_inc(o_sb, 1)

        @block.vector
        def _(dve):
            sin = const[:, slice_of("ret_sin")].rearrange("p (b n) -> p b n", b=BPS)
            decay = const[:, slice_of("ret_decay")].rearrange("p (h n) -> p h n", h=R_HEADS)
            hd = R_DK // 2

            def halves(t, which):
                return t.rearrange("p b (n two d) -> p two (b n) d", two=2, d=hd)[:, which]

            dve.wait_ge(w_in, 64)
            dve.wait_ge(zeroed, 1)
            with dve.Fori(0, SEQS) as s:
                dve.wait_ge(raw_ready, BPS * (s + 1))
                for out_half in range(2):
                    last = nc.vector.tensor_tensor(halves(part2[:, :, :], out_half), halves(raw[:, :, :], 1 - out_half),
                                                   halves(sin, out_half), ALU.mult)
                last.then_inc(rot_steps, 1)
                dve.wait_ge(rot_steps, s + 1)
                dve.wait_ge(part1_done, s + 1)
                nc.vector.tensor_tensor(rot[:, :, :], part1[:, :, :], part2[:, :, :], ALU.add).then_inc(rot_ready, 1)
                for h in range(R_HEADS):
                    dve.wait_ge(scores_ready, s * R_HEADS + h + 1)
                    nc.vector.tensor_tensor(probs_t[:, h, :], bank[3 + h][:, 0:3 * P], decay[:, h, :], ALU.mult).then_inc(decayed, 1)
                dve.wait_ge(squared, s + 1)
                nc.vector.tensor_reduce(ms[:, :], sq[:, :, :], AX.X, ALU.add).then_inc(ms_done, 1)
                g = gnorm[:, :].unsqueeze(1).broadcast_to([P, NBH, R_DV])
                dve.wait_ge(o_copied, s + 1)
                nc.vector.tensor_tensor(o_n[:, :, :], o_raw[:, :, :], g, ALU.mult).then_inc(norm_steps, 1)
                dve.wait_ge(norm_steps, 2 * s + 1)
                gt = gate[:, bass.ds(s * BPS, BPS), :].rearrange("p b (h d) -> p (b h) d", d=R_DV)
                nc.vector.tensor_tensor(o_n[:, :, :], o_n[:, :, :], gt, ALU.mult).then_inc(norm_steps, 1)
                dve.wait_ge(norm_steps, 2 * s + 2)
                dve.wait_ge(rstd_done, s + 1)
                nc.vector.tensor_tensor(gated[:, :, :], o_n[:, :, :], rstd[:, :].unsqueeze(2).broadcast_to([P, NBH, R_DV]),
                                        ALU.mult).then_inc(gated_done, 1)
                for b in range(BPS):
                    dve.wait_ge(wo_psum, s * BPS + b + 1)
                    dst = x1[:, bass.ds(s * BPS + b, 1), :].rearrange("p o f -> p (o f)")
                    nc.vector.tensor_tensor(dst, bank[b][:, 0:D], dst, ALU.add).then_inc(added, 1)


LAYERS, HEADS, DIM, WINDOW = 6, 16, 64, 32
PAIRS = HEADS // 2
HIDDEN = 341
H_ROWS = (128, 128, 85)
QK_SCALE = 8.0
VEC = {"ln_g": 0, "ln_b": 1, "b2": 2, "b_a": 3, "b_gate": 6}
N_VEC = 9


def rotary_base():
    half = np.arange(0, DIM, 2, dtype=np.float32)
    inv_freq = (1.0 / np.float32(10000.0) ** (half / np.float32(DIM))).astype(np.float32)
    t = np.arange(TOKENS, dtype=np.float32)
    freqs = t[:, None] * inv_freq[None, :]
    base = ((half + np.float32(0.4 * DIM)) / np.float32(1.4 * DIM)).astype(np.float32)
    power = ((t - TOKENS // 2) / (WINDOW // 2)).astype(np.float32)
    scale = base[None, :] ** power[:, None]
    scale = np.concatenate([scale, scale], 1)
    cos = np.concatenate([np.cos(freqs)] * 2, 1)
    sin = np.concatenate([-np.sin(freqs), np.sin(freqs)], 1)
    t4 = np.stack([cos * scale, sin * scale, cos / scale, sin / scale], 1)
    return t4.reshape(BPS, P, 4 * DIM).transpose(1, 0, 2).reshape(P, -1)


def band_masks():
    i, j = np.arange(P)[:, None], np.arange(P)[None, :]
    own = np.where((j <= i) & (i - j <= WINDOW), 0.0, MASKED)
    before = np.where(i <= j[:, 0:WINDOW], 0.0, MASKED)
    return {"band": np.tile(own, (1, 4)), "band_prev": np.tile(before, (1, HEADS))}


def transformer(nc, t, y_t, const, ident_f, ident_b, eps):
    with ExitStack() as stack:
        m = Memory(nc, stack, "tr")
        wqkv = m.sb("wqkv", [P, 3 * HEADS * DIM])
        wo = m.sb("wo", [P, PAIRS, D])
        w1 = m.sb("w1", [P, 2 * HIDDEN])
        w2 = m.sb("w2", [P, 3, D])
        vec = m.sb("vec", [P, N_VEC])
        qk_scales = m.sb("qk_scales", [P, 4 * DIM])
        table = m.sb("table", [P, BPS, 4, DIM])
        ones = m.sb("ones", [P, P])
        carrier, carrier_a = m.sb("carrier", [P, 1]), m.sb("carrier_a", [P, 1])
        band_b, prev_b = m.sb("band_b", [P, 4 * P], BF16), m.sb("prev_b", [P, 512], BF16)
        ln_q = m.sb("ln_q", [P, 2])
        xs = m.sb("xs", [P, BPS, P])
        raw, sq, part1, part2 = (m.sb(n, [P, 2, 512]) for n in ("raw", "sq", "part1", "part2"))
        rot = m.sb("rot", [P, 4, 512])
        norm2 = m.sb("norm2", [P, BPS, 4, 8])
        ln_n = m.sb("ln_n", [P, 2, 8])
        q_even, q_odd, k_t = (m.sb(n, [P, PAIRS, TOKENS]) for n in ("q_even", "q_odd", "k_t"))
        v = m.sb("v", [P, BPS, HEADS * DIM])
        top, top_prev, neg_top = m.sb("top", [P, 8, 4]), m.sb("top_prev", [WINDOW, 4, 4]), m.sb("neg_top", [P, 8, 4])
        sums, sum_prev, inv = m.sb("sums", [P, 8, 4]), m.sb("sum_prev", [WINDOW, 4, 4]), m.sb("inv", [P, 8, 4])
        probs = m.sb("probs", [P, 4, 4, P])
        arg_prev = m.sb("arg_prev", [WINDOW, 4, 4, WINDOW])
        probs_prev = m.sb("probs_prev", [WINDOW, 4, 4, WINDOW])
        probs_t = m.sb("probs_t", [P, 2, 4 * P])
        probs_prev_t = m.sb("probs_prev_t", [P, 4, 4 * WINDOW])
        o_t = m.sb("o_t", [P, PAIRS, TOKENS])
        xf, centred, sq_f, ln_var, rstd_f, scaled, xn_f = (m.sb(n, [P, TOKENS]) for n in (
            "xf", "centred", "sq_f", "ln_var", "rstd_f", "scaled", "xn_f"))
        gelu = m.sb("gelu", [P, 3, TOKENS])
        hid = m.sb("hid", [P, 3, TOKENS])
        bank = m.banks()
        unit_bank, v_bank, score_bank, q_turn_bank, p_turn_bank, out_bank, misc_bank = (
            bank[0], bank[1], bank[2:4], bank[4], bank[5], bank[6], bank[7])
        w1_bank = (bank[1], bank[0], bank[1])
        S = {n: m.sem(n) for n in (
            "const_done", "zeroed", "wqkv_in", "wo_in", "ffn_in", "scales_in", "table_done",
            "xs_ready", "unit_psum", "raw_ready", "part1_done", "norm2_done", "ln_n_done", "inv_norm_done",
            "part2_done", "rot_done", "k_scaled", "unit_turned", "q_even_sb", "q_odd_sb", "k_sb",
            "v_psum", "v_sb", "prev_psum", "scores_psum", "top_done", "top_joined", "neg_top_done", "exp_done",
            "arg_scaled", "arg_ready", "exp_prev_done", "sum_prev_done", "sums_joined", "inv_done",
            "prev_normed", "prev_turned", "probs_ready", "turned", "turned_sb", "out_psum", "o_sb", "wo_psum", "y_added",
            "xf_ready", "mean_psum", "centred_done", "sq_f_done", "var_psum", "ln_var_done", "rstd_f_done",
            "scaled_done", "xn_f_done", "w1_psum", "gelu_done", "hid_done", "w2_psum", "ffn_added")}
        block = stack.enter_context(nc.Block())
        K = 8


        def jobs(eng, body, ffn_alone, layer_start):
            with eng.Fori(0, LAYERS) as layer:
                layer_start(layer)
                body(layer, 0, layer * SEQS, False, True)
                with eng.Fori(1, SEQS - 1) as s:
                    body(layer, s, layer * SEQS + s, True, True)
                body(layer, SEQS - 1, layer * SEQS + SEQS - 1, True, False)
                ffn_alone(layer * SEQS + SEQS - 1)

        def plain_wait(eng):
            eng.wait_ge(S["zeroed"], 7)

        def units_of(slot, J):
            return 8 * J + 5 + slot, 1 if slot < 3 or slot == 7 else 0, (slot + 1) % 4

        def has_unit(slot, has_next):
            return 0 <= slot < (K if has_next else 3)

        def first_unit(u, J):
            return 8 * J + u, u // 4, u % 4

        def y_tokens(s, start, n):
            return y_t[:, bass.ds(s * TOKENS + start, n)]

        @block.sync
        def _(sp):
            def load(layer):
                sp.wait_ge(S["v_psum"], layer * (4 * SEQS) + 3)
                sp.dma_start(wqkv[:, :], t["tr_qkv"][bass.ds(layer, 1), :, :].rearrange("o p n -> p (o n)")).then_inc(S["wqkv_in"], 16)
                sp.wait_ge(S["table_done"], layer + 1)
                sp.dma_start(qk_scales[:, :], t["tr_scales"][bass.ds(layer, 1), :].partition_broadcast(P).rearrange("p o n -> p (o n)")
                             ).then_inc(S["scales_in"], 16)
                sp.wait_ge(S["wo_psum"], layer * SEQS + 1)
                sp.dma_start(wo[:, :, :], t["tr_o"][bass.ds(layer, 1), :, :].rearrange("o (c p) f -> p (o c) f", p=P)).then_inc(S["wo_in"], 16)
                sp.wait_ge(S["ffn_added"], layer * SEQS + 1)
                sp.dma_start(w1[:, :], t["tr_w1"][bass.ds(layer, 1), :, :].rearrange("o p n -> p (o n)")).then_inc(S["ffn_in"], 16)
                for c, rows in enumerate(H_ROWS):
                    sp.dma_start(w2[0:rows, c, :], t["tr_w2"][bass.ds(layer, 1), c * P:c * P + rows, :].rearrange("o p n -> p (o n)")
                                 ).then_inc(S["ffn_in"], 16)
                sp.dma_start(vec[:, :], t["tr_vec"][bass.ds(layer, 1), :, :].rearrange("o p n -> p (o n)")).then_inc(S["ffn_in"], 16)

            with sp.Fori(0, LAYERS) as layer:
                load(layer)

        @block.gpsimd
        def _(pool):
            g = nc.gpsimd
            g.memset(ones[:, :], 1.0 / D).then_inc(S["zeroed"], 1)
            pool.wait_ge(S["zeroed"], 1)
            g.memset(xs[:, :, :], 0.0).then_inc(S["zeroed"], 1)
            pool.wait_ge(S["zeroed"], 2)
            g.memset(xf[:, :], 0.0).then_inc(S["zeroed"], 1)
            pool.wait_ge(S["zeroed"], 3)
            g.memset(q_even[:, :, :], 0.0).then_inc(S["zeroed"], 1)
            pool.wait_ge(S["zeroed"], 4)
            g.memset(q_odd[:, :, :], 0.0).then_inc(S["zeroed"], 1)
            pool.wait_ge(S["zeroed"], 5)
            g.memset(ln_q[:, 0:1], float(np.log(QK_SCALE) + 8 * np.log(2.0))).then_inc(S["zeroed"], 1)
            pool.wait_ge(S["zeroed"], 6)
            g.memset(ln_q[:, 1:2], float(8 * np.log(2.0))).then_inc(S["zeroed"], 1)
            pool.wait_ge(S["zeroed"], 7)
            h = D // 2

            def carry_wait():
                g.tensor_tensor(carrier[0:h, :], ones[0:h, 0:1], ones[0:h, 0:1], ALU.mult)

            def products_written(pairs, extra=0):
                pool.wait_ge(S["rot_done"], 2 * pairs + extra + 2)
                pool.wait_ge(S["k_scaled"], pairs)

            def load_xs(s, J, b):
                pool.wait_ge(S["v_psum"], 4 * J + 2 * b + 1)
                carry_wait()
                g.tensor_copy(xs[0:h, b, :], y_t[0:h, bass.ds(s * TOKENS + b * P, P)]).then_inc(S["xs_ready"], 1)
                if b == 0:
                    g.tensor_copy(xs[h:D, 0, 1:P], y_t[h:D, bass.ds(s * TOKENS, P - 1)]).then_inc(S["xs_ready"], 1)
                else:
                    g.tensor_copy(xs[h:D, 1, :], y_t[h:D, bass.ds(s * TOKENS + P - 1, P)]).then_inc(S["xs_ready"], 1)
                pool.wait_ge(S["xs_ready"], 4 * J + 2 * b + 2)

            def cosines(U, b, u):
                kind = u % 2
                pool.wait_ge(S["raw_ready"], U + 1)
                src = raw[:, u % 2, :].rearrange("p (n d) -> p n d", d=DIM)
                cos = table[:, b, 2 * kind, :].unsqueeze(1).broadcast_to([P, 8, DIM])
                g.tensor_tensor(part1[:, u % 2, :].rearrange("p (n d) -> p n d", d=DIM), src, cos, ALU.mult).then_inc(S["part1_done"], 1)

            def rotated(U, b, u):
                pool.wait_ge(S["part1_done"], U + 1)
                pool.wait_ge(S["unit_turned"], U + 1)
                pool.wait_ge(S["part2_done"], U + 1)
                g.tensor_tensor(rot[:, u, :], part1[:, u % 2, :], part2[:, u % 2, :], ALU.add).then_inc(S["rot_done"], 1)

            def scale_k(U, b, u):
                pool.wait_ge(S["rot_done"], U + 3)
                pool.wait_ge(S["inv_norm_done"], U + 1)
                r = rot[:, u, :].rearrange("p (n d) -> p n d", d=DIM)
                g.tensor_tensor(r, r, norm2[:, b, u, :].unsqueeze(2).broadcast_to([P, 8, DIM]), ALU.mult).then_inc(S["k_scaled"], 1)

            def body(layer, s, J, has_ffn, has_next):
                for slot in range(K + 1):
                    if slot == 2 and has_next:
                        products_written(4 * J + 3, 1)
                        load_xs(s + 1, J + 1, 0)
                    if has_unit(slot, has_next):
                        cosines(*units_of(slot, J))
                    if slot % 2 and has_unit(slot - 1, has_next):
                        scale_k(*units_of(slot - 1, J))
                    if has_unit(slot, has_next):
                        rotated(*units_of(slot, J))
                    if slot == 4 and has_next:
                        products_written(4 * J + 4, 2)
                        load_xs(s + 1, J + 1, 1)

            def layer_start(layer):
                J = layer * SEQS
                pool.wait_ge(S["ffn_added"], J + 1)
                load_xs(0, J, 0)
                load_xs(0, J, 1)
                pool.wait_ge(S["table_done"], layer + 2)
                for u in range(5):
                    cosines(*first_unit(u, J))
                    if u in (2, 4):
                        scale_k(*first_unit(u - 1, J))
                    rotated(*first_unit(u, J))

            jobs(pool, body, lambda F: products_written(4 * F + 4), layer_start)

        @block.tensor
        def _(pe):
            mm = nc.tensor.matmul

            def unit_project(U, b, u, first=False):
                if not first:
                    pe.wait_ge(S["raw_ready"], U)
                half = u // 2
                at = (u % 2) * HEADS * DIM + half * 512
                mm(unit_bank[:, :], xs[:, b, :], wqkv[:, at:at + 512], start=True, stop=True).then_inc(S["unit_psum"], 1)

            def unit_turn(U, b, u, J_unit):
                if u % 2:
                    pe.wait_ge(S["k_scaled"], 4 * J_unit + 2 * b + u // 2 + 1)
                else:
                    pe.wait_ge(S["rot_done"], U + 3)
                if u % 2:
                    pe.wait_ge(S["q_even_sb"], 4 * J_unit + 2 * b + u // 2 + 2)
                    pe.wait_ge(S["q_odd_sb"], 4 * J_unit + 2 * b + u // 2 + 2)
                else:
                    pe.wait_ge(S["k_sb"], 4 * J_unit + 2 * b + u // 2 + 1)
                for i in range(4):
                    last = nc.tensor.transpose(q_turn_bank[:, i * P:(i + 1) * P], rot[:, u, i * P:(i + 1) * P], ident_f)
                last.then_inc(S["unit_turned"], 1)

            def v_project(J, u):
                b, half = u // 2, u % 2
                if u:
                    pe.wait_ge(S["v_sb"], 4 * J + u)
                at = 2 * HEADS * DIM + half * 512
                mm(v_bank[:, :], xs[:, b, :], wqkv[:, at:at + 512], start=True, stop=True).then_inc(S["v_psum"], 1)

            def scores(J, k):
                b, g4 = k // 4, k % 4
                if k % 2 == 0:
                    n = 4 * J + 2 * b + g4 // 2 + 1 + 1
                    pe.wait_ge(S["q_even_sb"], n)
                    pe.wait_ge(S["q_odd_sb"], n)
                    pe.wait_ge(S["k_sb"], n)
                pe.wait_ge(S["exp_done"], K * J + k - 1 + 2)
                sc = score_bank[k % 2]
                mm(sc[:, :], ident_b[:, :], band_b[:, :], start=True, stop=False)
                for i in range(4):
                    h = 4 * g4 + i
                    q = (q_even, q_odd)[h % 2]
                    tok = slice(b * P, (b + 1) * P)
                    last = mm(sc[:, i * P:(i + 1) * P], q[:, h // 2, tok], k_t[:, h // 2, tok], start=False, stop=i == 3)
                last.then_inc(S["scores_psum"], 1)

            def scores_before(J, has_ffn):
                for name in ("q_even_sb", "q_odd_sb"):
                    pe.wait_ge(S[name], 4 * J + 2 + 2 + 1)
                if has_ffn:
                    pe.wait_ge(S["ln_var_done"], J)
                else:
                    pe.wait_ge(S["ffn_added"], J + 1)
                mm(misc_bank[0:WINDOW, :], ident_b[:, 0:WINDOW], prev_b[:, :], start=True, stop=False)
                for h in range(HEADS):
                    q = (q_even, q_odd)[h % 2]
                    last = mm(misc_bank[0:WINDOW, h * WINDOW:(h + 1) * WINDOW], q[:, h // 2, P:P + WINDOW],
                              k_t[:, h // 2, P - WINDOW:P], start=False, stop=h == HEADS - 1)
                last.then_inc(S["prev_psum"], 1)

            def turn_probs(J, k):
                pe.wait_ge(S["probs_ready"], K * J + k + 1)
                pe.wait_ge(S["turned_sb"], K * J + k + 1)
                for i in range(4):
                    last = nc.tensor.transpose(p_turn_bank[:, i * P:(i + 1) * P], probs[:, k % 4, i, :], ident_f)
                last.then_inc(S["turned"], 1)

            def outputs(J, k):
                b, g4 = k // 4, k % 4
                if k % 2 == 0:
                    pe.wait_ge(S["o_sb"], 4 * J + k // 2 + 1)
                    pe.wait_ge(S["v_sb"], 4 * J + 2 * b + (k % 4) // 2 + 1)
                pe.wait_ge(S["turned_sb"], K * J + k + 2)
                if b:
                    pe.wait_ge(S["prev_turned"], 4 * J + k - 4 + 1)
                for i in range(4):
                    h = 4 * g4 + i
                    rows = slice(h % 2 * DIM, (h % 2 + 1) * DIM)
                    at = (h // 2 % 4) * P
                    hd = slice(h * DIM, (h + 1) * DIM)
                    last = mm(out_bank[rows, at:at + P], v[:, b, hd], probs_t[:, k % 2, i * P:(i + 1) * P], start=True, stop=b == 0)
                    if b:
                        last = mm(out_bank[rows, at:at + WINDOW], v[P - WINDOW:P, 0, hd],
                                  probs_prev_t[P - WINDOW:P, g4, i * WINDOW:(i + 1) * WINDOW], start=False, stop=True)
                last.then_inc(S["out_psum"], 1)

            def project_out(J):
                pe.wait_ge(S["o_sb"], 4 * J + 4 + 1)
                pe.wait_ge(S["ffn_added"], J + 1)
                for c in range(PAIRS):
                    last = mm(misc_bank[:, 0:TOKENS], wo[:, c, :], o_t[:, c, :], start=c == 0, stop=c == PAIRS - 1)
                last.then_inc(S["wo_psum"], 1)

            def ffn_mean(F):
                pe.wait_ge(S["xf_ready"], 2 * F + 2)
                mm(misc_bank[:, 0:TOKENS], ones[:, :], xf[:, :], start=True, stop=True).then_inc(S["mean_psum"], 1)

            def ffn_var(F):
                pe.wait_ge(S["sq_f_done"], F + 1)
                mm(misc_bank[:, 0:TOKENS], ones[:, :], sq_f[:, :], start=True, stop=True).then_inc(S["var_psum"], 1)

            def ffn_w1(F, c):
                rows = H_ROWS[c]
                if c == 0:
                    pe.wait_ge(S["xn_f_done"], F + 1)
                if c == 2:
                    pe.wait_ge(S["hid_done"], 3 * F + 1)
                for i in range(2):
                    at = i * HIDDEN + c * P
                    last = mm(w1_bank[c][0:rows, i * TOKENS:(i + 1) * TOKENS], w1[:, at:at + rows], xn_f[:, :], start=True, stop=True)
                last.then_inc(S["w1_psum"], 1)

            def ffn_w2(F):
                pe.wait_ge(S["hid_done"], 3 * F + 3)
                for c, rows in enumerate(H_ROWS):
                    last = mm(misc_bank[:, 0:TOKENS], w2[0:rows, c, :], hid[0:rows, c, :], start=c == 0, stop=c == 2)
                last.then_inc(S["w2_psum"], 1)

            def next_unit(k, J):
                if k in (3, 7):
                    pe.wait_ge(S["xs_ready"], 4 * J + (6 if k == 3 else 8))
                unit_project(*units_of(k, J))

            def body(layer, s, J, has_ffn, has_next):
                for k in range(K + 3):
                    if 1 <= k < K:
                        scores(J, k)
                    if k == K + 1 and has_next:
                        scores(J + 1, 0)
                    if k == 4:
                        scores_before(J, has_ffn)
                    if 2 <= k < K + 2:
                        turn_probs(J, k - 2)
                    if k < 4:
                        v_project(J, k)
                    if k == K + 1 and has_ffn:
                        ffn_w1(J - 1, 2)
                    if k >= K:
                        outputs(J, k - 3)
                    if k == K and has_ffn:
                        pe.wait_ge(S["raw_ready"], 8 * J + (13 if has_next else 8))
                        ffn_w1(J - 1, 1)
                    if k == K + 2 and has_ffn:
                        ffn_w2(J - 1)
                    if has_unit(k - 2, has_next):
                        U, b, u = units_of(k - 2, J)
                        unit_turn(U, b, u, J if k - 2 < 3 else J + 1)
                    if k == K + 1 and has_next:
                        if has_ffn:
                            pe.wait_ge(S["hid_done"], 3 * (J - 1) + 2)
                        next_unit(0, J + 1)
                    if has_unit(k + 1, has_next):
                        next_unit(k + 1, J)
                    if 3 <= k < K:
                        outputs(J, k - 3)
                    if k == K - 1 and has_ffn:
                        pe.wait_ge(S["v_sb"], 4 * J + 4)
                        ffn_w1(J - 1, 0)
                    if k == 1 and has_ffn:
                        project_out(J - 1)
                    if k == 2 and has_ffn:
                        ffn_mean(J - 1)
                    if k == 3 and has_ffn:
                        ffn_var(J - 1)

            def layer_start(layer):
                J = layer * SEQS
                pe.wait_ge(S["wqkv_in"], 16 * (layer + 1))
                pe.wait_ge(S["xs_ready"], 4 * J + 4)
                for u in range(7):
                    if u < 5:
                        unit_project(*first_unit(u, J), first=u == 0)
                    if u >= 2:
                        unit_turn(*first_unit(u - 2, J), J)
                scores(J, 0)
                next_unit(0, J)
                plain_wait(pe)
                pe.wait_ge(S["wo_in"], 16 * (layer + 1))
                pe.wait_ge(S["ffn_in"], 16 * 5 * (layer + 1))

            def ffn_alone(F):
                project_out(F)
                ffn_mean(F)
                ffn_var(F)
                for c in range(3):
                    ffn_w1(F, c)
                ffn_w2(F)
                plain_wait(pe)
                pe.wait_ge(S["ffn_added"], F + 2)

            pe.sem_inc(S["v_psum"], 3)
            pe.sem_inc(S["wo_psum"], 1)
            pe.wait_ge(S["const_done"], 2)
            pe.wait_ge(S["zeroed"], 7)
            jobs(pe, body, ffn_alone, layer_start)

        @block.scalar
        def _(act):
            a = nc.scalar.activation

            def unit_copy(U, b, u):
                act.wait_ge(S["unit_psum"], U + 1)
                act.wait_ge(S["rot_done"], U + 1)
                a(raw[:, u % 2, :], unit_bank[:, :], ACT.Copy)
                a(sq[:, u % 2, :], unit_bank[:, :], ACT.Square).then_inc(S["raw_ready"], 1)

            def unit_norm(U, b, u):
                act.wait_ge(S["norm2_done"], 2 * U + 2)
                a(ln_n[:, u % 2, :], norm2[:, b, u, :], ACT.Ln, scale=2.0 ** 16).then_inc(S["ln_n_done"], 1)
                act.wait_ge(S["ln_n_done"], U + 1)
                a(norm2[:, b, u, :], ln_n[:, u % 2, :], ACT.Exp, scale=-0.5, bias=ln_q[:, u % 2:u % 2 + 1]).then_inc(S["inv_norm_done"], 1)

            def unit_out(U, b, u):
                act.wait_ge(S["unit_turned"], U + 1 + 4)
                src = q_turn_bank[:, :].rearrange("p (c t) -> p c t", t=P)
                pairs, tok = slice(u // 2 * 4, u // 2 * 4 + 4), slice(b * P, (b + 1) * P)
                if u % 2:
                    a(k_t[:, pairs, tok], src, ACT.Copy).then_inc(S["k_sb"], 1)
                else:
                    a(q_even[0:DIM, pairs, tok], src[0:DIM], ACT.Copy).then_inc(S["q_even_sb"], 1)

            def v_copy(J, u):
                act.wait_ge(S["v_psum"], 4 * J + u + 1 + 3)
                b, half = u // 2, u % 2
                a(v[:, b, half * 512:(half + 1) * 512], v_bank[:, :], ACT.Copy).then_inc(S["v_sb"], 1)

            def exps(J, k):
                b, g4 = k // 4, k % 4
                act.wait_ge(S["neg_top_done"], K * J + k + 1)
                for i in range(4):
                    h = 4 * g4 + i
                    last = a(probs[:, k % 4, i, :], score_bank[k % 2][:, i * P:(i + 1) * P], ACT.Exp,
                             scale=norm2[:, b, h // 8 * 2, h % 8:h % 8 + 1], bias=neg_top[:, k, i:i + 1],
                             accum_out=sums[:, k, i:i + 1])
                last.then_inc(S["exp_done"], 1)
                if b:
                    act.wait_ge(S["arg_ready"], 4 * J + g4 + 1)
                    a(probs_prev[:, g4, :, :], arg_prev[:, g4, :, :], ACT.Exp).then_inc(S["exp_prev_done"], 1)

            def turned_copy(J, k):
                act.wait_ge(S["turned"], K * J + k + 1)
                a(probs_t[:, k % 2, :], p_turn_bank[:, :], ACT.Copy).then_inc(S["turned_sb"], 1)

            def load_xf(s, F):
                h = D // 2
                act.wait_ge(S["centred_done"], F + 1)
                act.wait_ge(S["y_added"], F + 1)
                a(carrier_a[:, :], eps[:, :], ACT.Copy)
                a(xf[0:h, :], y_t[0:h, bass.ds(s * TOKENS, TOKENS)], ACT.Copy).then_inc(S["xf_ready"], 1)
                a(xf[h:D, 1:TOKENS], y_t[h:D, bass.ds(s * TOKENS, TOKENS - 1)], ACT.Copy).then_inc(S["xf_ready"], 1)

            def ffn_square(F):
                act.wait_ge(S["centred_done"], F + 2)
                a(sq_f[:, :], centred[:, :], ACT.Square).then_inc(S["sq_f_done"], 1)

            def ffn_rstd(F):
                act.wait_ge(S["var_psum"], F + 1)
                a(ln_var[:, :], misc_bank[:, 0:TOKENS], ACT.Ln, bias=eps[:, 0:1]).then_inc(S["ln_var_done"], 1)
                act.wait_ge(S["ln_var_done"], F + 1)
                a(rstd_f[:, :], ln_var[:, :], ACT.Exp, scale=-0.5).then_inc(S["rstd_f_done"], 1)

            def ffn_gelu(F, c):
                rows = H_ROWS[c]
                act.wait_ge(S["w1_psum"], 3 * F + c + 1)
                a(gelu[0:rows, c, :], w1_bank[c][0:rows, TOKENS:2 * TOKENS], ACT.Gelu,
                  bias=vec[0:rows, VEC["b_gate"] + c:VEC["b_gate"] + c + 1]).then_inc(S["gelu_done"], 1)

            def begin(J):
                unit_copy(*units_of(0, J))
                exps(J, 0)

            def body(layer, s, J, has_ffn, has_next):
                for k in range(K + 3):
                    if k and has_unit(k, has_next):
                        unit_copy(*units_of(k, J))
                    if has_unit(k - 3, has_next):
                        unit_out(*units_of(k - 3, J))
                    if k == 4 and has_ffn:
                        ffn_rstd(J - 1)
                    if has_unit(k - 1, has_next):
                        unit_norm(*units_of(k - 1, J))
                    if 2 <= k < K + 2:
                        turned_copy(J, k - 2)
                    if k == 2 and has_ffn:
                        load_xf(s - 1, J - 1)
                    if k == 3 and has_ffn:
                        ffn_square(J - 1)
                    if 1 <= k < K:
                        exps(J, k)
                    if k < 4:
                        v_copy(J, k)
                    if k == K and has_ffn:
                        ffn_gelu(J - 1, 0)
                        ffn_gelu(J - 1, 1)
                    if k == K + 1 and has_ffn:
                        ffn_gelu(J - 1, 2)
                        nc.scalar.preload_act_table_set(LN_EXP)
                    if k == K + 1 and has_next:
                        begin(J + 1)

            def layer_start(layer):
                J = layer * SEQS
                for u in range(7):
                    if u < 5:
                        unit_copy(*first_unit(u, J))
                    if 1 <= u <= 5:
                        unit_norm(*first_unit(u - 1, J))
                    if u >= 2:
                        unit_out(*first_unit(u - 2, J))
                begin(J)

            def ffn_alone(F):
                load_xf(SEQS - 1, F)
                ffn_square(F)
                ffn_rstd(F)
                for c in range(3):
                    ffn_gelu(F, c)
                nc.scalar.preload_act_table_set(LN_EXP)

            nc.scalar.preload_act_table_set(LN_EXP)
            act.sem_inc(S["exp_done"], 2)
            act.sem_inc(S["turned_sb"], 1)
            act.sem_inc(S["k_sb"], 1)
            act.sem_inc(S["q_even_sb"], 1)
            act.wait_ge(S["zeroed"], 7)
            jobs(act, body, ffn_alone, layer_start)

        @block.vector
        def _(dve):
            w = nc.vector
            hd = DIM // 2

            def unit_rotate(U, b, u):
                kind, slot = u % 2, u % 2
                dve.wait_ge(S["raw_ready"], U + 1)
                w.tensor_reduce(norm2[:, b, u, :], sq[:, slot, :].rearrange("p (n d) -> p n d", d=DIM), AX.X, ALU.add
                                ).then_inc(S["norm2_done"], 1)
                src = raw[:, slot, :].rearrange("p (n two d) -> p two n d", two=2, d=hd)
                dst = part2[:, slot, :].rearrange("p (n two d) -> p two n d", two=2, d=hd)
                for o in range(2):
                    sin = table[:, b, 2 * kind + 1, o * hd:(o + 1) * hd].unsqueeze(1).broadcast_to([P, 8, hd])
                    last = w.tensor_tensor(dst[:, o], src[:, 1 - o], sin, ALU.mult)
                last.then_inc(S["part2_done"], 1)
                dve.wait_ge(S["norm2_done"], 2 * U + 1)
                w.tensor_scalar(norm2[:, b, u, :], norm2[:, b, u, :], 1e-24, None, ALU.max).then_inc(S["norm2_done"], 1)

            def unit_out(U, b, u):
                if u % 2 == 0:
                    dve.wait_ge(S["unit_turned"], U + 1 + 4)
                    src = q_turn_bank[:, :].rearrange("p (c t) -> p c t", t=P)
                    w.tensor_copy(q_odd[DIM:P, u // 2 * 4:u // 2 * 4 + 4, b * P:(b + 1) * P], src[DIM:P]).then_inc(S["q_odd_sb"], 1)

            def softmax_steps(J, k):
                new, old = k < K, k >= 1
                b, g4, b0, h4 = k // 4, k % 4, (k - 1) // 4, (k - 1) % 4
                new_prev, old_prev = new and b == 1, old and b0 == 1
                spread = lambda t: t.unsqueeze(2).broadcast_to([WINDOW, 4, WINDOW])
                if new:
                    inv_q = norm2[:, b, g4 // 2 * 2, g4 % 2 * 4:g4 % 2 * 4 + 4]
                    dve.wait_ge(S["scores_psum"], K * J + k + 1)
                    last = w.tensor_reduce(top[:, k, :], score_bank[k % 2][:, :].rearrange("p (n j) -> p n j", j=P), AX.X, ALU.max)
                if new_prev:
                    dve.wait_ge(S["prev_psum"], J + 1)
                    before = misc_bank[0:WINDOW, g4 * P:(g4 + 1) * P].rearrange("p (n j) -> p n j", j=WINDOW)
                    last = w.tensor_reduce(top_prev[:, g4, :], before, AX.X, ALU.max)
                if new:
                    last.then_inc(S["top_done"], 1)
                if old:
                    dve.wait_ge(S["exp_done"], K * J + k + 2)
                if old_prev:
                    dve.wait_ge(S["exp_prev_done"], 4 * J + h4 + 1)
                    w.tensor_reduce(sum_prev[:, h4, :], probs_prev[:, h4, :, :], AX.X, ALU.add).then_inc(S["sum_prev_done"], 1)
                if new:
                    dve.wait_ge(S["top_done"], K * J + k + 1)
                if new_prev:
                    w.tensor_tensor(top[0:WINDOW, k, :], top[0:WINDOW, k, :], top_prev[:, g4, :], ALU.max).then_inc(S["top_joined"], 1)
                if old_prev:
                    dve.wait_ge(S["sum_prev_done"], 4 * J + h4 + 1)
                    w.tensor_tensor(sums[0:WINDOW, k - 1, :], sums[0:WINDOW, k - 1, :], sum_prev[:, h4, :], ALU.add).then_inc(S["sums_joined"], 1)
                if new_prev:
                    dve.wait_ge(S["top_joined"], 4 * J + g4 + 1)
                if new:
                    w.scalar_tensor_tensor(neg_top[:, k, :], top[:, k, :], -1.0, inv_q, ALU.mult, ALU.mult).then_inc(S["neg_top_done"], 1)
                if new_prev:
                    w.tensor_tensor(arg_prev[:, g4, :, :], before, spread(inv_q[0:WINDOW]), ALU.mult).then_inc(S["arg_scaled"], 1)
                if old_prev:
                    dve.wait_ge(S["sums_joined"], 4 * J + h4 + 1)
                if old:
                    w.reciprocal(inv[:, k - 1, :], sums[:, k - 1, :]).then_inc(S["inv_done"], 1)
                if new_prev:
                    dve.wait_ge(S["arg_scaled"], 4 * J + g4 + 1 + 1)
                    dve.wait_ge(S["neg_top_done"], K * J + k + 1)
                    w.tensor_tensor(arg_prev[:, g4, :, :], arg_prev[:, g4, :, :], spread(neg_top[0:WINDOW, k, :]), ALU.add
                                    ).then_inc(S["arg_ready"], 1)
                if old:
                    dve.wait_ge(S["inv_done"], K * J + k)
                if old_prev:
                    w.tensor_tensor(probs_prev[:, h4, :, :], probs_prev[:, h4, :, :], spread(inv[0:WINDOW, k - 1, :]), ALU.mult
                                    ).then_inc(S["prev_normed"], 1)
                if old:
                    w.tensor_tensor(probs[:, (k - 1) % 4, :, :], probs[:, (k - 1) % 4, :, :],
                                    inv[:, k - 1, :].unsqueeze(2).broadcast_to([P, 4, P]), ALU.mult).then_inc(S["probs_ready"], 1)
                if old_prev:
                    dve.wait_ge(S["prev_normed"], 4 * J + h4 + 1)
                    w.transpose(probs_prev_t[P - WINDOW:P, h4, :], probs_prev[:, h4, :, :].rearrange("p n j -> p (n j)")).then_inc(S["prev_turned"], 1)

            def out_copy(J, f):
                dve.wait_ge(S["out_psum"], K * J + 2 * f + 2)
                b, half = f // 2, f % 2
                w.tensor_copy(o_t[:, 4 * half:4 * half + 4, b * P:(b + 1) * P], out_bank[:, :].rearrange("p (c t) -> p c t", t=P)
                              ).then_inc(S["o_sb"], 1)

            def residual(s, J):
                dve.wait_ge(S["wo_psum"], J + 2)
                dst = y_tokens(s, 0, TOKENS)
                w.tensor_tensor(dst, misc_bank[:, 0:TOKENS], dst, ALU.add).then_inc(S["y_added"], 1)

            def ffn_centre(F):
                dve.wait_ge(S["mean_psum"], F + 1)
                w.tensor_tensor(centred[:, :], xf[:, :], misc_bank[:, 0:TOKENS], ALU.subtract).then_inc(S["centred_done"], 1)

            def ffn_norm(F):
                dve.wait_ge(S["rstd_f_done"], F + 1)
                w.scalar_tensor_tensor(scaled[:, :], centred[:, :], vec[:, VEC["ln_g"]:VEC["ln_g"] + 1], rstd_f[:, :],
                                       ALU.mult, ALU.mult).then_inc(S["scaled_done"], 1)
                dve.wait_ge(S["scaled_done"], F + 1)
                w.tensor_scalar(xn_f[:, :], scaled[:, :], vec[:, VEC["ln_b"]:VEC["ln_b"] + 1], None, ALU.add).then_inc(S["xn_f_done"], 1)

            def ffn_hidden(F, c):
                rows = H_ROWS[c]
                dve.wait_ge(S["gelu_done"], 3 * F + c + 1)
                w.scalar_tensor_tensor(hid[0:rows, c, :], w1_bank[c][0:rows, 0:TOKENS], vec[0:rows, VEC["b_a"] + c:VEC["b_a"] + c + 1],
                                       gelu[0:rows, c, :], ALU.add, ALU.mult).then_inc(S["hid_done"], 1)

            def ffn_add(s, F):
                dve.wait_ge(S["w2_psum"], F + 1)
                dst = y_tokens(s, 0, TOKENS)
                w.scalar_tensor_tensor(dst, misc_bank[:, 0:TOKENS], vec[:, VEC["b2"]:VEC["b2"] + 1], dst, ALU.add, ALU.add
                                       ).then_inc(S["ffn_added"], 1)

            def body(layer, s, J, has_ffn, has_next):
                for k in range(K + 3):
                    if has_unit(k - 3, has_next):
                        unit_out(*units_of(k - 3, J))
                    if k in (5, 7):
                        out_copy(J, (k - 5) // 2)
                    if k == 3 and has_ffn:
                        ffn_centre(J - 1)
                    if 1 <= k <= K:
                        softmax_steps(J, k)
                    if k == K + 1 and has_next:
                        softmax_steps(J + 1, 0)
                    if has_unit(k, has_next):
                        unit_rotate(*units_of(k, J))
                    if k == 1 and has_ffn:
                        residual(s - 1, J - 1)
                    if k == 5 and has_ffn:
                        ffn_norm(J - 1)
                    if k == K:
                        out_copy(J, 2)
                    if k == K and has_ffn:
                        ffn_hidden(J - 1, 0)
                        ffn_hidden(J - 1, 1)
                    if k == K + 1 and has_ffn:
                        ffn_hidden(J - 1, 2)
                    if k == K + 2:
                        out_copy(J, 3)
                    if k == K + 2 and has_ffn:
                        ffn_add(s - 1, J - 1)

            def layer_start(layer):
                J = layer * SEQS
                dve.wait_ge(S["scales_in"], 16 * (layer + 1))
                for b in range(BPS):
                    base = const[:, slice_of("rotary")].rearrange("p (b n) -> p b n", b=BPS)[:, b, :]
                    last = w.tensor_tensor(table[:, b, :, :].rearrange("p a d -> p (a d)"), base, qk_scales[:, :], ALU.mult)
                last.then_inc(S["table_done"], 1)
                dve.wait_ge(S["table_done"], layer + 2)
                for u in range(7):
                    if u < 5:
                        unit_rotate(*first_unit(u, J))
                    if u >= 2:
                        unit_out(*first_unit(u - 2, J))
                softmax_steps(J, 0)
                dve.wait_ge(S["ffn_in"], 16 * 5 * (layer + 1))

            def ffn_alone(F):
                residual(SEQS - 1, F)
                ffn_centre(F)
                ffn_norm(F)
                for c in range(3):
                    ffn_hidden(F, c)
                ffn_add(SEQS - 1, F)

            w.tensor_copy(band_b[:, :], const[:, slice_of("band")]).then_inc(S["const_done"], 1)
            w.tensor_copy(prev_b[:, :], const[:, slice_of("band_prev")]).then_inc(S["const_done"], 1)
            for name, n in (("rot_done", 2), ("unit_turned", 4), ("q_odd_sb", 1), ("o_sb", 1), ("table_done", 1),
                            ("ffn_added", 1), ("centred_done", 1), ("arg_scaled", 1)):
                dve.sem_inc(S[name], n)
            dve.wait_ge(S["zeroed"], 7)
            jobs(dve, body, ffn_alone, layer_start)


def add_transposed(nc, x1, y_t, ident):
    with ExitStack() as stack:
        m = Memory(nc, stack, "last")
        bank = m.banks()
        turned, added = m.sem("turned"), m.sem("added")
        block = stack.enter_context(nc.Block())

        @block.tensor
        def _(pe):
            for k in range(BLOCKS):
                last = nc.tensor.transpose(bank[k // 4][:, k % 4 * P:(k % 4 + 1) * P], y_t[:, k * P:(k + 1) * P], ident)
                if k % 4 == 3:
                    last.then_inc(turned, 1)

        @block.vector
        def _(dve):
            for q in range(8):
                dve.wait_ge(turned, q + 1)
                dst = x1[:, 4 * q:4 * q + 4, :]
                nc.vector.tensor_tensor(dst, bank[q][:, :].rearrange("p (k f) -> p k f", f=D), dst, ALU.add).then_inc(added, 1)


def store_output(nc, x1, out_dram):
    with ExitStack() as stack:
        m = Memory(nc, stack, "store")
        stored = m.sem("stored")
        block = stack.enter_context(nc.Block())
        view = out_dram.rearrange("s (b p) f -> p (s b) f", p=P)

        @block.sync
        def _(sp):
            sp.dma_start(view, x1[:, :, :]).then_inc(stored, 16)
            sp.wait_ge(stored, 16)


def program(nc, t, out):
    with ExitStack() as stack:
        m = Memory(nc, stack, "main")
        x1 = m.sb("x1", [P, BLOCKS, D])
        xn_t = m.sb("xn_t", [P, SEQS * TOKENS])
        const = m.sb("const", [P, N_CONST])
        eps = m.sb("eps", [P, 1])
        ident_b = m.sb("ident_b", [P, P], BF16)
        ident_f = const[:, slice_of("ident")]
        with ExitStack() as first_layer:
            f = Memory(nc, first_layer, "layer0")
            causal_b = f.sb("causal_b", [P, 3 * P], BF16)
            staged = f.sb("staged", [P, 2, 2, D_FF])
            wd = f.sb("wd", [P, EXPERTS, FC, D])
            normalise(nc, "norm0", x1, xn_t, const, eps, t["x"], t["const"], ((ident_b, "ident"), (causal_b, "causal")))
            causal_attention(nc, t["wq"], t["wk"], t["wv"], t["wo"], x1, xn_t, ident_f, ident_b, causal_b,
                             tuple((staged[:, e, side, :], t[name][e]) for e in range(2) for side, name in enumerate(("moe_gate", "moe_up")))
                             + ((wd[:, :, :, :], t["moe_down"].rearrange("e (c p) n -> p e c n", p=P)),))
            mixture_of_experts(nc, t["router"], (t["moe_gate"], t["moe_up"]), x1, xn_t, const, staged, wd)
        normalise(nc, "norm1", x1, xn_t, const, eps)
        retention(nc, t["ret_qkv"], t["ret_g"], t["ret_o"], t["ret_gnorm"], x1, xn_t, const, eps)
        transformer(nc, t, xn_t, const, ident_f, ident_b, eps)
        add_transposed(nc, x1, xn_t, ident_f)
        store_output(nc, x1, out)


def kernel(**inputs):
    import concourse.bacc as bacc
    from concourse.bass_utils import run_bass_kernel_spmd

    a = {n: np.asarray(v) for n, v in inputs.items()}

    def proj(w):
        return w.reshape(-1, D).T

    b1 = np.zeros((LAYERS, 2, 3 * P), np.float32)
    b1[:, :, 0:HIDDEN] = a["L1_ffn_b1"].reshape(LAYERS, 2, HIDDEN)
    vectors = np.concatenate([a["L1_ffn_ln_g"][:, None], a["L1_ffn_ln_b"][:, None], a["L1_ffn_b2"][:, None],
                              b1.reshape(LAYERS, 6, P)], 1).transpose(0, 2, 1)
    scales = np.concatenate([f(a[n]) for n in ("L1_ffn_q_scale", "L1_ffn_k_scale")
                             for f in (lambda w: w, lambda w: np.roll(w, DIM // 2, 1))], 1)
    arrays = {
        "tr_qkv": a["L1_ffn_Wqkv"], "tr_o": a["L1_ffn_Wo"], "tr_w1": a["L1_ffn_W1"], "tr_w2": a["L1_ffn_W2"],
        "tr_vec": vectors, "tr_scales": scales,
        "x": a["L0_attn_x_q"],
        "const": const_tables(),
        "router": a["L0_ffn_router_w"].T, "moe_gate": a["L0_ffn_w_gate"], "moe_up": a["L0_ffn_w_up"], "moe_down": a["L0_ffn_w_down"],
        "ret_qkv": np.concatenate([a["L1_attn_Wq"].T, a["L1_attn_Wk"].T, a["L1_attn_Wv"].T], 1),
        "ret_g": a["L1_attn_Wg"].T, "ret_o": a["L1_attn_Wo"].T, "ret_gnorm": a["L1_attn_gnorm_w"],
        "wq": proj(a["L0_attn_w_q"]), "wk": proj(a["L0_attn_w_k"]), "wv": proj(a["L0_attn_w_v"]), "wo": a["L0_attn_w_o"],
    }
    arrays = {"in_" + n: np.ascontiguousarray(v) for n, v in arrays.items()}
    nc = bacc.Bacc("TRN2", target_bir_lowering=False, num_devices=1)
    t = {n[3:]: nc.dram_tensor(n, list(v.shape), F32, kind="ExternalInput").ap() for n, v in arrays.items()}
    out = nc.dram_tensor("result", [SEQS, TOKENS, D], F32, kind="ExternalOutput").ap()
    program(nc, t, out)
    r = run_bass_kernel_spmd(nc, [arrays], core_ids=[0])
    return r.results[0]["result"]
```

```python
from contextlib import ExitStack

import numpy as np

import concourse.bass as bass
from concourse import mybir

F32 = mybir.dt.float32
BF16 = mybir.dt.bfloat16
I32 = mybir.dt.int32
F32R = mybir.dt.float32r
TOP_BITS = -4096
ACT = mybir.ActivationFunctionType
ALU = mybir.AluOpType
AX = mybir.AxisListType

P = 128
SEQS, TOKENS, D = 16, 256, 128
BLOCKS = SEQS * TOKENS // P
BPS = TOKENS // P
LN_EPS = 1e-5
MASKED = -1e30
LN_EXP = "natural_log_exp_and_others"

CONSTS = {}
_at = 0
for _name, _n in (("ident", P), ("causal", 3 * P), ("rank", 256), ("ret_cos", 512), ("ret_sin", 512),
                  ("ret_decay", 4 * 3 * P), ("rotary", 512), ("band", 512), ("band_prev", 512)):
    CONSTS[_name] = (_at, _n)
    _at += _n
N_CONST = _at


def const_tables():
    p = np.arange(P)[:, None]
    j = np.arange(P)[None, :]
    causal = np.where(j > p, MASKED, 0.0)
    parts = {
        "ident": np.eye(P),
        "causal": np.concatenate([causal, np.zeros((P, P)), causal], 1),
    }
    parts["rank"] = np.tile(8.0 - np.arange(8), (P, 32))
    parts.update(retention_tables())
    parts["rotary"] = rotary_base()
    parts.update(band_masks())
    return np.ascontiguousarray(np.concatenate([parts[n] for n in CONSTS], 1).astype(np.float32))


class Memory:

    def __init__(self, nc, stack, phase):
        self.nc, self.stack, self.phase = nc, stack, phase

    def sb(self, name, shape, dt=F32):
        return self.stack.enter_context(self.nc.sbuf_tensor(f"{self.phase}_{name}", shape, dt))

    def banks(self):
        return [self.stack.enter_context(self.nc.psum_tensor(f"{self.phase}_bank{i}", [P, 512], F32)) for i in range(8)]

    def sem(self, name):
        return self.stack.enter_context(self.nc.semaphore(f"{self.phase}_{name}"))


def normalise(nc, phase, x1, xn_t, const, eps, x_dram=None, const_dram=None, bf16_tables=()):
    groups, per = 4, BLOCKS // 4
    with ExitStack() as stack:
        m = Memory(nc, stack, phase)
        xn = m.sb("xn", [P, BLOCKS, D])
        stats = m.sb("stats", [P, BLOCKS, 6])
        mv = m.sb("mean_var", [P, BLOCKS, 2])
        rstd = m.sb("rstd", [P, BLOCKS])
        std = m.sb("std", [P, BLOCKS])
        bank = m.banks()
        if x_dram is not None:
            x_in, const_in, eps_done = [m.sem(f"x_in{g}") for g in range(groups)], m.sem("const_in"), m.sem("eps_done")
            tables_done = m.sem("tables_done")
        stats_done, mv_done, std_done = m.sem("stats_done"), m.sem("mv_done"), m.sem("std_done")
        rstd_done, xn_done = m.sem("rstd_done"), m.sem("xn_done")
        turned, copied = m.sem("turned"), m.sem("copied")
        block = stack.enter_context(nc.Block())

        @block.sync
        def _(sp):
            if x_dram is not None:
                x_view = x_dram.rearrange("s (b p) f -> p (s b) f", p=P)
                for g in range(groups):
                    ks = slice(g * per, (g + 1) * per)
                    sp.dma_start(x1[:, ks, :], x_view[:, ks, :]).then_inc(x_in[g], 16)
                sp.dma_start(const[:, :], const_dram).then_inc(const_in, 16)

        @block.gpsimd
        def _(pool):
            if x_dram is not None:
                pool.memset(eps[:, :], LN_EPS).then_inc(eps_done, 1)

        @block.vector
        def _(dve):
            for g in range(groups):
                ks = range(g * per, (g + 1) * per)
                if x_dram is not None:
                    dve.wait_ge(x_in[g], 16)
                for k in ks:
                    last = nc.vector.bn_stats(stats[:, k, :], x1[:, k, :])
                last.then_inc(stats_done, 1)
                dve.wait_ge(stats_done, g + 1)
                for k in ks:
                    last = nc.vector.bn_aggr(mv[:, k, :], stats[:, k, :])
                last.then_inc(mv_done, 1)
                dve.wait_ge(std_done, g + 1)
                nc.vector.reciprocal(rstd[:, g * per:(g + 1) * per], std[:, g * per:(g + 1) * per]).then_inc(rstd_done, 1)
                dve.wait_ge(rstd_done, g + 1)
                for k in ks:
                    nc.vector.tensor_scalar(xn[:, k, :], x1[:, k, :], mv[:, k, 0:1], rstd[:, k:k + 1],
                                            ALU.subtract, ALU.mult).then_inc(xn_done, 1)
            if x_dram is not None:
                dve.wait_ge(const_in, 16)
            for table, name in bf16_tables:
                nc.vector.tensor_copy(table[:, :], const[:, slice_of(name)]).then_inc(tables_done, 1)

        @block.tensor
        def _(pe):
            if x_dram is not None:
                pe.wait_ge(const_in, 16)
            ident = const[:, slice_of("ident")]
            for k in range(BLOCKS):
                pe.wait_ge(xn_done, k + 1)
                last = nc.tensor.transpose(bank[k // 4][:, k % 4 * P:(k % 4 + 1) * P], xn[:, k, :], ident)
                if k % 4 == 3:
                    last.then_inc(turned, 1)

        @block.scalar
        def _(act):
            if x_dram is not None:
                act.wait_ge(eps_done, 1)
            for g in range(groups):
                act.wait_ge(mv_done, g + 1)
                nc.scalar.activation(std[:, g * per:(g + 1) * per], mv[:, g * per:(g + 1) * per, 1],
                                     ACT.Sqrt, bias=eps[:, 0:1]).then_inc(std_done, 1)
            for q in range(8):
                act.wait_ge(turned, q + 1)
                nc.scalar.activation(xn_t[:, q * 512:(q + 1) * 512], bank[q][:, :], ACT.Copy).then_inc(copied, 1)


def product_of_halves(nc, out, w_high, w_low, x_high, x_low, first=True, final=True):
    nc.tensor.matmul(out, w_high, x_high, start=first, stop=False)
    nc.tensor.matmul(out, w_high, x_low, start=False, stop=False)
    return nc.tensor.matmul(out, w_low, x_high, start=False, stop=final)


def slice_of(name):
    at, n = CONSTS[name]
    return slice(at, at + n)


A_HEADS, A_DIM = 16, 64
A_CHUNKS = A_HEADS // 2
A_WIDE = A_HEADS * A_DIM


def causal_attention(nc, wq_dram, wk_dram, wv_dram, wo_dram, x1, xn_t, ident_f, ident_b, causal_b,
                     for_later):
    with ExitStack() as stack:
        m = Memory(nc, stack, "att")
        wq, wk, wv = (m.sb(n, [P, A_WIDE]) for n in ("wq", "wk", "wv"))
        wo = m.sb("wo", [P, A_CHUNKS, D])
        xs = m.sb("xs", [P, TOKENS])
        q_even = m.sb("q_even", [P, A_CHUNKS, TOKENS])
        q_odd = m.sb("q_odd", [P, A_CHUNKS, TOKENS])
        k_t = m.sb("k_t", [P, A_CHUNKS, TOKENS])
        v = m.sb("v", [P, BPS, A_WIDE])
        probs = m.sb("probs", [P, 4, 3 * P])
        probs_t = m.sb("probs_t", [P, 2, 3 * P])
        neg_max = m.sb("neg_max", [P, A_HEADS, 2])
        sums = m.sb("sums", [P, A_HEADS, 2])
        inv = m.sb("inv", [P, A_HEADS, 2])
        o_t = m.sb("o_t", [P, A_CHUNKS, TOKENS])
        bank = m.banks()
        proj_bank, score_bank, turn_bank, out_bank = bank[0:2], bank[2:4], bank[4:6], bank[6:8]
        w_in, zeros_done = m.sem("w_in"), m.sem("zeros_done")
        xs_ready = m.sem("xs_ready")
        qk_psum, v_psum, wo_psum = m.sem("qk_psum"), m.sem("v_psum"), m.sem("wo_psum")
        qk_act, qk_dve, v_act, v_dve = m.sem("qk_act"), m.sem("qk_dve"), m.sem("v_act"), m.sem("v_dve")
        scores_ready, max_ready, exp_done = m.sem("scores_ready"), m.sem("max_ready"), m.sem("exp_done")
        inv_done, probs_ready = m.sem("inv_done"), m.sem("probs_ready")
        turned, turned_sb, out_psum, out_sb = m.sem("turned"), m.sem("turned_sb"), m.sem("out_psum"), m.sem("out_sb")
        added, later_in = m.sem("added"), m.sem("later_in")
        block = stack.enter_context(nc.Block())
        H, C = A_HEADS, A_CHUNKS
        WO_AT = 0

        @block.sync
        def _(sp):
            for w, dram in ((wq, wq_dram), (wk, wk_dram), (wv, wv_dram)):
                sp.dma_start(w[:, :], dram).then_inc(w_in, 16)
            sp.dma_start(wo[:, :, :], wo_dram.rearrange("(c p) f -> p c f", p=P)).then_inc(w_in, 16)
            for i, (tile, dram) in enumerate(for_later):
                sp.dma_start(tile, dram).then_inc(later_in, 16)
            sp.wait_ge(later_in, 16 * len(for_later))

        @block.gpsimd
        def _(pool):
            nc.gpsimd.memset(q_even[A_DIM:P, :, :], 0.0).then_inc(zeros_done, 1)
            pool.wait_ge(zeros_done, 1)
            nc.gpsimd.memset(q_odd[0:A_DIM, :, :], 0.0).then_inc(zeros_done, 1)
            pool.wait_ge(zeros_done, 2)
            nc.gpsimd.tensor_copy(xs[:, :], xn_t[:, 0:TOKENS]).then_inc(xs_ready, 1)
            with pool.Fori(1, SEQS) as s:
                pool.wait_ge(v_psum, s * 4)
                nc.gpsimd.tensor_copy(xs[:, :], xn_t[:, bass.ds(s * TOKENS, TOKENS)]).then_inc(xs_ready, 1)

        @block.tensor
        def _(pe):
            def project_qk(n, c, first=False):
                if c >= 2:
                    pe.wait_ge(qk_act if c % 2 == 0 else qk_dve, n * (C // 2) + c // 2)
                elif not first:
                    pe.wait_ge(v_act if c % 2 == 0 else v_dve, n * 2)
                    pe.wait_ge(added, n * BPS)
                for i, w in enumerate((wq, wk)):
                    last = nc.tensor.matmul(proj_bank[c % 2][:, i * TOKENS:(i + 1) * TOKENS],
                                            w[:, c * P:(c + 1) * P], xs[:, :], start=True, stop=True)
                last.then_inc(qk_psum, 1)

            def project_v(n, u):
                if u < 2:
                    pe.wait_ge(qk_act if u == 0 else qk_dve, (n + 1) * (C // 2))
                else:
                    pe.wait_ge(v_act if u % 2 == 0 else v_dve, n * 2 + u // 2)
                last = nc.tensor.matmul(proj_bank[u % 2][:, :], xs[:, u // 2 * P:(u // 2 + 1) * P],
                                        wv[:, u % 2 * 512:(u % 2 + 1) * 512], start=True, stop=True)
                last.then_inc(v_psum, 1)

            def job(s, has_before, ahead):
                for t in range(H + 3):
                    if t < H:
                        c = t // 2
                        if t % 2 == 0:
                            pe.wait_ge(qk_act if c % 2 == 0 else qk_dve, s * (C // 2) + c // 2 + 1)
                        pe.wait_ge(exp_done, s * H + t)
                        sc, q = score_bank[t % 2], (q_even, q_odd)[t % 2]
                        nc.tensor.matmul(sc[:, 0:3 * P], ident_b[:, :], causal_b[:, :], start=True, stop=False)
                        nc.tensor.matmul(sc[:, 0:P], q[:, c, 0:P], k_t[:, c, 0:P], start=False, stop=False)
                        nc.tensor.matmul(sc[:, P:3 * P], q[:, c, P:TOKENS], k_t[:, c, :],
                                         start=False, stop=True).then_inc(scores_ready, 1)
                    elif ahead:
                        for c in range(3 * (t - H), min(3 * (t - H) + 3, C)):
                            if t == H and c == 0:
                                pe.wait_ge(xs_ready, s + 2)
                            project_qk(s + 1, c)
                    h = t - 2
                    if 0 <= h < H:
                        if h == WO_AT and has_before:
                            project_out(s - 1, 2 * (s + 1))
                        pe.wait_ge(probs_ready, s * H + h + 1)
                        pe.wait_ge(turned_sb, s * H + h)
                        for i, at in enumerate((0, P, 2 * P)):
                            last = nc.tensor.transpose(turn_bank[h % 2][:, i * P:(i + 1) * P],
                                                       probs[:, h % 4, at:at + P], ident_f)
                        last.then_inc(turned, 1)
                    h = t - 3
                    if h >= 0:
                        if h == 0:
                            pe.wait_ge(v_act, 2 * (s + 1))
                            pe.wait_ge(v_dve, 2 * (s + 1))
                        if h % 2 == 0:
                            pe.wait_ge(out_sb, s * C + h // 2 + 1)
                        pe.wait_ge(turned_sb, s * H + h + 2)
                        rows = slice(h % 2 * A_DIM, (h % 2 + 1) * A_DIM)
                        dst = out_bank[h // 2 % 2][rows, 0:TOKENS]
                        nc.tensor.matmul(dst, v[:, 0, h * A_DIM:(h + 1) * A_DIM], probs_t[:, h % 2, 0:TOKENS],
                                         start=True, stop=False)
                        nc.tensor.matmul(out_bank[h // 2 % 2][rows, P:TOKENS], v[:, 1, h * A_DIM:(h + 1) * A_DIM],
                                         probs_t[:, h % 2, TOKENS:3 * P], start=False, stop=True).then_inc(out_psum, 1)
                if ahead:
                    for u in range(4):
                        project_v(s + 1, u)

            def project_out(s, v_copied):
                pe.wait_ge(out_sb, (s + 1) * C + 2)
                for b in range(BPS):
                    pe.wait_ge((v_act, v_dve)[b], v_copied)
                    for c in range(C):
                        last = nc.tensor.matmul(proj_bank[b][:, 0:D], o_t[:, c, b * P:(b + 1) * P], wo[:, c, :],
                                                start=c == 0, stop=c == C - 1)
                    last.then_inc(wo_psum, 1)

            pe.wait_ge(w_in, 64)
            pe.wait_ge(xs_ready, 1)
            for c in range(C):
                project_qk(0, c, first=True)
            for u in range(4):
                project_v(0, u)
            pe.wait_ge(zeros_done, 2)
            job(0, False, True)
            with pe.Fori(1, SEQS - 1) as s:
                job(s, True, True)
            job(SEQS - 1, True, False)
            project_out(SEQS - 1, 2 * SEQS)

        def copy_qk(copy, c, done):
            src = proj_bank[c % 2]
            copy(q_even[0:A_DIM, c, :], src[0:A_DIM, 0:TOKENS], A_DIM ** -0.5)
            copy(q_odd[A_DIM:P, c, :], src[A_DIM:P, 0:TOKENS], A_DIM ** -0.5)
            copy(k_t[:, c, :], src[:, TOKENS:2 * TOKENS], 1.0).then_inc(done, 1)

        @block.scalar
        def _(act):
            def copy(out, src, scale):
                return nc.scalar.activation(out, src, ACT.Copy, scale=scale)

            def job(s, ahead):
                for t in range(H + 3):
                    if t < H:
                        act.wait_ge(max_ready, s * H + t + 1)
                        if t >= 4:
                            act.wait_ge(turned, s * H + t - 3)
                        for i, (a, e) in enumerate(((0, P), (P, 3 * P))):
                            last = nc.scalar.activation(probs[:, t % 4, a:e], score_bank[t % 2][:, a:e], ACT.Exp,
                                                        bias=neg_max[:, t, i:i + 1], accum_out=sums[:, t, i:i + 1])
                        last.then_inc(exp_done, 1)
                    elif ahead:
                        for c in range(3 * (t - H), min(3 * (t - H) + 3, C)):
                            if c % 2 == 0:
                                act.wait_ge(qk_psum, (s + 1) * C + c + 1)
                                copy_qk(copy, c, qk_act)
                    h = t - 2
                    if 0 <= h < H:
                        act.wait_ge(turned, s * H + h + 1)
                        if h >= 2:
                            act.wait_ge(out_psum, s * H + h - 1)
                        nc.scalar.activation(probs_t[:, h % 2, :], turn_bank[h % 2][:, 0:3 * P], ACT.Copy).then_inc(turned_sb, 1)
                if ahead:
                    copy_v(s + 1)

            def copy_v(n):
                for u in (0, 2):
                    act.wait_ge(v_psum, n * 4 + u + 1)
                    nc.scalar.activation(v[:, u // 2, 0:512], proj_bank[0][:, :], ACT.Copy).then_inc(v_act, 1)

            act.sem_inc(exp_done, 1)
            act.sem_inc(turned_sb, 1)
            for c in range(0, C, 2):
                act.wait_ge(qk_psum, c + 1)
                copy_qk(copy, c, qk_act)
            copy_v(0)
            with act.Fori(0, SEQS - 1) as s:
                job(s, True)
            job(SEQS - 1, False)

        @block.vector
        def _(dve):
            def copy(out, src, scale):
                return nc.vector.tensor_scalar(out, src, scale, None, ALU.mult)

            def job(s, has_before, ahead):
                for t in range(H + 4):
                    if t < H:
                        dve.wait_ge(scores_ready, s * H + t + 1)
                        for i, (a, e) in enumerate(((0, P), (P, 3 * P))):
                            last = nc.vector.tensor_reduce(neg_max[:, t, i:i + 1], score_bank[t % 2][:, a:e], AX.X, ALU.max,
                                                           negate=True)
                        last.then_inc(max_ready, 1)
                    if t == WO_AT + 3 and has_before:
                        add_outputs(s - 1)
                    h = t - 1
                    if 0 <= h < H:
                        dve.wait_ge(exp_done, s * H + h + 2)
                        nc.vector.reciprocal(inv[:, h, :], sums[:, h, :]).then_inc(inv_done, 1)
                        dve.wait_ge(inv_done, s * H + h + 1)
                        for i, (a, e) in enumerate(((0, P), (P, 3 * P))):
                            last = nc.vector.tensor_scalar(probs[:, h % 4, a:e], probs[:, h % 4, a:e], inv[:, h, i:i + 1],
                                                           None, ALU.mult)
                        last.then_inc(probs_ready, 1)
                    if ahead and t >= H:
                        for c in range(3 * (t - H), min(3 * (t - H) + 3, C)):
                            if c % 2 == 1:
                                dve.wait_ge(qk_psum, (s + 1) * C + c + 1)
                                copy_qk(copy, c, qk_dve)
                    h = t - 4
                    if h >= 0 and h % 2 == 1:
                        dve.wait_ge(out_psum, s * H + h + 1)
                        nc.vector.tensor_copy(o_t[:, h // 2, :], out_bank[h // 2 % 2][:, 0:TOKENS]).then_inc(out_sb, 1)
                if ahead:
                    copy_v(s + 1)

            def add_outputs(s):
                for b in range(BPS):
                    dve.wait_ge(wo_psum, BPS * s + b + 1)
                    dst = x1[:, bass.ds(s * BPS + b, 1), :]
                    nc.vector.tensor_tensor(dst, proj_bank[b][:, 0:D].rearrange("p (o f) -> p o f", o=1), dst, ALU.add).then_inc(added, 1)

            def copy_v(n):
                for u in (1, 3):
                    dve.wait_ge(v_psum, n * 4 + u + 1)
                    nc.vector.tensor_copy(v[:, u // 2, 512:1024], proj_bank[1][:, :]).then_inc(v_dve, 1)

            dve.sem_inc(out_sb, 2)
            dve.sem_inc(added, BPS)
            for c in range(1, C, 2):
                dve.wait_ge(qk_psum, c + 1)
                copy_qk(copy, c, qk_dve)
            copy_v(0)
            job(0, False, True)
            with dve.Fori(1, SEQS - 1) as s:
                job(s, True, True)
            job(SEQS - 1, True, False)
            add_outputs(SEQS - 1)


EXPERTS, D_FF = 8, 512
FC = D_FF // P


def mixture_of_experts(nc, router_dram, w_drams, x1, xn_t, const, staged, wd):
    NB, E = BLOCKS, EXPERTS
    TC = 4
    CHUNKS = NB // TC
    with ExitStack() as stack:
        m = Memory(nc, stack, "moe")
        rw = m.sb("router_w", [P, E])
        small = {n: m.sb(n, [P, NB, E]) for n in ("logit", "below", "ranked", "first", "rest", "ranked2", "second", "chosen",
                                                 "expo", "picked", "weight")}
        top = {n: m.sb(n, [P, NB]) for n in ("max1", "rank1", "max2", "rank2", "total", "inv")}
        w_top = m.sb("w_top", [P, 2, 2, D_FF], I32)
        w_high, w_low = m.sb("w_high", [P, 2, E, D_FF], F32R), m.sb("w_low", [P, 2, E, D_FF], F32R)
        xs_top = m.sb("xs_top", [P, TC * P], I32)
        xs_high, xs_low = m.sb("xs_high", [P, TC * P], F32R), m.sb("xs_low", [P, TC * P], F32R)
        gate = m.sb("gate", [P, 2, TC * P])
        hid = m.sb("hidden", [P, 2, FC, TC * P])
        bank = m.banks()
        gate_bank, up_bank, down_bank, route_bank = bank[0:2], bank[2:4], bank[4:6], bank[6]
        rw_in, logits_psum, route, expo_done = m.sem("rw_in"), m.sem("logits_psum"), m.sem("route"), m.sem("expo_done")
        xs_ready, gate_psum, up_psum, gate_done = m.sem("xs_ready"), m.sem("gate_psum"), m.sem("up_psum"), m.sem("gate_done")
        hid_done, down_psum, added = m.sem("hid_done"), m.sem("down_psum"), m.sem("added")
        w_top_done, w_low_done, w_high_done = m.sem("w_top_done"), m.sem("w_low_done"), m.sem("w_high_done")
        xs_top_done = m.sem("xs_top_done")
        staged_in = [[m.sem(f"staged_in{place}{side}") for side in range(2)] for place in range(2)]
        block = stack.enter_context(nc.Block())

        @block.sync
        def _(sp):
            sp.dma_start(rw[:, :], router_dram).then_inc(rw_in, 16)
            for e in range(2, E):
                for side in range(2):
                    sp.wait_ge(w_low_done, 2 * (e - 2) + side + 1)
                    sp.dma_start(staged[:, e % 2, side, :], w_drams[side][e]).then_inc(staged_in[e % 2][side], 16)

        @block.gpsimd
        def _(pool):
            def halves_of_xs(pool, n):
                pool.wait_ge(xs_top_done, n + 1)
                nc.gpsimd.tensor_tensor(xs_low[:, :], xn_t[:, bass.ds(n * (TC * P), TC * P)], xs_top[:, :].bitcast(F32), ALU.subtract
                                        ).then_inc(xs_ready, 1)
                nc.gpsimd.tensor_copy(xs_high[:, :], xs_top[:, :].bitcast(F32)).then_inc(xs_ready, 1)

            for e in range(E):
                for side in range(2):
                    pool.wait_ge(w_top_done, 2 * e + side + 1)
                    nc.gpsimd.tensor_tensor(w_low[:, side, e, :], staged[:, e % 2, side, :], w_top[:, e % 2, side, :].bitcast(F32), ALU.subtract
                                            ).then_inc(w_low_done, 1)
                if e == 0:
                    halves_of_xs(pool, 0)
            with pool.Fori(1, CHUNKS) as n:
                pool.wait_ge(up_psum, n * E * FC)
                halves_of_xs(pool, n)

        @block.tensor
        def _(pe):
            def down(n, e):
                pe.wait_ge(hid_done, (n * E + e + 1) * FC)
                pe.wait_ge(added, (n * E + e - 1) * TC + 2 * TC)
                for b in range(TC):
                    for c in range(FC):
                        last = nc.tensor.matmul(down_bank[e % 2][:, b * P:(b + 1) * P], hid[:, e % 2, c, b * P:(b + 1) * P],
                                                wd[:, e, c, :], start=c == 0, stop=c == FC - 1)
                last.then_inc(down_psum, 1)

            pe.wait_ge(rw_in, 16)
            for k in range(NB):
                last = nc.tensor.matmul(route_bank[:, k * E:(k + 1) * E], xn_t[:, k * P:(k + 1) * P], rw[:, :],
                                        start=True, stop=True)
            last.then_inc(logits_psum, 1)
            with pe.Fori(0, CHUNKS) as n:
                pe.wait_ge(xs_ready, 2 * n + 2)
                for e in range(E):
                    pe.wait_ge(w_high_done, 2 * e + 2)
                    for c in range(FC):
                        i = e * FC + c
                        ff = slice(c * P, (c + 1) * P)
                        pe.wait_ge(gate_done, n * (E * FC) + i + 1)
                        product_of_halves(nc, gate_bank[i % 2][:, :], w_high[:, 0, e, ff], w_low[:, 0, e, ff],
                                          xs_high[:, :], xs_low[:, :]).then_inc(gate_psum, 1)
                        if i >= 2:
                            pe.wait_ge(hid_done, n * (E * FC) + i - 1)
                        product_of_halves(nc, up_bank[i % 2][:, :], w_high[:, 1, e, ff], w_low[:, 1, e, ff],
                                          xs_high[:, :], xs_low[:, :]).then_inc(up_psum, 1)
                        if c == 1 and e > 0:
                            down(n, e - 1)
                down(n, E - 1)

        @block.scalar
        def _(act):
            for e in range(E):
                for side in range(2):
                    act.wait_ge(w_low_done, 2 * e + side + 1)
                    nc.scalar.activation(w_high[:, side, e, :], w_top[:, e % 2, side, :].bitcast(F32), ACT.Copy).then_inc(w_high_done, 1)
            act.wait_ge(route, 2)
            nc.scalar.activation(small["expo"][:, :, :], small["below"][:, :, :], ACT.Exp).then_inc(expo_done, 1)
            act.sem_inc(gate_done, 2)
            with act.Fori(0, CHUNKS) as n:
                for i in range(E * FC):
                    act.wait_ge(gate_psum, n * (E * FC) + i + 1)
                    if i >= 2:
                        act.wait_ge(hid_done, n * (E * FC) + i - 1)
                    nc.scalar.activation(gate[:, i % 2, :], gate_bank[i % 2][:, :], ACT.Silu).then_inc(gate_done, 1)

        @block.vector
        def _(dve):
            s, v = small, nc.vector

            def over_experts(t):
                return t[:, :].unsqueeze(2).broadcast_to([P, NB, E])

            v.tensor_scalar(xs_top[:, :], xn_t[:, 0:TC * P].bitcast(I32), TOP_BITS, None, ALU.bitwise_and).then_inc(xs_top_done, 1)
            for e in range(E):
                for side in range(2):
                    if e >= 2:
                        dve.wait_ge(staged_in[e % 2][side], 16 * (e // 2))
                        dve.wait_ge(w_high_done, 2 * (e - 2) + side + 1)
                    v.tensor_scalar(w_top[:, e % 2, side, :], staged[:, e % 2, side, :].bitcast(I32), TOP_BITS, None, ALU.bitwise_and
                                    ).then_inc(w_top_done, 1)
            rank = const[:, slice_of("rank")].rearrange("p (k e) -> p k e", e=E)
            logits = route_bank[:, 0:NB * E].rearrange("p (k e) -> p k e", e=E)
            dve.wait_ge(logits_psum, 1)
            v.tensor_reduce(top["max1"][:, :], logits, AX.X, ALU.max).then_inc(route, 1)
            dve.wait_ge(route, 1)
            v.tensor_tensor(s["below"][:, :, :], logits, over_experts(top["max1"]), ALU.subtract).then_inc(route, 1)
            dve.wait_ge(route, 2)
            v.scalar_tensor_tensor(s["ranked"][:, :, :], s["below"][:, :, :], 0.0, rank, ALU.is_ge, ALU.mult).then_inc(route, 1)
            dve.wait_ge(route, 3)
            v.tensor_reduce(top["rank1"][:, :], s["ranked"][:, :, :], AX.X, ALU.max).then_inc(route, 1)
            dve.wait_ge(route, 4)
            v.tensor_tensor(s["first"][:, :, :], s["ranked"][:, :, :], over_experts(top["rank1"]), ALU.is_equal).then_inc(route, 1)
            dve.wait_ge(route, 5)
            v.scalar_tensor_tensor(s["rest"][:, :, :], s["first"][:, :, :], MASKED, s["below"][:, :, :], ALU.mult, ALU.add).then_inc(route, 1)
            dve.wait_ge(route, 6)
            v.tensor_reduce(top["max2"][:, :], s["rest"][:, :, :], AX.X, ALU.max).then_inc(route, 1)
            dve.wait_ge(route, 7)
            v.tensor_tensor(s["chosen"][:, :, :], s["rest"][:, :, :], over_experts(top["max2"]), ALU.is_equal).then_inc(route, 1)
            dve.wait_ge(route, 8)
            v.tensor_tensor(s["ranked2"][:, :, :], s["chosen"][:, :, :], rank, ALU.mult).then_inc(route, 1)
            dve.wait_ge(route, 9)
            v.tensor_reduce(top["rank2"][:, :], s["ranked2"][:, :, :], AX.X, ALU.max).then_inc(route, 1)
            dve.wait_ge(route, 10)
            v.tensor_tensor(s["second"][:, :, :], s["ranked2"][:, :, :], over_experts(top["rank2"]), ALU.is_equal).then_inc(route, 1)
            dve.wait_ge(route, 11)
            v.tensor_tensor(s["picked"][:, :, :], s["first"][:, :, :], s["second"][:, :, :], ALU.add).then_inc(route, 1)
            dve.wait_ge(route, 12)
            dve.wait_ge(expo_done, 1)
            v.tensor_tensor(s["picked"][:, :, :], s["picked"][:, :, :], s["expo"][:, :, :], ALU.mult).then_inc(route, 1)
            dve.wait_ge(route, 13)
            v.tensor_reduce(top["total"][:, :], s["picked"][:, :, :], AX.X, ALU.add).then_inc(route, 1)
            dve.wait_ge(route, 14)
            v.reciprocal(top["inv"][:, :], top["total"][:, :]).then_inc(route, 1)
            dve.wait_ge(route, 15)
            v.tensor_tensor(s["weight"][:, :, :], s["picked"][:, :, :], over_experts(top["inv"]), ALU.mult).then_inc(route, 1)
            dve.wait_ge(route, 16)

            def add_expert(n, e):
                dve.wait_ge(down_psum, n * E + e + 1)
                dve.wait_ge(added, (n * E + e) * TC + TC)
                for b in range(TC):
                    dst = x1[:, bass.ds(n * TC + b, 1), :].rearrange("p o f -> p (o f)")
                    w = s["weight"][:, bass.ds(n * TC + b, 1), e]
                    v.scalar_tensor_tensor(dst, down_bank[e % 2][:, b * P:(b + 1) * P], w, dst, ALU.mult, ALU.add).then_inc(added, 1)

            dve.sem_inc(added, TC)

            def chunk(n, has_next):
                for e in range(E):
                    if e == E - 1 and has_next:
                        dve.wait_ge(xs_ready, 2 * n + 2)
                        v.tensor_scalar(xs_top[:, :], xn_t[:, bass.ds((n + 1) * (TC * P), TC * P)].bitcast(I32), TOP_BITS, None,
                                        ALU.bitwise_and).then_inc(xs_top_done, 1)
                    for c in range(FC):
                        i = e * FC + c
                        dve.wait_ge(gate_done, n * (E * FC) + i + 3)
                        dve.wait_ge(up_psum, n * (E * FC) + i + 1)
                        if e >= 2 and c == 0:
                            dve.wait_ge(down_psum, n * E + e - 1)
                        v.tensor_tensor(hid[:, e % 2, c, :], gate[:, i % 2, :], up_bank[i % 2][:, :], ALU.mult).then_inc(hid_done, 1)
                        if c == 2 and e > 0:
                            add_expert(n, e - 1)
                add_expert(n, E - 1)

            with dve.Fori(0, CHUNKS - 1) as n:
                chunk(n, True)
            chunk(CHUNKS - 1, False)


R_HEADS, R_DK, R_DV = 4, 32, 64


def retention_tables():
    half = R_DK // 2
    inv_freq = (1.0 / np.float32(10000.0) ** (np.arange(0, R_DK, 2, dtype=np.float32) / R_DK)).astype(np.float32)
    freqs = np.arange(TOKENS, dtype=np.float32)[:, None] * inv_freq[None, :]
    cos, sin = np.cos(freqs), np.sin(freqs)
    c = np.concatenate([cos, cos], 1)
    s = np.concatenate([-sin, sin], 1)
    scale = np.repeat([R_DK ** -0.5, 1.0], R_HEADS)
    wide = {}
    for name, t in (("ret_cos", c), ("ret_sin", s)):
        w = scale[None, :, None] * t[:, None, :]
        wide[name] = w.reshape(BPS, P, -1).transpose(1, 0, 2).reshape(P, -1)
    gamma = 1.0 - 2.0 ** (-5.0 - np.arange(R_HEADS))
    j, i = np.arange(P)[:, None], np.arange(TOKENS)[None, :]
    d0 = np.where(i >= j, gamma[:, None, None] ** np.maximum(i - j, 0), 0.0)
    d1 = d0[:, :, 0:P]
    decay = np.concatenate([d0, d1], 2)
    wide["ret_decay"] = decay.transpose(1, 0, 2).reshape(P, -1)
    return wide


def retention(nc, wqkv_dram, wg_dram, wo_dram, gnorm_dram, x1, xn_t, const, eps):
    V_WIDE = R_HEADS * R_DV
    with ExitStack() as stack:
        m = Memory(nc, stack, "ret")
        wqkv = m.sb("wqkv", [P, 512])
        wg = m.sb("wg", [P, V_WIDE])
        wo = m.sb("wo", [P, 2, D])
        gnorm = m.sb("gnorm", [P, R_DV])
        gate = m.sb("gate", [P, BLOCKS, V_WIDE])
        xs = m.sb("xs", [P, TOKENS])
        raw = m.sb("raw", [P, BPS, 256])
        part1 = m.sb("part1", [P, BPS, 256])
        part2 = m.sb("part2", [P, BPS, 256])
        rot = m.sb("rot", [P, BPS, 256])
        v = m.sb("v", [P, 2, BPS, V_WIDE])
        q_t = m.sb("q_t", [P, R_HEADS, TOKENS])
        k_t = m.sb("k_t", [P, TOKENS])
        probs_t = m.sb("probs_t", [P, R_HEADS, 3 * P])
        o_raw = m.sb("o_raw", [P, BPS * R_HEADS, R_DV])
        sq = m.sb("sq", [P, BPS * R_HEADS, R_DV])
        ms = m.sb("ms", [P, BPS * R_HEADS])
        ln_ms = m.sb("ln_ms", [P, BPS * R_HEADS])
        rstd = m.sb("rstd", [P, BPS * R_HEADS])
        o_n = m.sb("o_n", [P, BPS * R_HEADS, R_DV])
        gated = m.sb("gated", [P, BPS * R_HEADS, R_DV])
        o_t = m.sb("o_t", [P, BPS, 2, P])
        bank = m.banks()
        w_in, zeroed = m.sem("w_in"), m.sem("zeroed")
        gate_psum, gate_done, xs_ready = m.sem("gate_psum"), m.sem("gate_done"), m.sem("xs_ready")
        qkv_psum, raw_ready, rot_steps, rot_ready = m.sem("qkv_psum"), m.sem("raw_ready"), m.sem("rot_steps"), m.sem("rot_ready")
        part1_done = m.sem("part1_done")
        qk_turned, qk_sb, scores_ready, decayed = m.sem("qk_turned"), m.sem("qk_sb"), m.sem("scores_ready"), m.sem("decayed")
        out_psum, o_copied, squared, ms_done, ln_done, rstd_done = (m.sem(n) for n in (
            "out_psum", "o_copied", "squared", "ms_done", "ln_done", "rstd_done"))
        norm_steps, gated_done, o_turned, o_sb, wo_psum, added = (m.sem(n) for n in (
            "norm_steps", "gated_done", "o_turned", "o_sb", "wo_psum", "added"))
        block = stack.enter_context(nc.Block())
        NBH = BPS * R_HEADS

        def steps(eng, start, step, finish):
            start()
            step(0, 0, False, True)
            with eng.Fori(0, SEQS // 2 - 1) as i:
                step(i * 2 + 1, 1, True, True)
                step(i * 2 + 2, 0, True, True)
            step(SEQS - 1, 1, True, False)
            finish(SEQS - 1)

        @block.sync
        def _(sp):
            sp.dma_start(wqkv[:, :], wqkv_dram).then_inc(w_in, 16)
            sp.dma_start(wg[:, :], wg_dram).then_inc(w_in, 16)
            sp.dma_start(wo[:, :, :], wo_dram.rearrange("(c p) f -> p c f", p=P)).then_inc(w_in, 16)
            sp.dma_start(gnorm[:, :], gnorm_dram.partition_broadcast(P)).then_inc(w_in, 16)

        @block.gpsimd
        def _(pool):
            nc.gpsimd.memset(q_t[:, :, :], 0.0).then_inc(zeroed, 1)
            cos = const[:, slice_of("ret_cos")].rearrange("p (b n) -> p b n", b=BPS)

            def job(s):
                pool.wait_ge(qkv_psum, s * BPS + 1)
                nc.gpsimd.tensor_copy(xs[:, :], xn_t[:, bass.ds(s * TOKENS, TOKENS)]).then_inc(xs_ready, 1)
                pool.wait_ge(raw_ready, BPS * (s + 1))
                nc.gpsimd.tensor_tensor(part1[:, :, :], raw[:, :, :], cos, ALU.mult).then_inc(part1_done, 1)

            with pool.Fori(0, SEQS) as s:
                job(s)

        @block.tensor
        def _(pe):
            ident = const[:, slice_of("ident")]
            pe.wait_ge(w_in, 64)
            for k in range(BLOCKS):
                if k >= 4 and k % 2 == 0:
                    pe.wait_ge(gate_done, k // 2 - 1)
                last = nc.tensor.matmul(bank[k // 2 % 2][:, k % 2 * V_WIDE:(k % 2 + 1) * V_WIDE],
                                        xn_t[:, k * P:(k + 1) * P], wg[:, :], start=True, stop=True)
                if k % 2 == 1:
                    last.then_inc(gate_psum, 1)
            pe.wait_ge(gate_done, BLOCKS // 2)
            pe.sem_inc(qkv_psum, 1)
            pe.sem_inc(added, BPS)

            def project(s):
                pe.wait_ge(xs_ready, s + 1)
                for b in range(BPS):
                    last = nc.tensor.matmul(bank[b][:, :], xs[:, b * P:(b + 1) * P], wqkv[:, :], start=True, stop=True)
                    last.then_inc(qkv_psum, 1)

            def turn_outputs(s):
                pe.wait_ge(gated_done, s + 1)
                for b in range(BPS):
                    for c in range(2):
                        at = (b * 2 + c) * P
                        last = nc.tensor.transpose(bank[2][:, at:at + P],
                                                   gated[:, b * R_HEADS + 2 * c:b * R_HEADS + 2 * c + 2, :].rearrange("p h d -> p (h d)"), ident)
                last.then_inc(o_turned, 1)

            def project_out(s):
                pe.wait_ge(o_sb, s + 1)
                for b in range(BPS):
                    for c in range(2):
                        last = nc.tensor.matmul(bank[3 + b][:, 0:D], o_t[:, b, c, :], wo[:, c, :], start=c == 0, stop=c == 1)
                    last.then_inc(wo_psum, 1)

            def step(s, place, has_before, has_next):
                pe.wait_ge(rot_ready, s + 1)
                for half in range(2):
                    for b in range(BPS):
                        at = (half * BPS + b) * P
                        last = nc.tensor.transpose(bank[2][:, at:at + P], rot[:, b, half * P:(half + 1) * P], ident)
                last.then_inc(qk_turned, 1)
                if has_next:
                    project(s + 1)
                pe.wait_ge(qk_sb, s + 1)
                if has_before:
                    pe.wait_ge(added, BPS * s)
                for h in range(R_HEADS):
                    sc = bank[3 + h]
                    nc.tensor.matmul(sc[:, 0:TOKENS], k_t[:, 0:P], q_t[:, h, :], start=True, stop=True)
                    nc.tensor.matmul(sc[:, TOKENS:3 * P], k_t[:, P:TOKENS], q_t[:, h, P:TOKENS],
                                     start=True, stop=True).then_inc(scores_ready, 1)
                if has_before:
                    turn_outputs(s - 1)
                for h in range(R_HEADS):
                    pe.wait_ge(decayed, s * R_HEADS + h + 1)
                    vs = slice(h * R_DV, (h + 1) * R_DV)
                    o0 = bank[7][:, vs]
                    o1 = bank[7][:, V_WIDE + h * R_DV:V_WIDE + (h + 1) * R_DV]
                    nc.tensor.matmul(o0, probs_t[:, h, 0:P], v[:, place, 0, vs], start=True, stop=True)
                    nc.tensor.matmul(o1, probs_t[:, h, P:TOKENS], v[:, place, 0, vs], start=True, stop=False)
                    last = nc.tensor.matmul(o1, probs_t[:, h, TOKENS:3 * P], v[:, place, 1, vs], start=False, stop=True)
                last.then_inc(out_psum, 1)
                if has_before:
                    project_out(s - 1)

            def finish(s):
                turn_outputs(s)
                project_out(s)

            steps(pe, lambda: project(0), step, finish)

        @block.scalar
        def _(act):
            for k in range(BLOCKS // 2):
                act.wait_ge(gate_psum, k + 1)
                nc.scalar.activation(gate[:, 2 * k:2 * k + 2, :], bank[k % 2][:, :].rearrange("p (b n) -> p b n", b=2),
                                     ACT.Silu).then_inc(gate_done, 1)
            nc.scalar.preload_act_table_set(LN_EXP)

            def copy_projections(s, place):
                for b in range(BPS):
                    act.wait_ge(qkv_psum, s * BPS + b + 2)
                    nc.scalar.activation(raw[:, b, :], bank[b][:, 0:256], ACT.Copy)
                    nc.scalar.activation(v[:, place, b, :], bank[b][:, 256:512], ACT.Copy).then_inc(raw_ready, 1)

            def norm(s):
                act.wait_ge(ms_done, s + 1)
                nc.scalar.activation(ln_ms[:, :], ms[:, :], ACT.Ln, scale=1.0 / R_DV, bias=eps[:, 0:1]).then_inc(ln_done, 1)
                act.wait_ge(ln_done, s + 1)
                nc.scalar.activation(rstd[:, :], ln_ms[:, :], ACT.Exp, scale=-0.5).then_inc(rstd_done, 1)

            def copy_turned_outputs(s):
                act.wait_ge(o_turned, s + 1)
                nc.scalar.activation(o_t[:, :, :, :], bank[2][:, :].rearrange("p (b c n) -> p b c n", b=BPS, c=2), ACT.Copy).then_inc(o_sb, 1)

            def step(s, place, has_before, has_next):
                act.wait_ge(qk_turned, s + 1)
                for h in range(R_HEADS):
                    rows = slice(h * R_DK, (h + 1) * R_DK)
                    nc.scalar.activation(q_t[rows, h, :], bank[2][rows, 0:TOKENS], ACT.Copy)
                nc.scalar.activation(k_t[:, :], bank[2][:, TOKENS:2 * TOKENS], ACT.Copy).then_inc(qk_sb, 1)
                if has_before:
                    norm(s - 1)
                if has_next:
                    copy_projections(s + 1, 1 - place)
                if has_before:
                    copy_turned_outputs(s - 1)
                act.wait_ge(out_psum, s + 1)
                nc.scalar.activation(o_raw[:, :, :], bank[7][:, :].rearrange("p (n d) -> p n d", d=R_DV), ACT.Copy).then_inc(o_copied, 1)
                nc.scalar.activation(sq[:, :, :], bank[7][:, :].rearrange("p (n d) -> p n d", d=R_DV), ACT.Square).then_inc(squared, 1)

            def finish(s):
                norm(s)
                copy_turned_outputs(s)

            steps(act, lambda: copy_projections(0, 0), step, finish)

        @block.vector
        def _(dve):
            sin = const[:, slice_of("ret_sin")].rearrange("p (b n) -> p b n", b=BPS)
            decay = const[:, slice_of("ret_decay")].rearrange("p (h n) -> p h n", h=R_HEADS)
            hd = R_DK // 2

            def halves(t, which):
                return t.rearrange("p b (n two d) -> p two (b n) d", two=2, d=hd)[:, which]

            dve.wait_ge(w_in, 64)
            dve.wait_ge(zeroed, 1)

            def rotate(s):
                dve.wait_ge(raw_ready, BPS * (s + 1))
                for out_half in range(2):
                    last = nc.vector.tensor_tensor(halves(part2[:, :, :], out_half), halves(raw[:, :, :], 1 - out_half),
                                                   halves(sin, out_half), ALU.mult)
                last.then_inc(rot_steps, 1)
                dve.wait_ge(rot_steps, s + 1)
                dve.wait_ge(part1_done, s + 1)
                nc.vector.tensor_tensor(rot[:, :, :], part1[:, :, :], part2[:, :, :], ALU.add).then_inc(rot_ready, 1)

            def norm_and_gate(s):
                dve.wait_ge(squared, s + 1)
                nc.vector.tensor_reduce(ms[:, :], sq[:, :, :], AX.X, ALU.add).then_inc(ms_done, 1)
                g = gnorm[:, :].unsqueeze(1).broadcast_to([P, NBH, R_DV])
                dve.wait_ge(o_copied, s + 1)
                nc.vector.tensor_tensor(o_n[:, :, :], o_raw[:, :, :], g, ALU.mult).then_inc(norm_steps, 1)
                dve.wait_ge(norm_steps, 2 * s + 1)
                gt = gate[:, bass.ds(s * BPS, BPS), :].rearrange("p b (h d) -> p (b h) d", d=R_DV)
                nc.vector.tensor_tensor(o_n[:, :, :], o_n[:, :, :], gt, ALU.mult).then_inc(norm_steps, 1)
                dve.wait_ge(norm_steps, 2 * s + 2)
                dve.wait_ge(rstd_done, s + 1)
                nc.vector.tensor_tensor(gated[:, :, :], o_n[:, :, :], rstd[:, :].unsqueeze(2).broadcast_to([P, NBH, R_DV]),
                                        ALU.mult).then_inc(gated_done, 1)

            def add_outputs(s):
                for b in range(BPS):
                    dve.wait_ge(wo_psum, s * BPS + b + 1)
                    dst = x1[:, bass.ds(s * BPS + b, 1), :].rearrange("p o f -> p (o f)")
                    nc.vector.tensor_tensor(dst, bank[3 + b][:, 0:D], dst, ALU.add).then_inc(added, 1)

            def step(s, place, has_before, has_next):
                if has_before:
                    norm_and_gate(s - 1)
                for h in range(R_HEADS):
                    dve.wait_ge(scores_ready, s * R_HEADS + h + 1)
                    nc.vector.tensor_tensor(probs_t[:, h, :], bank[3 + h][:, 0:3 * P], decay[:, h, :], ALU.mult).then_inc(decayed, 1)
                if has_next:
                    rotate(s + 1)
                if has_before:
                    add_outputs(s - 1)

            def finish(s):
                norm_and_gate(s)
                add_outputs(s)

            steps(dve, lambda: rotate(0), step, finish)


LAYERS, HEADS, DIM, WINDOW = 6, 16, 64, 32
PAIRS = HEADS // 2
HIDDEN = 341
H_ROWS = (128, 128, 85)
QK_SCALE = 8.0
VEC = {"ln_g": 0, "ln_b": 1, "b2": 2, "b_a": 3, "b_gate": 6}
N_VEC = 9


PIECES = 6
PIECE_COLUMNS = (0, 1024, 512, 1536, 2048, 2560)


def rotary_base():
    half = np.arange(0, DIM, 2, dtype=np.float32)
    inv_freq = (1.0 / np.float32(10000.0) ** (half / np.float32(DIM))).astype(np.float32)
    t = np.arange(TOKENS, dtype=np.float32)
    freqs = t[:, None] * inv_freq[None, :]
    base = ((half + np.float32(0.4 * DIM)) / np.float32(1.4 * DIM)).astype(np.float32)
    power = ((t - TOKENS // 2) / (WINDOW // 2)).astype(np.float32)
    scale = base[None, :] ** power[:, None]
    scale = np.concatenate([scale, scale], 1)
    cos = np.concatenate([np.cos(freqs)] * 2, 1)
    sin = np.concatenate([-np.sin(freqs), np.sin(freqs)], 1)
    t4 = np.stack([cos * scale, sin * scale, cos / scale, sin / scale], 1)
    return t4.reshape(BPS, P, 4 * DIM).transpose(1, 0, 2).reshape(P, -1)


def band_masks():
    i, j = np.arange(P)[:, None], np.arange(P)[None, :]
    own = np.where((j <= i) & (i - j <= WINDOW), 0.0, MASKED)
    before = np.where(i <= j[:, 0:WINDOW], 0.0, MASKED)
    return {"band": np.tile(own, (1, 4)), "band_prev": np.tile(before, (1, HEADS))}


def transformer(nc, t, y_t, const, ident_f, ident_b, eps):
    with ExitStack() as stack:
        m = Memory(nc, stack, "tr")
        w_raw, w_top = m.sb("w_raw", [P, 2, 512]), m.sb("w_top", [P, 2, 512], I32)
        w_high, w_low = m.sb("w_high", [P, PIECES, 512], F32R), m.sb("w_low", [P, PIECES, 512], F32R)
        wo = m.sb("wo", [P, PAIRS, D])
        w1 = m.sb("w1", [P, 2 * HIDDEN])
        w2 = m.sb("w2", [P, 3, D])
        vec = m.sb("vec", [P, N_VEC])
        qk_scales = m.sb("qk_scales", [P, 4 * DIM])
        table = m.sb("table", [P, BPS, 4, DIM])
        ones = m.sb("ones", [P, P])
        carrier, carrier_a = m.sb("carrier", [P, 1]), m.sb("carrier_a", [P, 1])
        band_b, prev_b = m.sb("band_b", [P, 4 * P], BF16), m.sb("prev_b", [P, 512], BF16)
        ln_q = m.sb("ln_q", [P, 2])
        xs = m.sb("xs", [P, BPS, P])
        xs_top = m.sb("xs_top", [P, BPS, P], I32)
        xs_high, xs_low = m.sb("xs_high", [P, BPS, P], F32R), m.sb("xs_low", [P, BPS, P], F32R)
        raw, sq, part1, part2 = (m.sb(n, [P, 2, 512]) for n in ("raw", "sq", "part1", "part2"))
        rot = m.sb("rot", [P, 4, 512])
        norm2 = m.sb("norm2", [P, BPS, 4, 8])
        ln_n = m.sb("ln_n", [P, 2, 8])
        q_even, q_odd, k_t = (m.sb(n, [P, PAIRS, TOKENS]) for n in ("q_even", "q_odd", "k_t"))
        v = m.sb("v", [P, BPS, HEADS * DIM])
        top, top_prev, neg_top = m.sb("top", [P, 8, 4]), m.sb("top_prev", [WINDOW, 4, 4]), m.sb("neg_top", [P, 8, 4])
        sums, sum_prev, inv = m.sb("sums", [P, 8, 4]), m.sb("sum_prev", [WINDOW, 4, 4]), m.sb("inv", [P, 8, 4])
        probs = m.sb("probs", [P, 4, 4, P])
        arg_prev = m.sb("arg_prev", [WINDOW, 4, 4, WINDOW])
        probs_prev = m.sb("probs_prev", [WINDOW, 4, 4, WINDOW])
        probs_t = m.sb("probs_t", [P, 2, 4 * P])
        probs_prev_t = m.sb("probs_prev_t", [P, 4, 4 * WINDOW])
        o_t = m.sb("o_t", [P, PAIRS, TOKENS])
        xf, centred, sq_f, ln_var, rstd_f, scaled, xn_f = (m.sb(n, [P, TOKENS]) for n in (
            "xf", "centred", "sq_f", "ln_var", "rstd_f", "scaled", "xn_f"))
        gelu = m.sb("gelu", [P, 3, TOKENS])
        hid = m.sb("hid", [P, 3, TOKENS])
        bank = m.banks()
        unit_bank, v_bank, score_bank, q_turn_bank, p_turn_bank, out_bank, misc_bank = (
            bank[0], bank[1], bank[2:4], bank[4], bank[5], bank[6], bank[7])
        w1_bank = (bank[1], bank[0], bank[1])
        S = {n: m.sem(n) for n in (
            "const_done", "zeroed", "w_in0", "w_in1", "w_top_done", "w_low_done", "w_high_done", "wo_in", "ffn_in", "scales_in", "table_done",
            "xs_loaded", "xs_top_done", "xs_ready", "unit_psum", "raw_ready", "sq_q_done", "sq_k_done", "part1_done", "norm2_done", "ln_n_done", "inv_norm_done",
            "part2_done", "rot_done", "k_scaled", "unit_turned", "q_even_sb", "q_odd_sb", "k_sb",
            "v_psum", "v_sb", "prev_psum", "scores_psum", "top_done", "top_joined", "neg_top_done", "exp_done",
            "arg_scaled", "arg_ready", "exp_prev_done", "sum_prev_done", "sums_joined", "inv_done",
            "prev_normed", "prev_turned", "probs_ready", "turned", "turned_sb", "out_psum", "o_sb", "wo_psum", "y_added",
            "xf_ready", "mean_psum", "centred_done", "sq_f_done", "var_psum", "ln_var_done", "rstd_f_done",
            "scaled_done", "xn_f_done", "w1_psum", "gelu_done", "hid_done", "w2_psum", "ffn_added")}
        block = stack.enter_context(nc.Block())
        K = 8


        def jobs(eng, body, ffn_alone, first_units):
            first, last = 0, SEQS - 1
            first_units()
            body(0, first, 0, False, True)
            with eng.Fori(1, last) as s:
                body(0, s, s, True, True)
            with eng.Fori(1, LAYERS) as layer:
                body(layer - 1, last, layer * SEQS - 1, True, True)
                body(layer, first, layer * SEQS, True, True)
                with eng.Fori(1, last) as s:
                    body(layer, s, layer * SEQS + s, True, True)
            body(LAYERS - 1, last, LAYERS * SEQS - 1, True, False)
            ffn_alone(LAYERS * SEQS - 1)

        def ends_layer(s):
            return isinstance(s, int) and s == SEQS - 1

        def starts_layer(s):
            return isinstance(s, int) and s == 0

        def next_seq(s):
            return 0 if ends_layer(s) else s + 1

        def ffn_of(layer, s):
            return (layer - 1, SEQS - 1) if starts_layer(s) else (layer, s - 1)

        def units_of(slot, J):
            return 8 * J + 5 + slot, 1 if slot < 3 or slot == 7 else 0, (slot + 1) % 4

        def has_unit(slot, has_next):
            return 0 <= slot < (K if has_next else 3)

        def first_unit(u, J):
            return 8 * J + u, u // 4, u % 4

        def y_tokens(s, start, n):
            return y_t[:, bass.ds(s * TOKENS + start, n)]

        @block.sync
        def _(sp):
            def load(layer, again):
                at = bass.ds(layer, 1)
                if again:
                    sp.wait_ge(S["table_done"], layer + 1)
                sp.dma_start(qk_scales[:, :], t["tr_scales"][at, :].partition_broadcast(P).rearrange("p o n -> p (o n)")
                             ).then_inc(S["scales_in"], 16)
                for i in range(PIECES):
                    if again or i >= 2:
                        sp.wait_ge(S["w_low_done"], layer * PIECES + i - 1)
                    at_i = slice(PIECE_COLUMNS[i], PIECE_COLUMNS[i] + 512)
                    sp.dma_start(w_raw[:, i % 2, :], t["tr_qkv"][at, :, at_i].rearrange("o p n -> p (o n)")).then_inc(S[f"w_in{i % 2}"], 16)
                if again:
                    sp.wait_ge(S["wo_psum"], layer * SEQS + 1)
                sp.dma_start(wo[:, :, :], t["tr_o"][at, :, :].rearrange("o (c p) f -> p (o c) f", p=P)).then_inc(S["wo_in"], 16)
                if again:
                    sp.wait_ge(S["ffn_added"], layer * SEQS + 1)
                sp.dma_start(w1[:, :], t["tr_w1"][at, :, :].rearrange("o p n -> p (o n)")).then_inc(S["ffn_in"], 16)
                for c, rows in enumerate(H_ROWS):
                    sp.dma_start(w2[0:rows, c, :], t["tr_w2"][at, c * P:c * P + rows, :].rearrange("o p n -> p (o n)")
                                 ).then_inc(S["ffn_in"], 16)
                sp.dma_start(vec[:, :], t["tr_vec"][at, :, :].rearrange("o p n -> p (o n)")).then_inc(S["ffn_in"], 16)

            load(0, False)
            with sp.Fori(1, LAYERS) as layer:
                load(layer, True)

        @block.gpsimd
        def _(pool):
            g = nc.gpsimd
            g.memset(ones[:, :], 1.0 / D).then_inc(S["zeroed"], 1)
            pool.wait_ge(S["zeroed"], 1)
            g.memset(xs[:, :, :], 0.0).then_inc(S["zeroed"], 1)
            pool.wait_ge(S["zeroed"], 2)
            g.memset(xf[:, :], 0.0).then_inc(S["zeroed"], 1)
            pool.wait_ge(S["zeroed"], 3)
            g.memset(q_even[:, :, :], 0.0).then_inc(S["zeroed"], 1)
            pool.wait_ge(S["zeroed"], 4)
            g.memset(q_odd[:, :, :], 0.0).then_inc(S["zeroed"], 1)
            pool.wait_ge(S["zeroed"], 5)
            g.memset(ln_q[:, 0:1], float(np.log(QK_SCALE) + 8 * np.log(2.0))).then_inc(S["zeroed"], 1)
            pool.wait_ge(S["zeroed"], 6)
            g.memset(ln_q[:, 1:2], float(8 * np.log(2.0))).then_inc(S["zeroed"], 1)
            pool.wait_ge(S["zeroed"], 7)
            h = D // 2

            def carry_wait():
                g.tensor_tensor(carrier[0:h, :], ones[0:h, 0:1], ones[0:h, 0:1], ALU.mult)

            def products_written(pairs, extra=0):
                pool.wait_ge(S["rot_done"], 2 * pairs + extra + 2)
                pool.wait_ge(S["k_scaled"], pairs)

            def load_xs(s, J, b):
                if not isinstance(J, int) or 4 * J + 2 * b:
                    pool.wait_ge(S["xs_ready"], 4 * J + 2 * b)
                carry_wait()
                g.tensor_copy(xs[0:h, b, :], y_t[0:h, bass.ds(s * TOKENS + b * P, P)]).then_inc(S["xs_loaded"], 1)
                if b == 0:
                    g.tensor_copy(xs[h:D, 0, 1:P], y_t[h:D, bass.ds(s * TOKENS, P - 1)]).then_inc(S["xs_loaded"], 1)
                else:
                    g.tensor_copy(xs[h:D, 1, :], y_t[h:D, bass.ds(s * TOKENS + P - 1, P)]).then_inc(S["xs_loaded"], 1)
                pool.wait_ge(S["xs_loaded"], 4 * J + 2 * b + 2)

            def halves_of_xs(J, b):
                pool.wait_ge(S["v_psum"], 4 * J + 2 * b + 1)
                pool.wait_ge(S["xs_top_done"], 2 * J + b + 1)
                g.tensor_tensor(xs_low[:, b, :], xs[:, b, :], xs_top[:, b, :].bitcast(F32), ALU.subtract).then_inc(S["xs_ready"], 1)
                g.tensor_copy(xs_high[:, b, :], xs_top[:, b, :].bitcast(F32)).then_inc(S["xs_ready"], 1)

            def lower_half_of_w(layer, i):
                if not isinstance(layer, int):
                    if i < 4:
                        pool.wait_ge(S["unit_psum"], layer * (8 * SEQS) - 3 + i)
                    else:
                        pool.wait_ge(S["v_psum"], layer * (4 * SEQS) + i - 2)
                pool.wait_ge(S["w_top_done"], layer * PIECES + i + 1)
                g.tensor_tensor(w_low[:, i, :], w_raw[:, i % 2, :], w_top[:, i % 2, :].bitcast(F32), ALU.subtract).then_inc(S["w_low_done"], 1)

            def squares(U, b, u):
                pool.wait_ge(S["raw_ready"], U + 1)
                g.tensor_tensor(sq[:, 0, :], raw[:, 0, :], raw[:, 0, :], ALU.mult).then_inc(S["sq_q_done"], 2)

            def cosines(U, b, u):
                kind = u % 2
                pool.wait_ge(S["raw_ready"], U + 1)
                src = raw[:, u % 2, :].rearrange("p (n d) -> p n d", d=DIM)
                cos = table[:, b, 2 * kind, :].unsqueeze(1).broadcast_to([P, 8, DIM])
                g.tensor_tensor(part1[:, u % 2, :].rearrange("p (n d) -> p n d", d=DIM), src, cos, ALU.mult).then_inc(S["part1_done"], 1)

            def rotated(U, b, u):
                pool.wait_ge(S["part1_done"], U + 1)
                pool.wait_ge(S["unit_turned"], U + 1)
                pool.wait_ge(S["part2_done"], U + 1)
                g.tensor_tensor(rot[:, u, :], part1[:, u % 2, :], part2[:, u % 2, :], ALU.add).then_inc(S["rot_done"], 1)

            def scale_k(U, b, u):
                pool.wait_ge(S["rot_done"], U + 3)
                pool.wait_ge(S["inv_norm_done"], U + 1)
                r = rot[:, u, :].rearrange("p (n d) -> p n d", d=DIM)
                g.tensor_tensor(r, r, norm2[:, b, u, :].unsqueeze(2).broadcast_to([P, 8, DIM]), ALU.mult).then_inc(S["k_scaled"], 1)

            def body(layer, s, J, has_ffn, has_next):
                for slot in range(K + 1):
                    if slot in (1, 4) and has_next:
                        products_written(4 * J + (2 if slot == 1 else 4), 2 if slot == 1 else 1)
                        if slot == 4 and ends_layer(s):
                            pool.wait_ge(S["w_low_done"], (layer + 1) * PIECES + 3)
                        load_xs(next_seq(s), J + 1, slot // 4)
                    if slot in (2, 5) and has_next:
                        halves_of_xs(J + 1, slot // 5)
                    if slot == 3 and has_next and ends_layer(s):
                        pool.wait_ge(S["table_done"], layer + 3)
                    if has_unit(slot, has_next):
                        if slot % 2:
                            squares(*units_of(slot, J))
                        cosines(*units_of(slot, J))
                    if slot % 2 and has_unit(slot - 1, has_next):
                        scale_k(*units_of(slot - 1, J))
                    if has_unit(slot, has_next):
                        rotated(*units_of(slot, J))
                    if 1 <= slot <= PIECES and has_next and ends_layer(s):
                        lower_half_of_w(layer + 1, slot - 1)

            def first_units():
                J = 0
                load_xs(0, J, 0)
                halves_of_xs(J, 0)
                load_xs(0, J, 1)
                halves_of_xs(J, 1)
                for i in range(PIECES):
                    lower_half_of_w(0, i)
                pool.wait_ge(S["table_done"], 2)
                for u in range(5):
                    if u % 2 == 0:
                        squares(*first_unit(u, J))
                    cosines(*first_unit(u, J))
                    if u in (2, 4):
                        scale_k(*first_unit(u - 1, J))
                    rotated(*first_unit(u, J))

            jobs(pool, body, lambda F: None, first_units)

        @block.tensor
        def _(pe):
            mm = nc.tensor.matmul

            def unit_project(U, b, u, first=False):
                if not first:
                    pe.wait_ge(S["raw_ready"], U)
                product_of_halves(nc, unit_bank[:, :], xs_high[:, b, :], xs_low[:, b, :], w_high[:, u, :], w_low[:, u, :]
                                  ).then_inc(S["unit_psum"], 1)

            def unit_turn(U, b, u, J_unit):
                if u % 2:
                    pe.wait_ge(S["k_scaled"], 4 * J_unit + 2 * b + u // 2 + 1)
                else:
                    pe.wait_ge(S["rot_done"], U + 3)
                if u % 2:
                    pe.wait_ge(S["q_even_sb"], 4 * J_unit + 2 * b + u // 2 + 2)
                    pe.wait_ge(S["q_odd_sb"], 4 * J_unit + 2 * b + u // 2 + 2)
                else:
                    pe.wait_ge(S["k_sb"], 4 * J_unit + 2 * b + u // 2 + 1)
                for i in range(4):
                    last = nc.tensor.transpose(q_turn_bank[:, i * P:(i + 1) * P], rot[:, u, i * P:(i + 1) * P], ident_f)
                last.then_inc(S["unit_turned"], 1)

            def v_project(J, u):
                b, half = u // 2, u % 2
                if u:
                    pe.wait_ge(S["v_sb"], 4 * J + u)
                product_of_halves(nc, v_bank[:, :], xs_high[:, b, :], xs_low[:, b, :], w_high[:, 4 + half, :], w_low[:, 4 + half, :]
                                  ).then_inc(S["v_psum"], 1)

            def scores(J, k):
                b, g4 = k // 4, k % 4
                if k % 2 == 0:
                    n = 4 * J + 2 * b + g4 // 2 + 1 + 1
                    pe.wait_ge(S["q_even_sb"], n)
                    pe.wait_ge(S["q_odd_sb"], n)
                    pe.wait_ge(S["k_sb"], n)
                pe.wait_ge(S["exp_done"], K * J + k - 1 + 2)
                sc = score_bank[k % 2]
                mm(sc[:, :], ident_b[:, :], band_b[:, :], start=True, stop=False)
                for i in range(4):
                    h = 4 * g4 + i
                    q = (q_even, q_odd)[h % 2]
                    tok = slice(b * P, (b + 1) * P)
                    last = mm(sc[:, i * P:(i + 1) * P], q[:, h // 2, tok], k_t[:, h // 2, tok], start=False, stop=i == 3)
                last.then_inc(S["scores_psum"], 1)

            def scores_before(J, has_ffn):
                for name in ("q_even_sb", "q_odd_sb"):
                    pe.wait_ge(S[name], 4 * J + 2 + 2 + 1)
                if has_ffn:
                    pe.wait_ge(S["ln_var_done"], J)
                else:
                    pe.wait_ge(S["ffn_added"], J + 1)
                mm(misc_bank[0:WINDOW, :], ident_b[:, 0:WINDOW], prev_b[:, :], start=True, stop=False)
                for h in range(HEADS):
                    q = (q_even, q_odd)[h % 2]
                    last = mm(misc_bank[0:WINDOW, h * WINDOW:(h + 1) * WINDOW], q[:, h // 2, P:P + WINDOW],
                              k_t[:, h // 2, P - WINDOW:P], start=False, stop=h == HEADS - 1)
                last.then_inc(S["prev_psum"], 1)

            def turn_probs(J, k):
                pe.wait_ge(S["probs_ready"], K * J + k + 1)
                pe.wait_ge(S["turned_sb"], K * J + k + 1)
                for i in range(4):
                    last = nc.tensor.transpose(p_turn_bank[:, i * P:(i + 1) * P], probs[:, k % 4, i, :], ident_f)
                last.then_inc(S["turned"], 1)

            def outputs(J, k):
                b, g4 = k // 4, k % 4
                if k % 2 == 0:
                    pe.wait_ge(S["o_sb"], 4 * J + k // 2 + 1)
                    pe.wait_ge(S["v_sb"], 4 * J + 2 * b + (k % 4) // 2 + 1)
                pe.wait_ge(S["turned_sb"], K * J + k + 2)
                if b:
                    pe.wait_ge(S["prev_turned"], 4 * J + k - 4 + 1)
                for i in range(4):
                    h = 4 * g4 + i
                    rows = slice(h % 2 * DIM, (h % 2 + 1) * DIM)
                    at = (h // 2 % 4) * P
                    hd = slice(h * DIM, (h + 1) * DIM)
                    last = mm(out_bank[rows, at:at + P], v[:, b, hd], probs_t[:, k % 2, i * P:(i + 1) * P], start=True, stop=b == 0)
                    if b:
                        last = mm(out_bank[rows, at:at + WINDOW], v[P - WINDOW:P, 0, hd],
                                  probs_prev_t[P - WINDOW:P, g4, i * WINDOW:(i + 1) * WINDOW], start=False, stop=True)
                last.then_inc(S["out_psum"], 1)

            def project_out(J):
                pe.wait_ge(S["o_sb"], 4 * J + 4 + 1)
                pe.wait_ge(S["ffn_added"], J + 1)
                for c in range(PAIRS):
                    last = mm(misc_bank[:, 0:TOKENS], wo[:, c, :], o_t[:, c, :], start=c == 0, stop=c == PAIRS - 1)
                last.then_inc(S["wo_psum"], 1)

            def ffn_mean(F):
                pe.wait_ge(S["xf_ready"], 2 * F + 2)
                mm(misc_bank[:, 0:TOKENS], ones[:, :], xf[:, :], start=True, stop=True).then_inc(S["mean_psum"], 1)

            def ffn_var(F):
                pe.wait_ge(S["sq_f_done"], F + 1)
                mm(misc_bank[:, 0:TOKENS], ones[:, :], sq_f[:, :], start=True, stop=True).then_inc(S["var_psum"], 1)

            def ffn_w1(F, c):
                rows = H_ROWS[c]
                if c == 0:
                    pe.wait_ge(S["xn_f_done"], F + 1)
                if c == 2:
                    pe.wait_ge(S["hid_done"], 3 * F + 1)
                for i in range(2):
                    at = i * HIDDEN + c * P
                    last = mm(w1_bank[c][0:rows, i * TOKENS:(i + 1) * TOKENS], w1[:, at:at + rows], xn_f[:, :], start=True, stop=True)
                last.then_inc(S["w1_psum"], 1)

            def ffn_w2(F):
                pe.wait_ge(S["hid_done"], 3 * F + 3)
                for c, rows in enumerate(H_ROWS):
                    last = mm(misc_bank[:, 0:TOKENS], w2[0:rows, c, :], hid[0:rows, c, :], start=c == 0, stop=c == 2)
                last.then_inc(S["w2_psum"], 1)

            def next_unit(k, J, new_layer=None):
                if k in (3, 7):
                    pe.wait_ge(S["xs_ready"], 4 * J + (6 if k == 3 else 8))
                if 3 <= k <= 6 and new_layer is not None:
                    pe.wait_ge(S["w_high_done"], new_layer * PIECES + k - 3 + 1)
                unit_project(*units_of(k, J))

            def body(layer, s, J, has_ffn, has_next):
                for k in range(K + 3):
                    if 1 <= k < K:
                        scores(J, k)
                    if k == K + 1 and has_next:
                        scores(J + 1, 0)
                    if k == 4:
                        scores_before(J, has_ffn)
                    if 2 <= k < K + 2:
                        turn_probs(J, k - 2)
                    if k == 0 and starts_layer(s):
                        pe.wait_ge(S["w_high_done"], layer * PIECES + PIECES)
                    if k < 4:
                        v_project(J, k)
                    if k == K + 1 and has_ffn:
                        ffn_w1(J - 1, 2)
                    if k >= K:
                        outputs(J, k - 3)
                    if k == K and has_ffn:
                        pe.wait_ge(S["raw_ready"], 8 * J + (13 if has_next else 8))
                        ffn_w1(J - 1, 1)
                    if k == K + 2 and has_ffn:
                        ffn_w2(J - 1)
                    if has_unit(k + 1, has_next):
                        next_unit(k + 1, J, layer + 1 if ends_layer(s) else None)
                    if has_unit(k - 2, has_next):
                        U, b, u = units_of(k - 2, J)
                        unit_turn(U, b, u, J if k - 2 < 3 else J + 1)
                    if k == K + 1 and has_next:
                        if has_ffn:
                            pe.wait_ge(S["hid_done"], 3 * (J - 1) + 2)
                        next_unit(0, J + 1)
                    if 3 <= k < K:
                        outputs(J, k - 3)
                    if k == K - 1 and has_ffn:
                        pe.wait_ge(S["v_sb"], 4 * J + 4)
                        pe.wait_ge(S["ffn_in"], 16 * 5 * (ffn_of(layer, s)[0] + 1))
                        ffn_w1(J - 1, 0)
                    if k == 1 and has_ffn:
                        pe.wait_ge(S["wo_in"], 16 * (ffn_of(layer, s)[0] + 1))
                        project_out(J - 1)
                    if k == 2 and has_ffn:
                        ffn_mean(J - 1)
                    if k == 3 and has_ffn:
                        ffn_var(J - 1)

            def first_units():
                J = 0
                pe.wait_ge(S["w_high_done"], 4)
                pe.wait_ge(S["xs_ready"], 4 * J + 4)
                for u in range(7):
                    if u < 5:
                        unit_project(*first_unit(u, J), first=u == 0)
                    if u >= 2:
                        unit_turn(*first_unit(u - 2, J), J)
                scores(J, 0)
                next_unit(0, J)

            def ffn_alone(F):
                project_out(F)
                ffn_mean(F)
                ffn_var(F)
                for c in range(3):
                    ffn_w1(F, c)
                ffn_w2(F)

            pe.sem_inc(S["v_psum"], 3)
            pe.sem_inc(S["wo_psum"], 1)
            pe.wait_ge(S["const_done"], 2)
            pe.wait_ge(S["zeroed"], 7)
            jobs(pe, body, ffn_alone, first_units)

        @block.scalar
        def _(act):
            a = nc.scalar.activation

            def upper_half_of_w(layer, i):
                act.wait_ge(S["w_low_done"], layer * PIECES + i + 1)
                a(w_high[:, i, :], w_top[:, i % 2, :].bitcast(F32), ACT.Copy).then_inc(S["w_high_done"], 1)

            def unit_copy(U, b, u):
                act.wait_ge(S["unit_psum"], U + 1)
                act.wait_ge(S["rot_done"], U + 1)
                a(raw[:, u % 2, :], unit_bank[:, :], ACT.Copy).then_inc(S["raw_ready"], 1)
                if u % 2:
                    act.wait_ge(S["raw_ready"], U + 1)
                    a(sq[:, 1, :], raw[:, 1, :], ACT.Square).then_inc(S["sq_k_done"], 2)

            def unit_norm(U, b, u):
                act.wait_ge(S["norm2_done"], 2 * U + 2)
                a(ln_n[:, u % 2, :], norm2[:, b, u, :], ACT.Ln, scale=2.0 ** 16).then_inc(S["ln_n_done"], 1)
                act.wait_ge(S["ln_n_done"], U + 1)
                a(norm2[:, b, u, :], ln_n[:, u % 2, :], ACT.Exp, scale=-0.5, bias=ln_q[:, u % 2:u % 2 + 1]).then_inc(S["inv_norm_done"], 1)

            def unit_out(U, b, u):
                act.wait_ge(S["unit_turned"], U + 1 + 4)
                src = q_turn_bank[:, :].rearrange("p (c t) -> p c t", t=P)
                pairs, tok = slice(u // 2 * 4, u // 2 * 4 + 4), slice(b * P, (b + 1) * P)
                if u % 2:
                    a(k_t[:, pairs, tok], src, ACT.Copy).then_inc(S["k_sb"], 1)
                else:
                    a(q_even[0:DIM, pairs, tok], src[0:DIM], ACT.Copy).then_inc(S["q_even_sb"], 1)

            def v_copy(J, u):
                act.wait_ge(S["v_psum"], 4 * J + u + 1 + 3)
                b, half = u // 2, u % 2
                a(v[:, b, half * 512:(half + 1) * 512], v_bank[:, :], ACT.Copy).then_inc(S["v_sb"], 1)

            def exps(J, k):
                b, g4 = k // 4, k % 4
                act.wait_ge(S["neg_top_done"], K * J + k + 1)
                for i in range(4):
                    h = 4 * g4 + i
                    last = a(probs[:, k % 4, i, :], score_bank[k % 2][:, i * P:(i + 1) * P], ACT.Exp,
                             scale=norm2[:, b, h // 8 * 2, h % 8:h % 8 + 1], bias=neg_top[:, k, i:i + 1],
                             accum_out=sums[:, k, i:i + 1])
                last.then_inc(S["exp_done"], 1)
                if b:
                    act.wait_ge(S["arg_ready"], 4 * J + g4 + 1)
                    a(probs_prev[:, g4, :, :], arg_prev[:, g4, :, :], ACT.Exp).then_inc(S["exp_prev_done"], 1)

            def turned_copy(J, k):
                act.wait_ge(S["turned"], K * J + k + 1)
                a(probs_t[:, k % 2, :], p_turn_bank[:, :], ACT.Copy).then_inc(S["turned_sb"], 1)

            def out_copy(J, f):
                act.wait_ge(S["out_psum"], K * J + 2 * f + 2)
                a(o_t[:, f % 2 * 4:f % 2 * 4 + 4, f // 2 * P:(f // 2 + 1) * P], out_bank[:, :].rearrange("p (c t) -> p c t", t=P), ACT.Copy).then_inc(S["o_sb"], 1)

            def load_xf(s, F):
                h = D // 2
                act.wait_ge(S["centred_done"], F + 1)
                act.wait_ge(S["y_added"], F + 1)
                a(carrier_a[:, :], eps[:, :], ACT.Copy)
                a(xf[0:h, :], y_t[0:h, bass.ds(s * TOKENS, TOKENS)], ACT.Copy).then_inc(S["xf_ready"], 1)
                a(xf[h:D, 1:TOKENS], y_t[h:D, bass.ds(s * TOKENS, TOKENS - 1)], ACT.Copy).then_inc(S["xf_ready"], 1)

            def ffn_square(F):
                act.wait_ge(S["centred_done"], F + 2)
                a(sq_f[:, :], centred[:, :], ACT.Square).then_inc(S["sq_f_done"], 1)

            def ffn_rstd(F):
                act.wait_ge(S["var_psum"], F + 1)
                a(ln_var[:, :], misc_bank[:, 0:TOKENS], ACT.Ln, bias=eps[:, 0:1]).then_inc(S["ln_var_done"], 1)
                act.wait_ge(S["ln_var_done"], F + 1)
                a(rstd_f[:, :], ln_var[:, :], ACT.Exp, scale=-0.5).then_inc(S["rstd_f_done"], 1)

            def ffn_gelu(F, c):
                rows = H_ROWS[c]
                act.wait_ge(S["w1_psum"], 3 * F + c + 1)
                a(gelu[0:rows, c, :], w1_bank[c][0:rows, TOKENS:2 * TOKENS], ACT.Gelu,
                  bias=vec[0:rows, VEC["b_gate"] + c:VEC["b_gate"] + c + 1]).then_inc(S["gelu_done"], 1)

            def begin(J):
                unit_copy(*units_of(0, J))
                exps(J, 0)

            def body(layer, s, J, has_ffn, has_next):
                for k in range(K + 3):
                    if k not in (0, 4) and has_unit(k, has_next):
                        unit_copy(*units_of(k, J))
                    if has_unit(k - 3, has_next):
                        unit_out(*units_of(k - 3, J))
                    if k == 4 and has_ffn:
                        ffn_rstd(J - 1)
                    if k == 4 and has_unit(k, has_next):
                        unit_copy(*units_of(k, J))
                    if has_unit(k - 1, has_next):
                        unit_norm(*units_of(k - 1, J))
                    if k in (5, 7, 9):
                        out_copy(J, (k - 5) // 2)
                    if 2 <= k < K + 2:
                        turned_copy(J, k - 2)
                    if k == 2 and has_ffn:
                        load_xf(ffn_of(layer, s)[1], J - 1)
                    if k == 3 and has_ffn:
                        ffn_square(J - 1)
                    if 1 <= k < K:
                        exps(J, k)
                    if k < 4:
                        v_copy(J, k)
                    if 1 <= k <= PIECES and has_next and ends_layer(s):
                        upper_half_of_w(layer + 1, k - 1)
                    if k == K and has_ffn:
                        ffn_gelu(J - 1, 0)
                        ffn_gelu(J - 1, 1)
                    if k == K + 1 and has_ffn:
                        ffn_gelu(J - 1, 2)
                        nc.scalar.preload_act_table_set(LN_EXP)
                    if k == K + 1 and has_next:
                        begin(J + 1)

            def first_units():
                J = 0
                for i in range(PIECES):
                    upper_half_of_w(0, i)
                for u in range(7):
                    if u < 5:
                        unit_copy(*first_unit(u, J))
                    if 1 <= u <= 5:
                        unit_norm(*first_unit(u - 1, J))
                    if u >= 2:
                        unit_out(*first_unit(u - 2, J))
                begin(J)

            def ffn_alone(F):
                load_xf(SEQS - 1, F)
                ffn_square(F)
                ffn_rstd(F)
                for c in range(3):
                    ffn_gelu(F, c)
                nc.scalar.preload_act_table_set(LN_EXP)

            nc.scalar.preload_act_table_set(LN_EXP)
            act.sem_inc(S["exp_done"], 2)
            act.sem_inc(S["turned_sb"], 1)
            act.sem_inc(S["k_sb"], 1)
            act.sem_inc(S["q_even_sb"], 1)
            act.wait_ge(S["zeroed"], 7)
            jobs(act, body, ffn_alone, first_units)

        @block.vector
        def _(dve):
            w = nc.vector
            hd = DIM // 2

            def top_of_w(layer, i):
                dve.wait_ge(S[f"w_in{i % 2}"], 16 * (layer * (PIECES // 2) + i // 2 + 1))
                if i >= 2 or not isinstance(layer, int):
                    dve.wait_ge(S["w_high_done"], layer * PIECES + i - 1)
                w.tensor_scalar(w_top[:, i % 2, :], w_raw[:, i % 2, :].bitcast(I32), TOP_BITS, None, ALU.bitwise_and
                                ).then_inc(S["w_top_done"], 1)

            def top_of_xs(J, b):
                dve.wait_ge(S["xs_loaded"], 4 * J + 2 * b + 2)
                w.tensor_scalar(xs_top[:, b, :], xs[:, b, :].bitcast(I32), TOP_BITS, None, ALU.bitwise_and).then_inc(S["xs_top_done"], 1)

            def unit_rotate(U, b, u):
                kind, slot = u % 2, u % 2
                dve.wait_ge(S["raw_ready"], U + 1)
                src = raw[:, slot, :].rearrange("p (n two d) -> p two n d", two=2, d=hd)
                dst = part2[:, slot, :].rearrange("p (n two d) -> p two n d", two=2, d=hd)
                for o in range(2):
                    sin = table[:, b, 2 * kind + 1, o * hd:(o + 1) * hd].unsqueeze(1).broadcast_to([P, 8, hd])
                    last = w.tensor_tensor(dst[:, o], src[:, 1 - o], sin, ALU.mult)
                last.then_inc(S["part2_done"], 1)
                if u % 2:
                    dve.wait_ge(S["sq_k_done"], U + 1)
                else:
                    dve.wait_ge(S["sq_q_done"], U + 2)
                w.tensor_reduce(norm2[:, b, u, :], sq[:, slot, :].rearrange("p (n d) -> p n d", d=DIM), AX.X, ALU.add
                                ).then_inc(S["norm2_done"], 1)
                dve.wait_ge(S["norm2_done"], 2 * U + 1)
                w.tensor_scalar(norm2[:, b, u, :], norm2[:, b, u, :], 1e-24, None, ALU.max).then_inc(S["norm2_done"], 1)

            def unit_out(U, b, u):
                if u % 2 == 0:
                    dve.wait_ge(S["unit_turned"], U + 1 + 4)
                    src = q_turn_bank[:, :].rearrange("p (c t) -> p c t", t=P)
                    w.tensor_copy(q_odd[DIM:P, u // 2 * 4:u // 2 * 4 + 4, b * P:(b + 1) * P], src[DIM:P]).then_inc(S["q_odd_sb"], 1)

            def softmax_steps(J, k):
                new, old = k < K, k >= 1
                b, g4, b0, h4 = k // 4, k % 4, (k - 1) // 4, (k - 1) % 4
                new_prev, old_prev = new and b == 1, old and b0 == 1
                spread = lambda t: t.unsqueeze(2).broadcast_to([WINDOW, 4, WINDOW])
                if new:
                    inv_q = norm2[:, b, g4 // 2 * 2, g4 % 2 * 4:g4 % 2 * 4 + 4]
                    dve.wait_ge(S["scores_psum"], K * J + k + 1)
                    last = w.tensor_reduce(top[:, k, :], score_bank[k % 2][:, :].rearrange("p (n j) -> p n j", j=P), AX.X, ALU.max)
                if new_prev:
                    dve.wait_ge(S["prev_psum"], J + 1)
                    before = misc_bank[0:WINDOW, g4 * P:(g4 + 1) * P].rearrange("p (n j) -> p n j", j=WINDOW)
                    last = w.tensor_reduce(top_prev[:, g4, :], before, AX.X, ALU.max)
                if new:
                    last.then_inc(S["top_done"], 1)
                if old_prev:
                    dve.wait_ge(S["exp_done"], K * J + k + 2)
                    dve.wait_ge(S["exp_prev_done"], 4 * J + h4 + 1)
                    w.tensor_reduce(sum_prev[:, h4, :], probs_prev[:, h4, :, :], AX.X, ALU.add).then_inc(S["sum_prev_done"], 1)
                if new:
                    dve.wait_ge(S["top_done"], K * J + k + 1)
                if new_prev:
                    w.tensor_tensor(top[0:WINDOW, k, :], top[0:WINDOW, k, :], top_prev[:, g4, :], ALU.max).then_inc(S["top_joined"], 1)
                if old_prev:
                    dve.wait_ge(S["sum_prev_done"], 4 * J + h4 + 1)
                    w.tensor_tensor(sums[0:WINDOW, k - 1, :], sums[0:WINDOW, k - 1, :], sum_prev[:, h4, :], ALU.add).then_inc(S["sums_joined"], 1)
                if new_prev:
                    dve.wait_ge(S["top_joined"], 4 * J + g4 + 1)
                if new:
                    w.scalar_tensor_tensor(neg_top[:, k, :], top[:, k, :], -1.0, inv_q, ALU.mult, ALU.mult).then_inc(S["neg_top_done"], 1)
                if new_prev:
                    w.tensor_tensor(arg_prev[:, g4, :, :], before, spread(inv_q[0:WINDOW]), ALU.mult).then_inc(S["arg_scaled"], 1)
                if old_prev:
                    dve.wait_ge(S["sums_joined"], 4 * J + h4 + 1)
                if old:
                    dve.wait_ge(S["exp_done"], K * J + k + 2)
                    w.reciprocal(inv[:, k - 1, :], sums[:, k - 1, :]).then_inc(S["inv_done"], 1)
                if new_prev:
                    dve.wait_ge(S["arg_scaled"], 4 * J + g4 + 1 + 1)
                    dve.wait_ge(S["neg_top_done"], K * J + k + 1)
                    w.tensor_tensor(arg_prev[:, g4, :, :], arg_prev[:, g4, :, :], spread(neg_top[0:WINDOW, k, :]), ALU.add
                                    ).then_inc(S["arg_ready"], 1)
                if old:
                    dve.wait_ge(S["inv_done"], K * J + k)
                if old_prev:
                    w.tensor_tensor(probs_prev[:, h4, :, :], probs_prev[:, h4, :, :], spread(inv[0:WINDOW, k - 1, :]), ALU.mult
                                    ).then_inc(S["prev_normed"], 1)
                if old:
                    w.tensor_tensor(probs[:, (k - 1) % 4, :, :], probs[:, (k - 1) % 4, :, :],
                                    inv[:, k - 1, :].unsqueeze(2).broadcast_to([P, 4, P]), ALU.mult).then_inc(S["probs_ready"], 1)
                if old_prev:
                    dve.wait_ge(S["prev_normed"], 4 * J + h4 + 1)
                    w.transpose(probs_prev_t[P - WINDOW:P, h4, :], probs_prev[:, h4, :, :].rearrange("p n j -> p (n j)")).then_inc(S["prev_turned"], 1)

            def out_copy(J, f):
                dve.wait_ge(S["out_psum"], K * J + 2 * f + 2)
                b, half = f // 2, f % 2
                w.tensor_copy(o_t[:, 4 * half:4 * half + 4, b * P:(b + 1) * P], out_bank[:, :].rearrange("p (c t) -> p c t", t=P)
                              ).then_inc(S["o_sb"], 1)

            def residual(s, J):
                dve.wait_ge(S["wo_psum"], J + 2)
                dst = y_tokens(s, 0, TOKENS)
                w.tensor_tensor(dst, misc_bank[:, 0:TOKENS], dst, ALU.add).then_inc(S["y_added"], 1)

            def ffn_centre(F):
                dve.wait_ge(S["mean_psum"], F + 1)
                w.tensor_tensor(centred[:, :], xf[:, :], misc_bank[:, 0:TOKENS], ALU.subtract).then_inc(S["centred_done"], 1)

            def ffn_norm(F):
                dve.wait_ge(S["rstd_f_done"], F + 1)
                w.scalar_tensor_tensor(scaled[:, :], centred[:, :], vec[:, VEC["ln_g"]:VEC["ln_g"] + 1], rstd_f[:, :],
                                       ALU.mult, ALU.mult).then_inc(S["scaled_done"], 1)
                dve.wait_ge(S["scaled_done"], F + 1)
                w.tensor_scalar(xn_f[:, :], scaled[:, :], vec[:, VEC["ln_b"]:VEC["ln_b"] + 1], None, ALU.add).then_inc(S["xn_f_done"], 1)

            def ffn_hidden(F, c):
                rows = H_ROWS[c]
                dve.wait_ge(S["gelu_done"], 3 * F + c + 1)
                w.scalar_tensor_tensor(hid[0:rows, c, :], w1_bank[c][0:rows, 0:TOKENS], vec[0:rows, VEC["b_a"] + c:VEC["b_a"] + c + 1],
                                       gelu[0:rows, c, :], ALU.add, ALU.mult).then_inc(S["hid_done"], 1)

            def ffn_add(s, F):
                dve.wait_ge(S["w2_psum"], F + 1)
                dst = y_tokens(s, 0, TOKENS)
                w.scalar_tensor_tensor(dst, misc_bank[:, 0:TOKENS], vec[:, VEC["b2"]:VEC["b2"] + 1], dst, ALU.add, ALU.add
                                       ).then_inc(S["ffn_added"], 1)

            def body(layer, s, J, has_ffn, has_next):
                for k in range(K + 3):
                    if has_unit(k - 3, has_next):
                        unit_out(*units_of(k - 3, J))
                    if k == 3 and has_ffn:
                        ffn_centre(J - 1)
                    if 1 <= k <= K:
                        softmax_steps(J, k)
                    if k == K + 1 and has_next:
                        softmax_steps(J + 1, 0)
                    if k == 3 and has_next and ends_layer(s):
                        make_table(layer + 1)
                    if has_unit(k, has_next):
                        unit_rotate(*units_of(k, J))
                    if k in (1, 4) and has_next:
                        top_of_xs(J + 1, k // 4)
                    if 1 <= k <= PIECES and has_next and ends_layer(s):
                        top_of_w(layer + 1, k - 1)
                    if k == 1 and has_ffn:
                        residual(ffn_of(layer, s)[1], J - 1)
                    if k == 5 and has_ffn:
                        dve.wait_ge(S["ffn_in"], 16 * 5 * (ffn_of(layer, s)[0] + 1))
                        ffn_norm(J - 1)
                    if k == K and has_ffn:
                        ffn_hidden(J - 1, 0)
                        ffn_hidden(J - 1, 1)
                    if k == K + 1 and has_ffn:
                        ffn_hidden(J - 1, 2)
                    if k == K + 2:
                        out_copy(J, 3)
                    if k == K + 2 and has_ffn:
                        ffn_add(ffn_of(layer, s)[1], J - 1)

            def make_table(layer):
                if not isinstance(layer, int):
                    dve.wait_ge(S["part1_done"], layer * (8 * SEQS))
                dve.wait_ge(S["scales_in"], 16 * (layer + 1))
                for b in range(BPS):
                    base = const[:, slice_of("rotary")].rearrange("p (b n) -> p b n", b=BPS)[:, b, :]
                    last = w.tensor_tensor(table[:, b, :, :].rearrange("p a d -> p (a d)"), base, qk_scales[:, :], ALU.mult)
                last.then_inc(S["table_done"], 1)
                dve.wait_ge(S["table_done"], layer + 2)

            def first_units():
                J = 0
                for b in range(BPS):
                    top_of_xs(J, b)
                for i in range(PIECES):
                    top_of_w(0, i)
                make_table(0)
                for u in range(7):
                    if u < 5:
                        unit_rotate(*first_unit(u, J))
                    if u >= 2:
                        unit_out(*first_unit(u - 2, J))
                softmax_steps(J, 0)

            def ffn_alone(F):
                residual(SEQS - 1, F)
                ffn_centre(F)
                ffn_norm(F)
                for c in range(3):
                    ffn_hidden(F, c)
                ffn_add(SEQS - 1, F)

            w.tensor_copy(band_b[:, :], const[:, slice_of("band")]).then_inc(S["const_done"], 1)
            w.tensor_copy(prev_b[:, :], const[:, slice_of("band_prev")]).then_inc(S["const_done"], 1)
            for name, n in (("rot_done", 2), ("unit_turned", 4), ("q_odd_sb", 1), ("o_sb", 1), ("table_done", 1),
                            ("ffn_added", 1), ("centred_done", 1), ("arg_scaled", 1)):
                dve.sem_inc(S[name], n)
            dve.wait_ge(S["zeroed"], 7)
            jobs(dve, body, ffn_alone, first_units)


def add_transposed(nc, x1, y_t, ident):
    with ExitStack() as stack:
        m = Memory(nc, stack, "last")
        bank = m.banks()
        turned, added = m.sem("turned"), m.sem("added")
        block = stack.enter_context(nc.Block())

        @block.tensor
        def _(pe):
            for k in range(BLOCKS):
                last = nc.tensor.transpose(bank[k // 4][:, k % 4 * P:(k % 4 + 1) * P], y_t[:, k * P:(k + 1) * P], ident)
                if k % 4 == 3:
                    last.then_inc(turned, 1)

        @block.vector
        def _(dve):
            for q in range(8):
                dve.wait_ge(turned, q + 1)
                dst = x1[:, 4 * q:4 * q + 4, :]
                nc.vector.tensor_tensor(dst, bank[q][:, :].rearrange("p (k f) -> p k f", f=D), dst, ALU.add).then_inc(added, 1)


def store_output(nc, x1, out_dram):
    with ExitStack() as stack:
        m = Memory(nc, stack, "store")
        stored = m.sem("stored")
        block = stack.enter_context(nc.Block())
        view = out_dram.rearrange("s (b p) f -> p (s b) f", p=P)

        @block.sync
        def _(sp):
            sp.dma_start(view, x1[:, :, :]).then_inc(stored, 16)
            sp.wait_ge(stored, 16)


def program(nc, t, out):
    with ExitStack() as stack:
        m = Memory(nc, stack, "main")
        x1 = m.sb("x1", [P, BLOCKS, D])
        xn_t = m.sb("xn_t", [P, SEQS * TOKENS])
        const = m.sb("const", [P, N_CONST])
        eps = m.sb("eps", [P, 1])
        ident_b = m.sb("ident_b", [P, P], BF16)
        ident_f = const[:, slice_of("ident")]
        with ExitStack() as first_layer:
            f = Memory(nc, first_layer, "layer0")
            causal_b = f.sb("causal_b", [P, 3 * P], BF16)
            staged = f.sb("staged", [P, 2, 2, D_FF])
            wd = f.sb("wd", [P, EXPERTS, FC, D])
            normalise(nc, "norm0", x1, xn_t, const, eps, t["x"], t["const"], ((ident_b, "ident"), (causal_b, "causal")))
            causal_attention(nc, t["wq"], t["wk"], t["wv"], t["wo"], x1, xn_t, ident_f, ident_b, causal_b,
                             tuple((staged[:, e, side, :], t[name][e]) for e in range(2) for side, name in enumerate(("moe_gate", "moe_up")))
                             + ((wd[:, :, :, :], t["moe_down"].rearrange("e (c p) n -> p e c n", p=P)),))
            mixture_of_experts(nc, t["router"], (t["moe_gate"], t["moe_up"]), x1, xn_t, const, staged, wd)
        normalise(nc, "norm1", x1, xn_t, const, eps)
        retention(nc, t["ret_qkv"], t["ret_g"], t["ret_o"], t["ret_gnorm"], x1, xn_t, const, eps)
        transformer(nc, t, xn_t, const, ident_f, ident_b, eps)
        add_transposed(nc, x1, xn_t, ident_f)
        store_output(nc, x1, out)


def kernel(**inputs):
    import concourse.bacc as bacc
    from concourse.bass_utils import run_bass_kernel_spmd

    a = {n: np.asarray(v) for n, v in inputs.items()}

    def proj(w):
        return w.reshape(-1, D).T

    b1 = np.zeros((LAYERS, 2, 3 * P), np.float32)
    b1[:, :, 0:HIDDEN] = a["L1_ffn_b1"].reshape(LAYERS, 2, HIDDEN)
    vectors = np.concatenate([a["L1_ffn_ln_g"][:, None], a["L1_ffn_ln_b"][:, None], a["L1_ffn_b2"][:, None],
                              b1.reshape(LAYERS, 6, P)], 1).transpose(0, 2, 1)
    scales = np.concatenate([f(a[n]) for n in ("L1_ffn_q_scale", "L1_ffn_k_scale")
                             for f in (lambda w: w, lambda w: np.roll(w, DIM // 2, 1))], 1)
    arrays = {
        "tr_qkv": a["L1_ffn_Wqkv"], "tr_o": a["L1_ffn_Wo"], "tr_w1": a["L1_ffn_W1"], "tr_w2": a["L1_ffn_W2"],
        "tr_vec": vectors, "tr_scales": scales,
        "x": a["L0_attn_x_q"],
        "const": const_tables(),
        "router": a["L0_ffn_router_w"].T, "moe_gate": a["L0_ffn_w_gate"], "moe_up": a["L0_ffn_w_up"], "moe_down": a["L0_ffn_w_down"],
        "ret_qkv": np.concatenate([a["L1_attn_Wq"].T, a["L1_attn_Wk"].T, a["L1_attn_Wv"].T], 1),
        "ret_g": a["L1_attn_Wg"].T, "ret_o": a["L1_attn_Wo"].T, "ret_gnorm": a["L1_attn_gnorm_w"],
        "wq": proj(a["L0_attn_w_q"]), "wk": proj(a["L0_attn_w_k"]), "wv": proj(a["L0_attn_w_v"]), "wo": a["L0_attn_w_o"],
    }
    arrays = {"in_" + n: np.ascontiguousarray(v) for n, v in arrays.items()}
    nc = bacc.Bacc("TRN2", target_bir_lowering=False, num_devices=1)
    t = {n[3:]: nc.dram_tensor(n, list(v.shape), F32, kind="ExternalInput").ap() for n, v in arrays.items()}
    out = nc.dram_tensor("result", [SEQS, TOKENS, D], F32, kind="ExternalOutput").ap()
    program(nc, t, out)
    r = run_bass_kernel_spmd(nc, [arrays], core_ids=[0])
    return r.results[0]["result"]
```
